# Optimizing a Trainium2 kernel written in Bass

```python
import numpy as np
import jax
import jax.numpy as jnp

def _softmax(x, axis=-1):
    return jax.nn.softmax(x, axis=axis)

def _gelu(x):
    return jax.nn.gelu(x, approximate=True)

def _silu(x):
    return jax.nn.silu(x)

def _sigmoid(x):
    return jax.nn.sigmoid(x)

def _layernorm(x, axis=-1, eps=1e-05):
    m = jnp.mean(x, axis=axis, keepdims=True)
    v = jnp.var(x, axis=axis, keepdims=True)
    return (x - m) / jnp.sqrt(v + eps)

def _scatter_add(tgt, idx, src, axis=0):
    return tgt.at[idx].add(src)

def _segment_sum(src, seg, n):
    return jax.ops.segment_sum(src, seg, n)
kernel_name = 'mk_conv_preact_d4_conv_nchw1024_r2_3c9fa2'

def setup_inputs(seed: int=0):
    np.random.seed(seed)
    _w = jnp.asarray

    def _rec_inputs():
        import jax
        import jax.numpy as jnp
        _gk = jax.random.key(seed)
        x = -0.000125 + 0.9999 * jax.random.normal(jax.random.fold_in(_gk, 1), (8, 512, 32, 32), jnp.float32)
        return x
    x = _rec_inputs()

    def _L0_conv_setup():
        import jax, jax.numpy as jnp
        import numpy as np
        K = 5
        PAD = K // 2
        EPS = 1e-12
        key = jax.random.key(seed)
        k1, k2, k3 = jax.random.split(key, 3)
        b, c, h, w = (8, 512, 32, 32)
        out_ch = 512
        feature = jax.random.normal(k1, (b, c, h, w), dtype=jnp.float32)
        conv_w = jax.random.normal(k2, (out_ch, c + K * K), dtype=jnp.float32) * 0.02
        conv_b = jax.random.normal(k3, (out_ch,), dtype=jnp.float32) * 0.02
        return {'feature': feature, 'conv_w': conv_w, 'conv_b': conv_b}
    _L0_conv_all = _L0_conv_setup()
    _L0_conv_in = {k: v for k, v in _L0_conv_all.items() if k in ('conv_w', 'conv_b')}
    del _L0_conv_all

    def _L1_conv_setup():
        import jax, jax.numpy as jnp
        import numpy as np
        from jax import lax
        C1 = 512
        C2 = 512
        D_STATE = 8
        HEADS = 2
        D_INNER = 512
        D_HEAD = D_INNER // HEADS

        def _mobius_perm(mobius, H, W):
            ys, xs = jnp.meshgrid(jnp.linspace(-1.0, 1.0, H), jnp.linspace(-1.0, 1.0, W), indexing='ij')
            z = (xs + 1j * ys).reshape(-1).astype(jnp.complex64)
            perms = []
            for h in range(mobius.shape[0]):
                a, b, c, d = (mobius[h, 0], mobius[h, 1], mobius[h, 2], mobius[h, 3])
                s = jnp.sqrt(jnp.clip(jnp.abs(a * d - b * c), 0.001))
                a, b, c, d = (a / s, b / s, c / s, d / s)
                w = (a * z + b) / (c * z + d + 1e-06)
                score = jnp.real(w) + 1.3 * jnp.imag(w)
                perms.append(jnp.argsort(score))
            return jnp.stack(perms, 0)

        def _gather_last(v, idx):
            return jnp.take_along_axis(v, jnp.broadcast_to(idx, v.shape[:-1] + (idx.shape[-1],)), axis=-1)

        def _selective_scan(x, dt, A, Bt, Ct, D):
            Bsz, Hh, Dh, N = x.shape
            S = A.shape[-1]
            dA = jnp.exp(dt[:, :, None, :] * A[None, :, :, None])
            dB = dt[:, :, None, :] * Bt

            def step(h, inp):
                dA_t, dB_t, x_t, C_t = inp
                h = dA_t[:, :, None, :] * h + dB_t[:, :, None, :] * x_t[..., None]
                y_t = jnp.einsum('bhds,bhs->bhd', h, C_t)
                return (h, y_t)
            h0 = jnp.zeros((Bsz, Hh, Dh, S), x.dtype)
            inputs = (jnp.moveaxis(dA, -1, 0), jnp.moveaxis(dB, -1, 0), jnp.moveaxis(x, -1, 0), jnp.moveaxis(Ct, -1, 0))
            _, ys = lax.scan(step, h0, inputs)
            return jnp.moveaxis(ys, 0, -1) + D[None, :, None, None] * x
        key = jax.random.key(seed)
        ks = jax.random.split(key, 8)
        S = D_STATE
        x = jax.random.normal(ks[0], (8, C1, 32, 32), jnp.float32)
        in_proj_w = jax.random.normal(ks[1], (3 * D_INNER, C1), jnp.float32) / np.sqrt(C1)
        in_proj_b = jnp.zeros((3 * D_INNER,), jnp.float32)
        dw_w = jax.random.normal(ks[2], (D_INNER, 1, 3), jnp.float32) / np.sqrt(3.0)
        dw_b = jnp.zeros((D_INNER,), jnp.float32)
        dbc_w = jax.random.normal(ks[3], (HEADS * (1 + 2 * S), D_INNER), jnp.float32) / np.sqrt(D_INNER)
        dbc_b = jnp.zeros((HEADS * (1 + 2 * S),), jnp.float32)
        A_log = jnp.log(jnp.tile(jnp.arange(1, S + 1, dtype=jnp.float32), (HEADS, 1)))
        Dparam = jnp.ones((HEADS,), jnp.float32)
        mobius = jnp.tile(jnp.array([[1.0, 0.0, 0.0, 1.0]], jnp.float32), (HEADS, 1)) + 0.05 * jax.random.normal(ks[4], (HEADS, 4), jnp.float32)
        out_proj_w = jax.random.normal(ks[5], (C2, D_INNER), jnp.float32) / np.sqrt(D_INNER)
        out_proj_b = jnp.zeros((C2,), jnp.float32)
        return dict(x=x, in_proj_w=in_proj_w, in_proj_b=in_proj_b, dw_w=dw_w, dw_b=dw_b, dbc_w=dbc_w, dbc_b=dbc_b, A_log=A_log, Dparam=Dparam, mobius=mobius, out_proj_w=out_proj_w, out_proj_b=out_proj_b)
    _L1_conv_all = _L1_conv_setup()
    _L1_conv_in = {k: v for k, v in _L1_conv_all.items() if k in ('in_proj_w', 'in_proj_b', 'dw_w', 'dw_b', 'dbc_w', 'dbc_b', 'A_log', 'Dparam', 'mobius', 'out_proj_w', 'out_proj_b')}
    del _L1_conv_all

    def _L2_conv_setup():
        import jax, jax.numpy as jnp
        import numpy as np
        IN_C = 512
        OUT_C = 512
        N, H, W = (32, 28, 28)
        key = jax.random.key(seed)
        k1, k2, k3 = jax.random.split(key, 3)
        x = jax.random.normal(k1, (N, IN_C, H, W), dtype=jnp.float32)
        weight = jax.random.normal(k2, (OUT_C, IN_C), dtype=jnp.float32)
        bound = 1.0 / np.sqrt(IN_C)
        bias = jax.random.uniform(k3, (OUT_C, 1), dtype=jnp.float32, minval=-bound, maxval=bound)
        return {'x': x, 'weight': weight, 'bias': bias}
    _L2_conv_all = _L2_conv_setup()
    _L2_conv_in = {k: v for k, v in _L2_conv_all.items() if k in ('weight', 'bias')}
    del _L2_conv_all

    def _L3_conv_setup():
        import jax, jax.numpy as jnp
        import numpy as np
        IN_C = 512
        OUT_C = 512
        N, H, W = (32, 28, 28)
        key = jax.random.key(seed)
        k1, k2, k3 = jax.random.split(key, 3)
        x = jax.random.normal(k1, (N, IN_C, H, W), dtype=jnp.float32)
        weight = jax.random.normal(k2, (OUT_C, IN_C), dtype=jnp.float32)
        bound = 1.0 / np.sqrt(IN_C)
        bias = jax.random.uniform(k3, (OUT_C, 1), dtype=jnp.float32, minval=-bound, maxval=bound)
        return {'x': x, 'weight': weight, 'bias': bias}
    _L3_conv_all = _L3_conv_setup()
    _L3_conv_in = {k: v for k, v in _L3_conv_all.items() if k in ('weight', 'bias')}
    del _L3_conv_all
    return {'x': x, 'L0_conv_conv_w': _L0_conv_in['conv_w'], 'L0_conv_conv_b': _L0_conv_in['conv_b'], 'L1_conv_in_proj_w': _L1_conv_in['in_proj_w'], 'L1_conv_in_proj_b': _L1_conv_in['in_proj_b'], 'L1_conv_dw_w': _L1_conv_in['dw_w'], 'L1_conv_dw_b': _L1_conv_in['dw_b'], 'L1_conv_dbc_w': _L1_conv_in['dbc_w'], 'L1_conv_dbc_b': _L1_conv_in['dbc_b'], 'L1_conv_A_log': _L1_conv_in['A_log'], 'L1_conv_Dparam': _L1_conv_in['Dparam'], 'L1_conv_mobius': _L1_conv_in['mobius'], 'L1_conv_out_proj_w': _L1_conv_in['out_proj_w'], 'L1_conv_out_proj_b': _L1_conv_in['out_proj_b'], 'L2_conv_weight': _L2_conv_in['weight'], 'L2_conv_bias': _L2_conv_in['bias'], 'L3_conv_weight': _L3_conv_in['weight'], 'L3_conv_bias': _L3_conv_in['bias']}

def reference(x, L0_conv_conv_w, L0_conv_conv_b, L1_conv_in_proj_w, L1_conv_in_proj_b, L1_conv_dw_w, L1_conv_dw_b, L1_conv_dbc_w, L1_conv_dbc_b, L1_conv_A_log, L1_conv_Dparam, L1_conv_mobius, L1_conv_out_proj_w, L1_conv_out_proj_b, L2_conv_weight, L2_conv_bias, L3_conv_weight, L3_conv_bias):
    import jax
    import jax.numpy as jnp

    def _L0_conv_ref(feature, conv_w, conv_b):
        import jax, jax.numpy as jnp
        import numpy as np
        K = 5
        PAD = K // 2
        EPS = 1e-12
        b, c, h, w = feature.shape
        norm = jnp.sqrt(jnp.sum(feature * feature, axis=1, keepdims=True))
        fn = feature / jnp.maximum(norm, EPS)
        fp = jnp.pad(fn, ((0, 0), (0, 0), (PAD, PAD), (PAD, PAD)))
        corr = jnp.stack([jnp.sum(fp[:, :, r:h + r, cc:w + cc] * fn, axis=1) for cc in range(K) for r in range(K)], axis=1)
        cat = jnp.concatenate([feature, corr], axis=1)
        y = jnp.einsum('oc,bchw->bohw', conv_w, cat) + conv_b[None, :, None, None]
        return jax.nn.relu(y)

    def _L1_conv_ref(x, in_proj_w, in_proj_b, dw_w, dw_b, dbc_w, dbc_b, A_log, Dparam, mobius, out_proj_w, out_proj_b):
        import jax, jax.numpy as jnp
        import numpy as np
        from jax import lax
        C1 = 512
        C2 = 512
        D_STATE = 8
        HEADS = 2
        D_INNER = 512
        D_HEAD = D_INNER // HEADS

        def _mobius_perm(mobius, H, W):
            ys, xs = jnp.meshgrid(jnp.linspace(-1.0, 1.0, H), jnp.linspace(-1.0, 1.0, W), indexing='ij')
            z = (xs + 1j * ys).reshape(-1).astype(jnp.complex64)
            perms = []
            for h in range(mobius.shape[0]):
                a, b, c, d = (mobius[h, 0], mobius[h, 1], mobius[h, 2], mobius[h, 3])
                s = jnp.sqrt(jnp.clip(jnp.abs(a * d - b * c), 0.001))
                a, b, c, d = (a / s, b / s, c / s, d / s)
                w = (a * z + b) / (c * z + d + 1e-06)
                score = jnp.real(w) + 1.3 * jnp.imag(w)
                perms.append(jnp.argsort(score))
            return jnp.stack(perms, 0)

        def _gather_last(v, idx):
            return jnp.take_along_axis(v, jnp.broadcast_to(idx, v.shape[:-1] + (idx.shape[-1],)), axis=-1)

        def _selective_scan(x, dt, A, Bt, Ct, D):
            Bsz, Hh, Dh, N = x.shape
            S = A.shape[-1]
            dA = jnp.exp(dt[:, :, None, :] * A[None, :, :, None])
            dB = dt[:, :, None, :] * Bt

            def step(h, inp):
                dA_t, dB_t, x_t, C_t = inp
                h = dA_t[:, :, None, :] * h + dB_t[:, :, None, :] * x_t[..., None]
                y_t = jnp.einsum('bhds,bhs->bhd', h, C_t)
                return (h, y_t)
            h0 = jnp.zeros((Bsz, Hh, Dh, S), x.dtype)
            inputs = (jnp.moveaxis(dA, -1, 0), jnp.moveaxis(dB, -1, 0), jnp.moveaxis(x, -1, 0), jnp.moveaxis(Ct, -1, 0))
            _, ys = lax.scan(step, h0, inputs)
            return jnp.moveaxis(ys, 0, -1) + D[None, :, None, None] * x
        Bsz, _, H, W = x.shape
        N = H * W
        heads, S = A_log.shape
        d_inner = dw_w.shape[0]
        d_head = d_inner // heads
        xz = jax.nn.silu(jnp.einsum('oc,bchw->bohw', in_proj_w, x) + in_proj_b[None, :, None, None])
        x_ssm, res, gate = jnp.split(xz, 3, axis=1)
        xf = x_ssm.reshape(Bsz, d_inner, N)
        xf = lax.conv_general_dilated(xf, dw_w, (1,), [(1, 1)], dimension_numbers=('NCH', 'OIH', 'NCH'), feature_group_count=d_inner) + dw_b[None, :, None]
        xf = jax.nn.silu(xf)
        x_h = xf.reshape(Bsz, heads, d_head, N)
        perm = _mobius_perm(mobius, H, W)
        x_h = _gather_last(x_h, perm[None, :, None, :])
        dbc = (jnp.einsum('oc,bcn->bon', dbc_w, xf) + dbc_b[None, :, None]).reshape(Bsz, heads, 1 + 2 * S, N)
        dt = jax.nn.softplus(dbc[:, :, 0])
        B_t = dbc[:, :, 1:1 + S]
        C_t = dbc[:, :, 1 + S:]
        dt = _gather_last(dt, perm[None, :, :])
        B_t = _gather_last(B_t, perm[None, :, None, :])
        C_t = _gather_last(C_t, perm[None, :, None, :])
        A = -jnp.exp(A_log)
        y_h = _selective_scan(x_h, dt, A, B_t, C_t, Dparam)
        inv = jnp.argsort(perm, axis=-1)
        y_h = _gather_last(y_h, inv[None, :, None, :])
        y = y_h.reshape(Bsz, d_inner, H, W)
        y = y * jax.nn.silu(gate) + res
        return jax.nn.silu(jnp.einsum('oc,bchw->bohw', out_proj_w, y) + out_proj_b[None, :, None, None])

    def _L2_conv_ref(x, weight, bias):
        import jax, jax.numpy as jnp
        import numpy as np
        IN_C = 512
        OUT_C = 512
        N, H, W = (32, 28, 28)
        out = jnp.einsum('oi,nihw->nohw', weight, x)
        out = out + bias[:, 0][None, :, None, None]
        return out

    def _L3_conv_ref(x, weight, bias):
        import jax, jax.numpy as jnp
        import numpy as np
        IN_C = 512
        OUT_C = 512
        N, H, W = (32, 28, 28)
        out = jnp.einsum('oi,nihw->nohw', weight, x)
        out = out + bias[:, 0][None, :, None, None]
        return out

    def _gn(v, G=32, eps=1e-05):
        B_, C_, H_, W_ = v.shape
        g = v.reshape(B_, G, C_ // G, H_, W_)
        m = jnp.mean(g, axis=(2, 3, 4), keepdims=True)
        s = jnp.var(g, axis=(2, 3, 4), keepdims=True)
        return ((g - m) / jnp.sqrt(s + eps)).reshape(v.shape)

    def _ln_c(v, eps=1e-06):
        m = jnp.mean(v, axis=1, keepdims=True)
        s = jnp.var(v, axis=1, keepdims=True)
        return (v - m) / jnp.sqrt(s + eps)

    def _ln_t(v, eps=1e-05):
        m = jnp.mean(v, axis=-1, keepdims=True)
        s = jnp.var(v, axis=-1, keepdims=True)
        return (v - m) / jnp.sqrt(s + eps)

    def _to_tokens(v):
        B_, C_, H_, W_ = v.shape
        return v.reshape(B_, C_, H_ * W_).transpose(0, 2, 1)

    def _from_tokens(t, like):
        B_, C_, H_, W_ = like.shape
        return t.transpose(0, 2, 1).reshape(B_, C_, H_, W_)
    x = x + _L0_conv_ref(_gn(x), L0_conv_conv_w, L0_conv_conv_b)
    x = x + _L1_conv_ref(_gn(x), L1_conv_in_proj_w, L1_conv_in_proj_b, L1_conv_dw_w, L1_conv_dw_b, L1_conv_dbc_w, L1_conv_dbc_b, L1_conv_A_log, L1_conv_Dparam, L1_conv_mobius, L1_conv_out_proj_w, L1_conv_out_proj_b)
    x = x + _L2_conv_ref(_gn(x), L2_conv_weight, L2_conv_bias)
    x = x + _L3_conv_ref(_gn(x), L3_conv_weight, L3_conv_bias)
    return x

_drawn_inputs = setup_inputs


def setup_inputs(seed=0):
    import zlib

    import numpy as np

    out = dict(_drawn_inputs(seed))
    spreads = {'L1_conv_in_proj_b': (0.0, 0.1),
     'L1_conv_dw_b': (0.0, 0.601),
     'L1_conv_dbc_b': (0.0, 0.657),
     'L1_conv_Dparam': (1.0, 0.6),
     'L1_conv_out_proj_b': (0.0, 0.1)}
    factors = {'L0_conv_conv_b': 4.188,
     'L1_conv_A_log': 8.0,
     'L1_conv_mobius': 7.761,
     'L2_conv_bias': 52.011,
     'L3_conv_bias': 64.0}
    for name, (base, spread) in spreads.items():
        noise = np.random.default_rng([zlib.crc32(name.encode()), seed]).standard_normal(out[name].shape)
        drawn = base * np.exp(spread * noise) if base else spread * noise
        out[name] = jnp.asarray(drawn.astype(out[name].dtype))
    for name, factor in factors.items():
        out[name] = (out[name] * factor).astype(out[name].dtype)
    return out
```

```python
from contextlib import ExitStack

import numpy as np

import concourse.bass as bass
from concourse import mybir

F32, F16, I32 = mybir.dt.float32, mybir.dt.float16, mybir.dt.int32
ALU, ACT, AX = mybir.AluOpType, mybir.ActivationFunctionType, mybir.AxisListType

P = 128
B, C, H, W = 8, 512, 32, 32
N = H * W
KC = C // P
HALF = 512
NT = N // P
S, HEADS = 8, 2
DH = C // HEADS
J = 1 + 2 * S
ROW = DH + J
G = 16
T8 = 8
TAPS = 25
ROWS_T = P // W
WIN = 2 * P
PITCH = WIN + 4
EPS = 1e-5
BIG = 1e20
FAR_GROUP = (0, 4)


def constants():
    v = np.arange(P)
    parts = {}
    parts["ident"] = np.eye(P)
    parts["upto"] = v[:, None] <= v[None, :]
    parts["after"] = v[:, None] > v[None, :]
    same8 = (v[:, None] // T8) == (v[None, :] // T8)
    parts["same8"] = same8
    parts["after8"] = same8 & (v[:, None] > v[None, :])
    parts["group_mean"] = ((v[:, None] // 16) == (v[None, :] // 16)) / 16.0
    parts["ones"] = np.ones((P, P))
    blocks = [(s, size) for size in (128, 64, 32, 16) for s in range(0, P, size)]
    left, right = np.zeros((P, HEADS, G)), np.zeros((P, HEADS, G))
    keep = np.ones((P, HEADS))
    for h in range(HEADS):
        groups = [g for g in range(G) if g != FAR_GROUP[h]]
        for g, (s, size) in zip(groups, blocks):
            left[s:s + size // 2, h, g] = 1
            right[s + size // 2:s + size, h, g] = 1
        left[:, h, FAR_GROUP[h]] = right[:, h, FAR_GROUP[h]] = 1
        keep[FAR_GROUP[h] * S:(FAR_GROUP[h] + 1) * S, h] = 0
    parts["left"], parts["right"] = left, right
    parts["off_left"], parts["off_right"] = BIG * (1 - left), BIG * (1 - right)
    parts["keep"] = keep
    parts["within8"] = (v[:, None] % T8) <= np.arange(T8)[None, :]
    parts["eq8"] = (v[:, None] % T8) == np.arange(T8)[None, :]
    parts["block16"] = (v[:, None] // T8) == np.arange(P // T8)[None, :]
    n = np.arange(N).reshape(NT, P).T
    y, x = n // W, n % W
    inside = np.zeros((P, NT, 5, 5))
    for r in range(5):
        for c in range(5):
            inside[:, :, r, c] = ((y + r - 2 >= 0) & (y + r - 2 < H) & (x + c - 2 >= 0) & (x + c - 2 < W))
    parts["inside"] = inside
    step = np.arange(W - 1, dtype=np.float32) / np.float32(W - 1)
    line = np.concatenate([np.float32(-1) * (np.float32(1) - step) + step, [np.float32(1)]]).astype(np.float32)
    parts["grid"] = np.concatenate([line[x], line[y]], axis=1)
    at, cols = {}, []
    pos = 0
    for name, a in parts.items():
        a = np.asarray(a, np.float32).reshape(P, -1)
        at[name] = (pos, a.shape[1])
        pos += a.shape[1]
        cols.append(a)
    j = np.arange(2 * N - P)
    before = (j[None, :] - (N - P) < v[:, None]).astype(np.float32)
    n = np.arange(N)
    return at, np.concatenate(cols, axis=1), before, np.stack([line[n % W], line[n // W]])


def build(nc, d):
    at, packed, before_np, _ = constants()
    with ExitStack() as ctx:
        def sb(name, shape, dt=F32):
            return ctx.enter_context(nc.sbuf_tensor(name, shape, dt))

        def sem(name):
            return ctx.enter_context(nc.semaphore(name))

        w_hi = {"L0": sb("w0_hi", [P, KC, C], F16), "in": sb("win_hi", [P, KC, 3 * C], F16),
                "L2": sb("w2_hi", [P, KC, C], F16), "L3": sb("w3_hi", [P, KC, C], F16)}
        w_lo = {"L0": sb("w0_lo", [P, KC, C], F16), "in": sb("win_lo", [P, KC, 3 * C], F16),
                "L2": sb("w2_lo", [P, KC, C], F16), "L3": sb("w3_lo", [P, KC, C], F16)}
        w_corr = sb("w_corr", [P, C], F16)
        w_out = sb("w_out", [P, KC, C])
        w_dbc = sb("w_dbc", [P, KC, HEADS * J])
        cst = sb("cst", [P, packed.shape[1]])

        def const(name):
            o, n = at[name]
            return cst[:, o:o + n]

        ident, upto, after, same8, after8 = map(const, ("ident", "upto", "after", "same8", "after8"))
        x = sb("x", [P, KC, N])
        x_next = sb("x_next", [P, KC, N])
        even = sb("even", [P, KC * N + 16])
        odd = sb("odd", [P, KC * N])
        gate = sb("gate", [P, KC, N])
        res = sb("res", [P, KC, N])
        rows = sb("rows", [P, HEADS * NT * ROW])
        work = sb("work", [P, 2 * N])
        work2 = sb("work2", [P, 7 * DH])
        arg8 = sb("arg8", [P, NT * T8, S])
        mvc = sb("mvc", [P, NT, T8, S])
        mv = sb("mv", [P, 2, NT, G])
        mv8 = sb("mv8", [P, NT, T8])
        md8 = sb("md8", [P, NT * T8])
        gam = sb("gam", [P, NT])
        sm = sb("sm", [P, 8, 16])
        bn = sb("bn", [P, 2, 2, 6])
        st = sb("st", [P, 2, 8])
        par = sb("par", [P, 64])
        corr = sb("corr", [P, 2 * HALF], F16)
        rank = sb("rank", [P, HEADS, NT], I32)
        deq8 = sb("deq8", [P, HEADS, T8])
        amat = sb("amat", [P, HEADS, S])
        gdiag = sb("gdiag", [P, 2, NT])

        def pair(t):
            v = t[:, 0:KC * N].bitcast(F16).rearrange("p (a k n) -> p a k n", a=2, k=KC)
            return v[:, 0], v[:, 1]

        even_hi, even_lo = pair(even)
        odd_hi, odd_lo = pair(odd)
        conv_in = even[:, 0:2 * (N + 2)].rearrange("p (b n) -> p b n", b=2)
        conv_out = even[:, 2 * (N + 2):2 * (N + 2) + 2 * N].rearrange("p (b n) -> p b n", b=2)
        yscan = even[:, 0:KC * N].rearrange("p (h c d) -> p h c d", h=HEADS, c=NT)
        rows4 = rows[:, :].rearrange("p (h t r) -> p h t r", h=HEADS, t=NT)
        ytok = [rows[:, h * NT * ROW:h * NT * ROW + NT * DH].rearrange("p (t d) -> p t d", t=NT)
                for h in range(HEADS)]
        gram = rows[:, 0:NT * PITCH].rearrange("p (t w) -> p t w", t=NT)
        rnorm = rows[:, NT * PITCH:NT * PITCH + N + 2 * 64]
        rdiag = rows[:, NT * PITCH + N + 128:NT * PITCH + 2 * N + 128].rearrange("p (t k) -> p t k", t=NT)
        corr_tok = gate[:, 0, 0:NT * TAPS].rearrange("p (t k) -> p t k", t=NT)
        corr3 = gate[:, 1, 0:NT * 96].rearrange("p (t a k) -> p t a k", t=NT, a=3)
        xn = x_next[:, :, :].rearrange("p k n -> p (k n)")
        pfac, qfac, pT, qT = (xn[:, a * N:(a + 1) * N] for a in range(4))
        mmat = work[:, 0:N]
        diag = work[:, N:2 * N]
        normed = work[:, :].rearrange("p (b n) -> p b n", b=2)
        tmp = work2[:, 0:3 * HALF].rearrange("p (b n) -> p b n", b=3)
        hst = work2[:, :].rearrange("p (c d) -> p c d", c=7)

        bdbc_sb = sb("bdbc_sb", [P, HEADS * J])
        ps = [ctx.enter_context(nc.psum_tensor(f"bank{i}", [P, HALF], F32)) for i in range(8)]

        gn_ps = [ps[7][:, 4 * a:4 * a + 2] for a in range(2)]
        gram_ps = lambda t: ps[t // 2][:, (t % 2) * WIN:(t % 2 + 1) * WIN]
        tok_banks = ((4, 5), (6, 3))
        yt_banks = ((3, 4), (5, 6))
        dh_bank = lambda c: 5 + (c // 2) % 2
        bank_of = ([4, 5, 6, 0, 1, 2, 4, 5] + [0, 1, 2, 3, 6, 4, 5, 0] + [1, 2] * 8
                   + [0, 1, 2, 3, 4, 5, 6, 0] + [1, 2, 3, 4, 5, 6, 0, 1] + [2, 3, 4, 5, 6, 0, 1, 2])
        bank_free = [max([p + 1 for p in range(n) if bank_of[p] == bank_of[n]], default=0) for n in range(56)]

        d_gram = nc.dram_tensor("d_gram", (NT, P, PITCH), F32, kind="Internal").ap()
        d_scan = [nc.dram_tensor(f"d_scan{h}", (N, ROW), F32, kind="Internal").ap() for h in range(HEADS)]
        d_y = [nc.dram_tensor(f"d_y{h}", (N, DH), F32, kind="Internal").ap() for h in range(HEADS)]

        B0, BIN, BCONV, BOUT, BL2, BL3, TAP, WMAX, SCL, INV = 0, 4, 16, 20, 24, 28, 32, 44, 48, 52
        WI = {"L0": 0, "in": 1, "L2": 2, "L3": 3}

        names = """w_in w_stage w_done w_max w_maxt w_maxr w_maxb w_scl w_corrz par_in cst_in
            p_abcd p_sqrt p_score p_rank a_in a_exp
            x_in x_out gn_raw gn_stat gn_sum gn_var gn_neg gn_rstd gn_bias gn_hi gn_split
            gram_mm gram_d gram_sqrt gram_r gram_rd gram_rb gram_row gram_ev gram_pad gram_out gram_in corr_msk corr_t corr_cp corr_lo
            gemm_done gemm_evac res_added
            conv_pad conv_mac conv_act tok_mm tok_ev dbc_mm sp_z sp_dve sp_act row_ready scattered scanrows
            fac_mv fac_mm fac_arg fac_exp fac_gam fac_pq fac_8 fac_diag fac_tp fac_ptq mm_m m_ev dh_mm h_st y_mm y_ev y_out y_in
            yt_mm y_gate y_res silu2 zeros""".split()
        s = {n: sem(n) for n in names}
        per = dict(x_in=16 * KC, x_out=16 * KC, gn_raw=48, gn_stat=16, gn_sum=16, gn_var=32, gn_neg=16, gn_rstd=16,
                   gn_bias=16, gn_hi=16, gn_split=32,
                   gram_mm=NT, gram_d=NT, gram_sqrt=1, gram_r=2, gram_rd=1, gram_rb=2, gram_row=2, gram_ev=NT,
                   gram_pad=5, gram_out=16, gram_in=16 * NT, corr_msk=1, corr_t=2, corr_cp=2, corr_lo=2,
                   gemm_done=56, gemm_evac=56, res_added=32,
                   conv_pad=1, conv_mac=3 * KC, conv_act=KC, tok_mm=KC, tok_ev=KC, dbc_mm=1, sp_z=2,
                   sp_dve=10, sp_act=2, row_ready=1, scattered=16 * HEADS * NT, scanrows=16 * HEADS,
                   fac_mv=8, fac_mm=2 * HEADS, fac_arg=3 * HEADS, fac_exp=3 * HEADS, fac_gam=HEADS, fac_pq=2 * HEADS,
                   fac_8=5 * HEADS, fac_diag=HEADS, fac_tp=4 * HEADS, fac_ptq=4 * HEADS, mm_m=2 * HEADS,
                   m_ev=2 * HEADS, dh_mm=4 * HEADS, h_st=7 * HEADS, y_mm=4 * HEADS, y_ev=4 * HEADS,
                   y_out=16 * HEADS, y_in=16 * HEADS * NT, yt_mm=KC, y_gate=KC, y_res=KC, silu2=8)

        primed = {"x_out": 16}

        def wait(eng, name, i, n):
            if n or name in primed:
                eng.wait_ge(s[name], i * per[name] + n + primed.get(name, 0))

        block = ctx.enter_context(nc.Block())

        wsrc = {"L0": (d["w0t"], C), "in": (d["wint"], 3 * C), "L2": (d["w2t"], C), "L3": (d["w3t"], C)}
        flat = lambda t: t[:, :, :].rearrange("p k n -> p (k n)")
        stage = {"L0": flat(x)[:, 0:KC * C], "L2": flat(x)[:, KC * C:2 * KC * C],
                 "L3": xn[:, 0:KC * C],
                 "in0": flat(gate), "in1": flat(res)[:, 0:2 * C]}
        in_stage = [flat(gate)[:, 0:3 * C], flat(gate)[:, 3 * C:6 * C], flat(res)[:, 0:3 * C], flat(res)[:, 3 * C:6 * C]] \
            if 6 * C <= KC * N else None
        wchunks = []
        for name in ("L0", "L2", "L3"):
            for k in range(KC):
                wchunks.append((name, k, stage[name][:, k * C:(k + 1) * C]))
        for k in range(KC):
            wchunks.append(("in", k, in_stage[k]))
        corr_stage = xn[:, KC * C:KC * C + C]
        before = odd[:, 0:2 * N - P]
        grow = even[:, 0:2 * N].rearrange("p (a n) -> p a n", a=2)
        score_row = work[:, :].rearrange("p (h n) -> p h n", h=HEADS)
        scr = [even[:, (2 + a) * N:(3 + a) * N] for a in range(2)] + [odd[:, 2 * N:3 * N], odd[:, 3 * N:4 * N]]
        mob = sb("mob", [P, 24])
        N_W = 16 * (12 + 4 + 3)

        @block.sync
        def _(eng):
            eng.dma_start(cst[:, :], d["cst"]).then_inc(s["cst_in"], 16)
            for name, k, v in wchunks:
                src, n = wsrc[name]
                eng.dma_start(v, src[k * P:(k + 1) * P, :]).then_inc(s["w_in"], 16)
            eng.wait_ge(s["w_corrz"], 1)
            for r in range(3):
                eng.dma_start(corr_stage[32 * r:32 * r + TAPS, :], d["wct"]).then_inc(s["w_in"], 16)
            eng.dma_start(before, d["before"]).then_inc(s["par_in"], 16)
            for a in range(2):
                eng.dma_start(grow[:, a, :], d["grid"][a:a + 1, :].broadcast_to([P, N])).then_inc(s["par_in"], 16)
            eng.dma_start(mob[:, 0:8], d["mob"].broadcast_to([P, 8])).then_inc(s["par_in"], 16)
            for name, col, n in (("b0", B0, 4), ("bin", BIN, 12), ("bconv", BCONV, 4), ("bout", BOUT, 4),
                                 ("bl2", BL2, 4), ("bl3", BL3, 4)):
                eng.dma_start(par[:, col:col + n], d[name]).then_inc(s["par_in"], 16)
            eng.dma_start(par[:, TAP:TAP + 3 * KC], d["taps"]).then_inc(s["par_in"], 16)
            eng.dma_start(w_out[:, :, :], d["woutt"].rearrange("(k p) o -> p k o", p=P)).then_inc(s["par_in"], 16)
            eng.dma_start(w_dbc[:, :, :], d["wdbct"].rearrange("(k p) o -> p k o", p=P)).then_inc(s["par_in"], 16)
            eng.dma_start(bdbc_sb[:, :], d["bdbc"].broadcast_to([P, HEADS * J])).then_inc(s["par_in"], 16)
            eng.dma_start(mob[:, 8:24], d["alog"].broadcast_to([P, 16])).then_inc(s["a_in"], 16)
            eng.dma_start(par[:, 56:58], d["dpar"].broadcast_to([P, 2])).then_inc(s["a_in"], 16)
            for h in range(HEADS):
                eng.dma_start(par[32 * h:32 * h + 8, 58:59], d["alog_col"][h]).then_inc(s["a_in"], 16)
            eng.wait_ge(s["w_done"], len(wchunks) * 2 + 2)
            for k in range(KC):
                eng.dma_start(x_next[:, k, :], d["x"][0, k * P:(k + 1) * P, :]).then_inc(s["x_in"], 16)

            def image(i, last):
                wait(eng, "gram_ev", i, NT)
                wait(eng, "gram_pad", i, 5)
                eng.dma_start(d_gram.rearrange("t p w -> p t w"), gram).then_inc(s["gram_out"], 16)
                wait(eng, "gram_out", i, 16)
                for t in range(NT):
                    band = bass.AP(d_gram.tensor, d_gram.offset + t * P * PITCH, [[PITCH + 1, P], [W, 5], [1, 5]])
                    eng.dma_start(corr_tok[:, t, :].rearrange("p (r c) -> p r c", r=5), band).then_inc(s["gram_in"], 16)
                wait(eng, "scattered", i, 16 * HEADS * NT)
                for h in range(HEADS):
                    eng.dma_start(rows4[:, h], d_scan[h].rearrange("(c p) r -> p c r", p=P)).then_inc(s["scanrows"], 16)
                for h in range(HEADS):
                    wait(eng, "y_ev", i, 4 * (h + 1))
                    eng.dma_start(d_y[h].rearrange("(c p) r -> p c r", p=P), yscan[:, h]).then_inc(s["y_out"], 16)
                if not last:
                    wait(eng, "y_mm", i, 4 * HEADS)
                    for k in range(KC):
                        eng.dma_start(x_next[:, k, :], d["x"][bass.ds(i + 1, 1), k * P:(k + 1) * P, :].rearrange("a p n -> (a p) n")).then_inc(s["x_in"], 16)
                for k in range(KC):
                    wait(eng, "res_added", i, 29 + k)
                    eng.dma_start(d["out"][bass.ds(i, 1), k * P:(k + 1) * P, :].rearrange("a p n -> (a p) n"), x[:, k, :]).then_inc(s["x_out"], 16)

            with eng.Fori(0, B - 1) as i:
                image(i, False)
            image(B - 1, True)
            eng.wait_ge(s["x_out"], B * per["x_out"] + primed["x_out"])

        @block.gpsimd
        def _(eng):
            halfexp = st[:, :, 7:8]
            eng.sem_inc(s["x_out"], primed["x_out"])
            eng.memset(corr_stage, 0.0).then_inc(s["w_corrz"], 1)
            eng.memset(st[:, :, :], -0.5).then_inc(s["zeros"], 1)
            eng.wait_ge(s["zeros"], 1)
            eng.wait_ge(s["p_rank"], 1)

            def rstd(i, g, k):
                q = 4 * g + k
                wait(eng, "gn_var", i, 2 * q + 2)
                eng.tensor_tensor(st[:, k % 2, 4:5], st[:, k % 2, 3:4], halfexp[:, k % 2, :], ALU.pow).then_inc(s["gn_rstd"], 1)

            def add(i, u, src, base):
                half, o = divmod(u % 8, KC)
                if u == 0:
                    wait(eng, "x_out", i, 0)
                wait(eng, "gemm_evac", i, base + u % 8 + 1)
                c = slice(half * HALF, (half + 1) * HALF)
                eng.tensor_tensor(x[:, o, c], src[:, o, c], tmp[:, u % 3, :], ALU.add).then_inc(s["res_added"], 1)

            def image(i):
                for k in range(KC):
                    rstd(i, 0, k)
                eng.memset(gram[:, :, 0:2], 0.0).then_inc(s["gram_pad"], 1)
                eng.memset(gram[:, :, 2 + WIN:PITCH], 0.0).then_inc(s["gram_pad"], 1)
                eng.memset(gram[:, 0, 2:2 + 64], 0.0).then_inc(s["gram_pad"], 1)
                eng.memset(gram[:, NT - 1, 2 + WIN - 64:2 + WIN], 0.0).then_inc(s["gram_pad"], 1)
                eng.memset(corr3[:, :, :, TAPS:], 0.0).then_inc(s["gram_pad"], 1)
                for u in range(8):
                    add(i, u, x_next, 0)
                    if u >= 5:
                        rstd(i, 1, u - 5)
                rstd(i, 1, 3)
                wait(eng, "gemm_done", i, 8)
                eng.nop(nofuse=True)
                eng.memset(conv_in[:, :, 0:N + 2:N + 1], 0.0).then_inc(s["conv_pad"], 1)
                wait(eng, "row_ready", i, 1)
                wait(eng, "tok_ev", i, KC)
                eng.nop(nofuse=True)
                for h in range(HEADS):
                    for t in range(NT):
                        eng.indirect_dma_start(d_scan[h], bass.IndirectOffsetOnAxis(ap=rank[:, h, t:t + 1], axis=0),
                                               rows4[:, h, t, :], None).then_inc(s["scattered"], 16)
                for h in range(HEADS):
                    wait(eng, "fac_8", i, 5 * h + 5)
                    wait(eng, "m_ev", i, 2 * h)
                    eng.tensor_tensor(diag.rearrange("p (c b t) -> p c b t", c=NT, t=T8),
                                      md8[:, :].rearrange("p (c t) -> p c t", c=NT).unsqueeze(2).broadcast_to([P, NT, 16, T8]),
                                      const("block16").unsqueeze(1).unsqueeze(3).broadcast_to([P, NT, 16, T8]),
                                      ALU.mult).then_inc(s["fac_diag"], 1)
                for h in range(HEADS):
                    wait(eng, "y_out", i, 16 * HEADS)
                    wait(eng, "y_mm", i, 4 * HEADS)
                    eng.nop(nofuse=True)
                    for t in range(NT):
                        eng.indirect_dma_start(ytok[h][:, t, :], None, d_y[h],
                                               bass.IndirectOffsetOnAxis(ap=rank[:, h, t:t + 1], axis=0)).then_inc(s["y_in"], 16)
                for k in range(KC):
                    wait(eng, "y_gate", i, k + 1)
                    wait(eng, "gemm_evac", i, 32)
                    eng.tensor_tensor(gate[:, k, :], gate[:, k, :], res[:, k, :], ALU.add).then_inc(s["y_res"], 1)
                for stg, base in ((1, 32), (2, 40), (3, 48)):
                    for u in range(8):
                        add(i, 8 * stg + u, x, base)
                        if stg < 3 and u >= 5:
                            rstd(i, stg + 1, u - 5)
                    if stg < 3:
                        rstd(i, stg + 1, 3)

            with eng.Fori(0, B) as i:
                image(i)

        @block.scalar
        def _(eng):
            act = eng.activation
            eng.wait_ge(s["a_in"], 64)
            eng.wait_ge(s["par_in"], 16 * 14)
            act(amat[:, :, :].rearrange("p h s -> p (h s)"), mob[:, 8:24], ACT.Exp).then_inc(s["a_exp"], 1)
            for h in range(HEADS):
                act(par[32 * h:32 * h + 8, 59:60], par[32 * h:32 * h + 8, 58:59], ACT.Exp).then_inc(s["a_exp"], 1)
            eng.wait_ge(s["w_scl"], 4)
            for n, (name, k, v) in enumerate(wchunks):
                act(w_hi[name][:, k, :], v, ACT.Copy, scale=par[:, SCL + WI[name]:SCL + WI[name] + 1]).then_inc(s["w_stage"], 1)
            for r in range(3):
                act(w_corr[32 * r:32 * r + 32, :], corr_stage[32 * r:32 * r + 32, :], ACT.Copy, scale=par[32 * r:32 * r + 32, SCL:SCL + 1]).then_inc(s["w_stage"], 1)
            eng.wait_ge(s["p_abcd"], 3)
            act(mob[:, 20:22], mob[:, 18:20], ACT.Sqrt).then_inc(s["p_sqrt"], 1)

            def hi(i, g, k, src):
                q = 4 * g + k
                dst = (even_hi, odd_hi)[g % 2]
                wait(eng, "gn_bias", i, q + 1)
                if g == 0:
                    wait(eng, "gemm_done", i, 0)
                if g == 1:
                    wait(eng, "gemm_done", i, 0)
                if g == 2:
                    wait(eng, "y_out", i, 16 * HEADS)
                if g == 3:
                    wait(eng, "gemm_done", i, 32)
                act(dst[:, k, :], src[:, k, :], ACT.Identity, bias=st[:, k % 2, 5:6], scale=st[:, k % 2, 4:5]).then_inc(s["gn_hi"], 1)

            def evac_res(i, u, base, bias, inv, func):
                half, o = divmod(u % 8, KC)
                wait(eng, "gemm_done", i, base + u % 8 + 1)
                wait(eng, "res_added", i, max(u - 2, 0))
                bank = bank_of[base + u % 8]
                act(tmp[:, u % 3, :], ps[bank][:, :], func, bias=par[:, bias + o:bias + o + 1],
                    scale=inv).then_inc(s["gemm_evac"], 1)

            def inv(name):
                return par[:, INV + WI[name]:INV + WI[name] + 1]

            def evac_unit(i, q):
                o3, half = divmod(q, 2)
                part, o = divmod(o3, KC)
                wait(eng, "gemm_done", i, 8 + q + 1)
                c = slice(half * HALF, (half + 1) * HALF)
                if part == 0:
                    if half == 0 and o >= 2:
                        wait(eng, "conv_mac", i, 3 * (o - 1))
                    dst = conv_in[:, o % 2, 1 + half * HALF:1 + (half + 1) * HALF]
                else:
                    dst = (gate, res)[part - 1][:, o, c]
                col = BIN + (0, 8, 4)[part] + o
                act(dst, ps[bank_of[8 + q]][:, :], ACT.Silu, bias=par[:, col:col + 1], scale=inv("in")).then_inc(s["gemm_evac"], 1)
                if part == 1:
                    wait(eng, "gemm_evac", i, 8 + q + 1)
                    act(dst, dst, ACT.Silu).then_inc(s["silu2"], 1)

            def image(i):
                for k in range(KC):
                    hi(i, 0, k, x_next)
                wait(eng, "gram_d", i, NT)
                act(gdiag[:, 1, :], gdiag[:, 0, :], ACT.Sqrt).then_inc(s["gram_sqrt"], 1)
                for half in range(2):
                    wait(eng, "gram_rb", i, half + 1)
                    act(rnorm[:, 64 + half * HALF:64 + (half + 1) * HALF], ps[7][:, :], ACT.Copy).then_inc(s["gram_row"], 1)
                for half in range(2):
                    wait(eng, "corr_t", i, half + 1)
                    act(corr[0:96, half * HALF:(half + 1) * HALF], ps[(7, 3)[half]][0:96, :], ACT.Copy).then_inc(s["corr_cp"], 1)
                for u in range(8):
                    evac_res(i, u, 0, B0, inv("L0"), ACT.Relu)
                    if u == 5:
                        hi(i, 1, 0, x)
                    if u == 6:
                        hi(i, 1, 1, x)
                hi(i, 1, 2, x)
                hi(i, 1, 3, x)
                wait(eng, "conv_pad", i, 1)
                for q in range(8):
                    evac_unit(i, q)
                    if q in (3, 5, 7):
                        conv_silu(i, (q - 3) // 2)
                fill = iter(range(8, 24))

                def filler(n):
                    for _ in range(n):
                        evac_unit(i, next(fill))

                tok_evac(i, 0)
                filler(1)
                conv_silu(i, 3)
                tok_evac(i, 1)
                filler(1)
                tok_evac(i, 2)
                filler(1)
                tok_evac(i, 3)
                filler(1)
                wait(eng, "sp_dve", i, 1)
                act(sm[:, 4, :], sm[:, 3, :], ACT.Exp, scale=-1.0).then_inc(s["sp_act"], 1)
                wait(eng, "sp_dve", i, 2)
                act(sm[:, 6, :], sm[:, 5, :], ACT.Ln).then_inc(s["sp_act"], 1)
                filler(6)
                for h in range(HEADS):
                    wait(eng, "fac_mm", i, 2 * h + 2)
                    act(gam[32 * h:32 * h + 8, :], ps[7][32 * h:32 * h + 8, 320:328], ACT.Exp,
                        scale=par[32 * h:32 * h + 8, 60:61]).then_inc(s["fac_gam"], 1)
                    for n, t in enumerate((pfac, qfac, arg8[:, :, :].rearrange("p a s -> p (a s)"))):
                        wait(eng, "fac_arg", i, 3 * h + n + 1)
                        act(t, t, ACT.Exp).then_inc(s["fac_exp"], 1)
                    filler(2)
                    for half in range(2):
                        wait(eng, "fac_tp", i, 4 * h + half + 1)
                        act(pT[:, half * HALF:(half + 1) * HALF], ps[3 + half][:, :], ACT.Copy,
                            scale=const("keep")[:, h:h + 1]).then_inc(s["fac_ptq"], 1)
                    for half in range(2):
                        wait(eng, "fac_tp", i, 4 * h + half + 3)
                        act(qT[:, half * HALF:(half + 1) * HALF], ps[5 + half][:, :], ACT.Copy).then_inc(s["fac_ptq"], 1)
                    if h == 0:
                        filler(2)
                    for j in range(4):
                        wait(eng, "y_mm", i, 4 * h + j + 1)
                        act(yscan[:, h, 2 * j:2 * j + 2, :], ps[3 + j % 2][:, :].rearrange("p (c d) -> p c d", c=2),
                            ACT.Copy).then_inc(s["y_ev"], 1)
                for u in range(8):
                    evac_res(i, 8 + u, 32, BOUT, 1.0, ACT.Silu)
                    if u >= 5:
                        hi(i, 2, u - 5, x)
                hi(i, 2, 3, x)
                for u in range(8):
                    evac_res(i, 16 + u, 40, BL2, inv("L2"), ACT.Identity)
                    if u >= 5:
                        hi(i, 3, u - 5, x)
                hi(i, 3, 3, x)
                for u in range(8):
                    evac_res(i, 24 + u, 48, BL3, inv("L3"), ACT.Identity)

            def conv_silu(i, k):
                wait(eng, "conv_mac", i, 3 * k + 3)
                act(conv_out[:, k % 2, :], conv_out[:, k % 2, :], ACT.Silu).then_inc(s["conv_act"], 1)

            def tok_evac(i, k):
                wait(eng, "tok_mm", i, k + 1)
                for half in range(2):
                    ins = act(rows4[:, k // 2, 4 * half:4 * half + 4, (k % 2) * P:(k % 2) * P + P],
                              ps[tok_banks[k % 2][half]][:, :].rearrange("p (t c) -> p t c", t=4), ACT.Copy)
                ins.then_inc(s["tok_ev"], 1)

            with eng.Fori(0, B) as i:
                image(i)

        @block.vector
        def _(eng):
            TT, TS, STT = eng.tensor_tensor, eng.tensor_scalar, eng.scalar_tensor_tensor
            eng.memset(par[:, WMAX:WMAX + 4], 0.0).then_inc(s["w_max"], 1)
            eng.wait_ge(s["cst_in"], 16)
            eng.wait_ge(s["par_in"], 16 * 14)
            eng.wait_ge(s["zeros"], 1)
            eng.wait_ge(s["w_in"], N_W)
            eng.wait_ge(s["w_max"], 1)
            cnt = 1
            parts = [(WI[name], v) for name, k, v in wchunks] + [(0, corr_stage)]
            for w, v in parts:
                eng.tensor_reduce(par[:, 62:63], v, AX.X, ALU.max, apply_absolute_value=True).then_inc(s["w_max"], 1)
                eng.wait_ge(s["w_max"], cnt + 1)
                TT(par[:, WMAX + w:WMAX + w + 1], par[:, WMAX + w:WMAX + w + 1], par[:, 62:63], ALU.max).then_inc(s["w_max"], 1)
                eng.wait_ge(s["w_max"], cnt + 2)
                cnt += 2
            eng.wait_ge(s["w_maxt"], 1)
            eng.tensor_reduce(par[0:4, 62:63], ps[7][0:4, 0:P], AX.X, ALU.max).then_inc(s["w_maxr"], 1)
            eng.wait_ge(s["w_maxr"], 1)
            TS(par[0:4, WMAX:WMAX + 4], ident[0:4, 0:4], par[0:4, 62:63], None, ALU.mult).then_inc(s["w_maxr"], 1)
            eng.wait_ge(s["w_maxb"], 1)
            scl = par[:, SCL:SCL + 4].bitcast(I32)
            invs = par[:, INV:INV + 4].bitcast(I32)
            eng.tensor_copy(par[:, SCL:SCL + 4], ps[7][:, 0:4]).then_inc(s["w_scl"], 1)
            eng.wait_ge(s["w_scl"], 1)
            TS(scl, scl, 0x7F800000, None, ALU.bitwise_and).then_inc(s["w_scl"], 1)
            eng.wait_ge(s["w_scl"], 2)
            TS(invs, scl, float(14 << 23), float(-(13 << 23)), ALU.max, ALU.add).then_inc(s["w_scl"], 1)
            eng.wait_ge(s["w_scl"], 3)
            TS(scl, invs, -1.0, float(254 << 23), ALU.mult, ALU.add).then_inc(s["w_scl"], 1)
            eng.wait_ge(s["w_scl"], 4)
            for n, (name, k, v) in enumerate(wchunks):
                eng.wait_ge(s["w_stage"], n + 1)
                STT(w_lo[name][:, k, :], v, par[:, SCL + WI[name]:SCL + WI[name] + 1], w_hi[name][:, k, :],
                    ALU.mult, ALU.subtract).then_inc(s["w_done"], 2)
            eng.wait_ge(s["w_stage"], len(wchunks) + 3)
            STT(w_corr[64:96, :], corr_stage[64:96, :], par[64:96, SCL:SCL + 1], w_corr[64:96, :],
                ALU.mult, ALU.subtract).then_inc(s["w_done"], 2)
            eng.wait_ge(s["a_exp"], 3)
            TS(amat[:, :, :], amat[:, :, :], -1.0, None, ALU.mult).then_inc(s["p_score"], 1)
            TS(par[0:8, 60:61], par[0:8, 59:60], -1.0, None, ALU.mult).then_inc(s["p_score"], 1)
            TS(par[32:40, 60:61], par[32:40, 59:60], -1.0, None, ALU.mult).then_inc(s["p_score"], 1)
            for h in range(HEADS):
                TS(deq8[:, h, :], const("eq8"), par[:, 56 + h:57 + h], None, ALU.mult).then_inc(s["p_score"], 1)
            m = mob[:, 0:8].rearrange("p (h c) -> p h c", h=HEADS)
            TT(mob[:, 16:18], m[:, :, 0], m[:, :, 3], ALU.mult).then_inc(s["p_abcd"], 1)
            TT(mob[:, 18:20], m[:, :, 1], m[:, :, 2], ALU.mult).then_inc(s["p_abcd"], 1)
            eng.wait_ge(s["p_abcd"], 2)
            TT(mob[:, 16:18], mob[:, 16:18], mob[:, 18:20], ALU.subtract).then_inc(s["p_score"], 1)
            eng.wait_ge(s["p_score"], 6)
            STT(mob[:, 18:20], mob[:, 16:18], -1.0, mob[:, 16:18], ALU.mult, ALU.max).then_inc(s["p_score"], 1)
            eng.wait_ge(s["p_score"], 7)
            TS(mob[:, 18:20], mob[:, 18:20], 0.001, None, ALU.max).then_inc(s["p_abcd"], 1)
            eng.wait_ge(s["p_sqrt"], 1)
            eng.reciprocal(mob[:, 22:24], mob[:, 20:22]).then_inc(s["p_score"], 1)
            c = 8
            eng.wait_ge(s["p_score"], c)
            for h in range(HEADS):
                TS(mob[:, 8 + 4 * h:12 + 4 * h], mob[:, 4 * h:4 * h + 4], mob[:, 22 + h:23 + h], None, ALU.mult).then_inc(s["p_score"], 1)
                c += 1
                eng.wait_ge(s["p_score"], c)

            def score(out, xs, ys, t, h, c):
                a, b, cc, dd = (mob[:, 8 + 4 * h + j:9 + 4 * h + j] for j in range(4))
                nr, dr, di = t
                steps = [
                    lambda: TS(nr, xs, a, b, ALU.mult, ALU.add),
                    lambda: TS(dr, xs, cc, dd, ALU.mult, ALU.add),
                    lambda: TS(di, ys, cc, None, ALU.mult),
                    lambda: TS(dr, dr, 1e-6, None, ALU.add),
                    lambda: STT(out, di, -1.3, dr, ALU.mult, ALU.add),
                    lambda: TT(nr, nr, out, ALU.mult),
                    lambda: STT(out, dr, 1.3, di, ALU.mult, ALU.add),
                    lambda: STT(out, ys, a, out, ALU.mult, ALU.mult),
                    lambda: TT(nr, nr, out, ALU.add),
                    lambda: TT(dr, dr, dr, ALU.mult),
                    lambda: TT(di, di, di, ALU.mult),
                    lambda: TT(dr, dr, di, ALU.add),
                    lambda: eng.reciprocal(dr, dr),
                    lambda: TT(out, nr, dr, ALU.mult),
                ]
                for f in steps:
                    f().then_inc(s["p_score"], 1)
                    c += 1
                    eng.wait_ge(s["p_score"], c)
                return c

            for h in range(HEADS):
                c = score(score_row[:, h, :], grow[:, 0, :], grow[:, 1, :], scr[0:3], h, c)
                c = score(md8[:, 8 * h:8 * h + 8], const("grid")[:, 0:8], const("grid")[:, 8:16],
                          [md8[:, 16 + 8 * a:24 + 8 * a] for a in range(3)], h, c)
            for h in range(HEADS):
                for t in range(NT):
                    own = md8[:, 8 * h + t:8 * h + t + 1]
                    TS(scr[0], score_row[:, h, :], own, None, ALU.is_lt).then_inc(s["p_score"], 1)
                    STT(scr[1], score_row[:, h, :], own, before[:, N - P - t * P:2 * N - P - t * P],
                        ALU.is_equal, ALU.mult).then_inc(s["p_score"], 1)
                    eng.wait_ge(s["p_score"], c + 2)
                    TT(scr[2], scr[0], scr[1], ALU.add).then_inc(s["p_score"], 1)
                    eng.wait_ge(s["p_score"], c + 3)
                    eng.tensor_reduce(md8[:, 48 + t:49 + t], scr[2], AX.X, ALU.add).then_inc(s["p_score"], 1)
                    c += 4
                eng.wait_ge(s["p_score"], c)
                ins = eng.tensor_copy(rank[:, h, :], md8[:, 48:56])
                if h == 0:
                    ins.then_inc(s["p_score"], 1)
                    c += 1
                    eng.wait_ge(s["p_score"], c)
            ins.then_inc(s["p_rank"], 1)
            eng.wait_ge(s["p_rank"], 1)

            def gn_a(i, g, k, src):
                q = 4 * g + k
                if g == 0:
                    eng.wait_ge(s["x_in"], (i + 1) * per["x_in"])
                else:
                    wait(eng, "res_added", i, 8 * (g - 1) + 5 + k)
                for half in range(2):
                    eng.bn_stats(bn[:, k % 2, half, :], src[:, k, half * HALF:(half + 1) * HALF]).then_inc(s["gn_raw"], 1)
                wait(eng, "gn_raw", i, 3 * q + 2)
                eng.nop(nofuse=True)
                eng.bn_aggr(st[:, k % 2, 0:2], bn[:, k % 2, :, :]).then_inc(s["gn_raw"], 1)
                wait(eng, "gn_raw", i, 3 * q + 3)
                STT(st[:, k % 2, 1:2], st[:, k % 2, 0:1], st[:, k % 2, 0:1], st[:, k % 2, 1:2],
                    ALU.mult, ALU.add).then_inc(s["gn_stat"], 1)

            def gn_b(i, g, k):
                q = 4 * g + k
                sums = gn_ps[k % 2]
                wait(eng, "gn_sum", i, q + 1)
                eng.tensor_copy(st[:, k % 2, 0:2], sums).then_inc(s["gn_var"], 1)
                wait(eng, "gn_var", i, 2 * q + 1)
                STT(st[:, k % 2, 2:3], st[:, k % 2, 0:1], st[:, k % 2, 0:1], st[:, k % 2, 1:2],
                    ALU.mult, ALU.subtract).then_inc(s["gn_neg"], 1)
                wait(eng, "gn_neg", i, q + 1)
                TS(st[:, k % 2, 3:4], st[:, k % 2, 2:3], -1.0, EPS, ALU.mult, ALU.add).then_inc(s["gn_var"], 1)

            def gn_c(i, g, k, src):
                q = 4 * g + k
                wait(eng, "gn_rstd", i, q + 1)
                STT(st[:, k % 2, 5:6], st[:, k % 2, 0:1], -1.0, st[:, k % 2, 4:5],
                    ALU.mult, ALU.mult).then_inc(s["gn_bias"], 1)
                wait(eng, "gn_bias", i, q + 1)
                TS(normed[:, k % 2, :], src[:, k, :], st[:, k % 2, 4:5], st[:, k % 2, 5:6],
                   ALU.mult, ALU.add).then_inc(s["gn_split"], 1)

            def gn_d(i, g, k):
                q = 4 * g + k
                his, los = ((even_hi, even_lo), (odd_hi, odd_lo))[g % 2]
                wait(eng, "gn_hi", i, q + 1)
                wait(eng, "gn_split", i, 2 * q + 1)
                TT(los[:, k, :], normed[:, k % 2, :], his[:, k, :], ALU.subtract).then_inc(s["gn_split"], 1)

            def group_norm(i, g, src):
                for k in range(KC):
                    gn_a(i, g, k, src)
                    gn_b(i, g, k)
                    gn_c(i, g, k, src)
                    gn_d(i, g, k)

            def image(i):
                group_norm(i, 0, x_next)
                for t in range(NT):
                    wait(eng, "gram_mm", i, (t | 1) + 1)
                    eng.tensor_tensor_reduce(normed[:, 0, t * P:(t + 1) * P], gram_ps(t)[:, 64:64 + P], ident, 1.0, 0.0,
                                             ALU.mult, ALU.add, gdiag[:, 0, t:t + 1]).then_inc(s["gram_d"], 1)
                wait(eng, "gram_sqrt", i, 1)
                TS(gdiag[:, 1, :], gdiag[:, 1, :], 1e-12, None, ALU.max).then_inc(s["gram_r"], 1)
                wait(eng, "gram_r", i, 1)
                eng.reciprocal(gdiag[:, 0, :], gdiag[:, 1, :]).then_inc(s["gram_r"], 1)
                wait(eng, "gram_r", i, 2)
                wait(eng, "yt_mm", i, 0)
                TT(rdiag, ident.unsqueeze(1).broadcast_to([P, NT, P]),
                   gdiag[:, 0, :].unsqueeze(2).broadcast_to([P, NT, P]), ALU.mult).then_inc(s["gram_rd"], 1)
                wait(eng, "gram_row", i, 2)
                for t in range(NT):
                    a, z = (64 if t == 0 else 0), (WIN - 64 if t == NT - 1 else WIN)
                    STT(gram[:, t, 2 + a:2 + z], gram_ps(t)[:, a:z], gdiag[:, 0, t:t + 1],
                        rnorm[:, t * P + a:t * P + z], ALU.mult, ALU.mult).then_inc(s["gram_ev"], 1)
                wait(eng, "gram_in", i, 16 * NT)
                TT(corr3[:, :, :, 0:TAPS], corr_tok.unsqueeze(2).broadcast_to([P, NT, 3, TAPS]),
                   const("inside").rearrange("p (t k) -> p t k", t=NT).unsqueeze(2).broadcast_to([P, NT, 3, TAPS]),
                   ALU.mult).then_inc(s["corr_msk"], 1)
                for half in range(2):
                    wait(eng, "corr_cp", i, half + 1)
                    c = slice(half * HALF, (half + 1) * HALF)
                    TT(corr[32:64, c], ps[(7, 3)[half]][32:64, :], corr[32:64, c], ALU.subtract).then_inc(s["corr_lo"], 1)
                group_norm(i, 1, x)
                for k in range(KC):
                    wait(eng, "gemm_evac", i, 8 + 2 * k + 2)
                    wait(eng, "conv_pad", i, 1)
                    if k >= 2:
                        wait(eng, "tok_mm", i, k - 1)
                    src, dst = conv_in[:, k % 2, :], conv_out[:, k % 2, :]
                    w = [par[:, TAP + 3 * k + j:TAP + 3 * k + j + 1] for j in range(3)]
                    TS(dst, src[:, 1:N + 1], w[1], par[:, BCONV + k:BCONV + k + 1], ALU.mult, ALU.add).then_inc(s["conv_mac"], 1)
                    wait(eng, "conv_mac", i, 3 * k + 1)
                    STT(dst, src[:, 0:N], w[0], dst, ALU.mult, ALU.add).then_inc(s["conv_mac"], 1)
                    wait(eng, "conv_mac", i, 3 * k + 2)
                    STT(dst, src[:, 2:N + 2], w[2], dst, ALU.mult, ALU.add).then_inc(s["conv_mac"], 1)
                wait(eng, "dbc_mm", i, 1)
                dbc = rows4[:, :, :, DH:ROW]
                for h in range(HEADS):
                    ins = TT(rows4[:, h, :, DH:ROW], ps[0][:, 0:NT * HEADS * J].rearrange("p (t h j) -> p h t j", t=NT, h=HEADS)[:, h],
                             bdbc_sb[:, h * J:(h + 1) * J].unsqueeze(1).broadcast_to([P, NT, J]), ALU.add)
                    ins.then_inc(s["sp_z"], 1)
                wait(eng, "sp_z", i, 2)
                z = rows4[:, :, :, DH]
                v = lambda a: sm[:, a, :].rearrange("p (h t) -> p h t", h=HEADS)
                STT(v(3), z, -1.0, z, ALU.mult, ALU.max).then_inc(s["sp_dve"], 1)
                wait(eng, "sp_act", i, 1)
                TS(v(5), v(4), 1.0, None, ALU.add).then_inc(s["sp_dve"], 1)
                wait(eng, "sp_dve", i, 2)
                TS(v(7), v(5), -1.0, None, ALU.add).then_inc(s["sp_dve"], 1)
                wait(eng, "sp_dve", i, 3)
                TS(v(3), v(7), 0.0, None, ALU.is_equal).then_inc(s["sp_dve"], 1)
                wait(eng, "sp_dve", i, 4)
                wait(eng, "sp_act", i, 2)
                TT(v(7), v(7), v(3), ALU.add).then_inc(s["sp_dve"], 1)
                TT(v(6), v(6), v(3), ALU.add).then_inc(s["sp_dve"], 1)
                wait(eng, "sp_dve", i, 6)
                eng.reciprocal(v(5), v(7)).then_inc(s["sp_dve"], 1)
                TT(v(6), v(6), v(4), ALU.mult).then_inc(s["sp_dve"], 1)
                wait(eng, "sp_dve", i, 8)
                TT(v(6), v(6), v(5), ALU.mult).then_inc(s["sp_dve"], 1)
                wait(eng, "sp_dve", i, 9)
                STT(z, z, 0.0, v(6), ALU.max, ALU.add).then_inc(s["sp_dve"], 1)
                wait(eng, "sp_dve", i, 10)
                for h in range(HEADS):
                    ins = TT(rows4[:, h, :, DH + 1:DH + 1 + S], rows4[:, h, :, DH + 1:DH + 1 + S],
                             rows4[:, h, :, DH].unsqueeze(2).broadcast_to([P, NT, S]), ALU.mult)
                ins.then_inc(s["row_ready"], 1)
                for h in range(HEADS):
                    scan_vec(i, h)
                for k in range(KC):
                    wait(eng, "yt_mm", i, k + 1)
                    wait(eng, "silu2", i, 8)
                    for half in range(2):
                        c = slice(half * HALF, (half + 1) * HALF)
                        ins = TT(gate[:, k, c], ps[yt_banks[k % 2][half]][:, :], gate[:, k, c], ALU.mult)
                    ins.then_inc(s["y_gate"], 1)
                group_norm(i, 2, x)
                group_norm(i, 3, x)

            def scan_vec(i, h):
                r = rows4[:, h]
                dt, wgt, cst_c = r[:, :, DH], r[:, :, DH + 1:DH + 1 + S], r[:, :, DH + 1 + S:ROW]
                wait(eng, "scanrows", i, 16 * HEADS)
                wait(eng, "fac_mm", i, 2 * h)
                dtg = dt.unsqueeze(2).broadcast_to([P, NT, G])
                left = const("left").rearrange("p (h g) -> p h g", h=HEADS)[:, h]
                right = const("right").rearrange("p (h g) -> p h g", h=HEADS)[:, h]
                TT(mv[:, 0], dtg, left.unsqueeze(1).broadcast_to([P, NT, G]), ALU.mult).then_inc(s["fac_mv"], 1)
                TT(mv[:, 1], dtg, right.unsqueeze(1).broadcast_to([P, NT, G]), ALU.mult).then_inc(s["fac_mv"], 1)
                TT(mv8[:, :, :], dt.unsqueeze(2).broadcast_to([P, NT, T8]),
                   const("within8").unsqueeze(1).broadcast_to([P, NT, T8]), ALU.mult).then_inc(s["fac_mv"], 1)
                TT(mvc[:, :, :, :], cst_c.unsqueeze(2).broadcast_to([P, NT, T8, S]),
                   const("eq8").unsqueeze(1).unsqueeze(3).broadcast_to([P, NT, T8, S]), ALU.mult).then_inc(s["fac_mv"], 1)
                a = amat[:, h, :].unsqueeze(1)
                wait(eng, "fac_mm", i, 2 * h + 2)
                wait(eng, "fac_gam", i, h + 1)
                wait(eng, "y_mm", i, 4 * h)
                for n, (dst, lo, cols) in enumerate(((pfac, 0, P), (qfac, P, P), (arg8[:, :, :].rearrange("p a s -> p (a s)"), 2 * P, 64))):
                    TT(dst.rearrange("p (c s) -> p c s", s=S), ps[7][:, lo:lo + cols].unsqueeze(2).broadcast_to([P, cols, S]),
                       a.broadcast_to([P, cols, S]), ALU.mult).then_inc(s["fac_arg"], 1)
                p4 = pfac.rearrange("p (c g s) -> p c g s", c=NT, g=G)
                q4 = qfac.rearrange("p (c g s) -> p c g s", c=NT, g=G)
                wait(eng, "fac_exp", i, 3 * h + 1)
                TT(p4, p4, wgt.unsqueeze(2).broadcast_to([P, NT, G, S]), ALU.mult).then_inc(s["fac_pq"], 1)
                wait(eng, "fac_exp", i, 3 * h + 2)
                TT(q4, q4, cst_c.unsqueeze(2).broadcast_to([P, NT, G, S]), ALU.mult).then_inc(s["fac_pq"], 1)
                wait(eng, "fac_exp", i, 3 * h + 3)
                a8 = arg8[:, :, :].rearrange("p (c t) s -> p c t s", c=NT)
                TT(arg8[:, :, :], ps[0][:, :].rearrange("p (a s) -> p a s", s=S), arg8[:, :, :], ALU.mult).then_inc(s["fac_8"], 1)
                wait(eng, "fac_8", i, 5 * h + 1)
                TT(a8, a8, wgt.unsqueeze(2).broadcast_to([P, NT, T8, S]), ALU.mult).then_inc(s["fac_8"], 1)
                wait(eng, "fac_8", i, 5 * h + 2)
                wait(eng, "fac_diag", i, h)
                eng.tensor_reduce(md8[:, :], arg8[:, :, :], AX.X, ALU.add).then_inc(s["fac_8"], 1)
                wait(eng, "fac_8", i, 5 * h + 3)
                m8 = md8[:, :].rearrange("p (c t) -> p c t", c=NT)
                TT(m8, m8, const("within8").unsqueeze(1).broadcast_to([P, NT, T8]), ALU.mult).then_inc(s["fac_8"], 1)
                wait(eng, "fac_8", i, 5 * h + 4)
                TT(m8, m8, deq8[:, h, :].unsqueeze(1).broadcast_to([P, NT, T8]), ALU.add).then_inc(s["fac_8"], 1)
                hp = slice(32 * h, 32 * h + 8)
                for c in range(NT - 1):
                    wait(eng, "dh_mm", i, 4 * h + c // 2 + 1)
                    inc = ps[dh_bank(c)][hp, (c % 2) * DH:(c % 2 + 1) * DH]
                    if c == 0:
                        eng.tensor_copy(hst[hp, 0, :], inc).then_inc(s["h_st"], 1)
                    else:
                        wait(eng, "h_st", i, 7 * h + c)
                        STT(hst[hp, c, :], hst[hp, c - 1, :], gam[hp, c:c + 1], inc, ALU.mult, ALU.add).then_inc(s["h_st"], 1)
                wait(eng, "fac_diag", i, h + 1)
                for half in range(2):
                    wait(eng, "mm_m", i, 2 * h + half + 1)
                    c = slice(half * HALF, (half + 1) * HALF)
                    TT(mmat[:, c], ps[3 + half][:, :], diag[:, c], ALU.add).then_inc(s["m_ev"], 1)

            with eng.Fori(0, B) as i:
                image(i)

        @block.tensor
        def _(eng):
            def mm(out, lhsT, rhs, start, stop, **kw):
                return eng.matmul(out, lhsT, rhs, start=start, stop=stop, skip_group_check=True, **kw)

            eng.wait_ge(s["cst_in"], 16)
            eng.wait_ge(s["w_max"], 1 + 2 * (len(wchunks) + 1))
            eng.transpose(ps[7][0:4, 0:P], par[:, WMAX:WMAX + 4], ident).then_inc(s["w_maxt"], 1)
            eng.wait_ge(s["w_maxr"], 2)
            mm(ps[7][:, 0:4], const("ones")[0:4, :], par[0:4, WMAX:WMAX + 4], True, True).then_inc(s["w_maxb"], 1)
            eng.wait_ge(s["p_rank"], 1)
            eng.wait_ge(s["w_done"], len(wchunks) * 2 + 2)

            def gn_sum(i, g, k):
                wait(eng, "gn_stat", i, 4 * g + k + 1)
                mm(gn_ps[k % 2], const("group_mean"), st[:, k % 2, 0:2], True, True).then_inc(s["gn_sum"], 1)

            def passes(wname, his, los, o, half, k, bank, start, stop):
                c = slice(half * HALF, (half + 1) * HALF)
                oc = slice(o * P, (o + 1) * P)
                a = ((w_hi[wname], his), (w_hi[wname], los), (w_lo[wname], his))
                for n, (w, v) in enumerate(a):
                    ins = mm(ps[bank][:, :], w[:, k, oc], v[:, k, c], start and n == 0, stop and n == 2)
                return ins

            def free_bank(i, n):
                wait(eng, "gemm_evac", i, bank_free[n])
                if 35 <= n <= 38:
                    wait(eng, "y_gate", i, KC)

            def behind(i, g, base, ready, part):
                for k in range(KC):
                    if g is not None and k in (1, 2):
                        gn_sum(i, g, k + 1)
                    ready(k)
                    for u in range(3):
                        if k == 0:
                            free_bank(i, base + u)
                        ins = part(u, k)
                        if k == KC - 1:
                            ins.then_inc(s["gemm_done"], 1)

            def image(i):
                for k in range(KC):
                    gn_sum(i, 0, k)
                wait(eng, "gn_split", i, 2 * KC)
                wait(eng, "gemm_evac", i, 0)
                for t in range(NT):
                    a, z = (64 if t == 0 else 0), (WIN - 64 if t == NT - 1 else WIN)
                    tok, win = slice(t * P, (t + 1) * P), slice(t * P - 64 + a, t * P - 64 + z)
                    for k in range(KC):
                        for n, (l, r) in enumerate(((even_hi, even_hi), (even_hi, even_lo), (even_lo, even_hi))):
                            ins = mm(gram_ps(t)[:, a:z], l[:, k, tok], r[:, k, win], k == 0 and n == 0, k == KC - 1 and n == 2)
                    ins.then_inc(s["gram_mm"], 1)
                def main(u):
                    half, o = divmod(u, KC)
                    for k in range(KC):
                        passes("L0", even_hi, even_lo, o, half, k, bank_of[u], k == 0, False)

                def corr_part(u):
                    half, o = divmod(u, KC)
                    mm(ps[bank_of[u]][:, :], w_corr[0:96, o * P:(o + 1) * P], corr[0:96, half * HALF:(half + 1) * HALF],
                       False, True).then_inc(s["gemm_done"], 1)

                main(0)
                main(1)
                wait(eng, "gram_rd", i, 1)
                for half in range(2):
                    wait(eng, "gram_row", i, half)
                    mm(ps[7][:, :], const("ones"), rdiag[:, 4 * half:4 * half + 4, :].rearrange("p t k -> p (t k)"),
                       True, True).then_inc(s["gram_rb"], 1)
                main(2)
                wait(eng, "gram_ev", i, NT)
                for u in (3, 4, 5):
                    main(u)
                wait(eng, "corr_msk", i, 1)
                wait(eng, "gram_pad", i, 5)
                wait(eng, "gram_row", i, 2)
                for half in range(2):
                    for t in range(4):
                        ins = eng.transpose(ps[(7, 3)[half]][0:96, t * P:(t + 1) * P],
                                            corr3[:, 4 * half + t].rearrange("p a k -> p (a k)"), ident)
                    ins.then_inc(s["corr_t"], 1)
                wait(eng, "corr_lo", i, 1)
                for u in (0, 1, 2, 3):
                    corr_part(u)
                wait(eng, "corr_lo", i, 2)
                for u in (4, 5):
                    corr_part(u)
                for u in (6, 7):
                    wait(eng, "gemm_evac", i, u - 5)
                    main(u)
                    corr_part(u)
                    if u == 7:
                        gn_sum(i, 1, 0)
                gn_sum(i, 1, 1)
                def in_part(q, k):
                    o3, half = divmod(q, 2)
                    part, o = divmod(o3, KC)
                    col = (0, 2, 1)[part] * KC + o
                    return passes("in", odd_hi, odd_lo, col, half, k, bank_of[8 + q], k == 0, k == KC - 1)

                def in_unit(q):
                    free_bank(i, 8 + q)
                    for k in range(KC):
                        ins = in_part(q, k)
                    ins.then_inc(s["gemm_done"], 1)

                behind(i, 1, 8, lambda k: wait(eng, "gn_split", i, 2 * (4 + k) + 2), in_part)
                for q in range(3, 8):
                    in_unit(q)
                fill = iter(range(8, 24))

                def filler(n):
                    for _ in range(n):
                        in_unit(next(fill))

                def tokens(k):
                    wait(eng, "conv_act", i, k + 1)
                    if k == 0:
                        wait(eng, "gemm_evac", i, 16)
                    if k >= 2:
                        wait(eng, "tok_ev", i, k - 1)
                    for t in range(NT):
                        lhsT = conv_out[:, k % 2, t * P:(t + 1) * P]
                        ins = mm(ps[0][:, t * HEADS * J:(t + 1) * HEADS * J], lhsT, w_dbc[:, k, :],
                                 k == 0 and t == 0, k == KC - 1)
                        if k == KC - 1 and t == NT - 1:
                            ins.then_inc(s["dbc_mm"], 1)
                    for t in range(NT):
                        ins = eng.transpose(ps[tok_banks[k % 2][t // 4]][:, (t % 4) * P:(t % 4 + 1) * P],
                                            conv_out[:, k % 2, t * P:(t + 1) * P], ident)
                    ins.then_inc(s["tok_mm"], 1)

                for k in range(KC):
                    tokens(k)
                    filler(1)
                filler(6)
                for h in range(HEADS):
                    wait(eng, "fac_mv", i, 4 * h + 4)
                    r = rows4[:, h]
                    offl = const("off_left").rearrange("p (h g) -> p h g", h=HEADS)[:, h].unsqueeze(1).broadcast_to([P, NT, G])
                    offr = const("off_right").rearrange("p (h g) -> p h g", h=HEADS)[:, h].unsqueeze(1).broadcast_to([P, NT, G])
                    b7 = ps[7]
                    v3 = lambda t: t.rearrange("p (c g) -> p c g", c=NT)
                    mm(v3(b7[:, 0:P]), after, mv[:, 0], True, False)
                    mm(v3(b7[:, 0:P]), ident, offl, False, True)
                    mm(v3(b7[:, P:2 * P]), upto, mv[:, 1], True, False)
                    mm(v3(b7[:, P:2 * P]), ident, offr, False, True)
                    mm(b7[:, 2 * P:2 * P + 64].rearrange("p (c t) -> p c t", c=NT), after8, mv8[:, :, :], True, True)
                    mm(b7[0:40, 320:328], const("ones")[:, 0:40], r[:, :, DH], True, True).then_inc(s["fac_mm"], 1)
                    if h == 0:
                        wait(eng, "sp_z", i, 2)
                    else:
                        wait(eng, "fac_8", i, 1)
                    mm(ps[0][:, :].rearrange("p (c t s) -> p c t s", c=NT, t=T8).rearrange("p c t s -> p (c t s)"), same8,
                       mvc[:, :, :, :].rearrange("p c t s -> p (c t s)"), True, True).then_inc(s["fac_mm"], 1)
                    filler(2)
                    if h == 0:
                        wait(eng, "tok_ev", i, KC)
                    else:
                        wait(eng, "y_ev", i, 4)
                        wait(eng, "h_st", i, 7)
                    for a, f in enumerate((pfac, qfac)):
                        wait(eng, "fac_pq", i, 2 * h + a + 1)
                        for c in range(NT):
                            ins = eng.transpose(ps[3 + 2 * a + c // 4][:, (c % 4) * P:(c % 4 + 1) * P],
                                                f[:, c * P:(c + 1) * P], ident)
                            if c % 4 == 3:
                                ins.then_inc(s["fac_tp"], 1)
                    for half in range(2):
                        wait(eng, "fac_ptq", i, 4 * h + (3 if half == 0 else 4))
                        for c in range(4 * half, 4 * half + 4):
                            ins = mm(ps[3 + half][:, (c % 4) * P:(c % 4 + 1) * P], pT[:, c * P:(c + 1) * P],
                                     qT[:, c * P:(c + 1) * P], True, True)
                        ins.then_inc(s["mm_m"], 1)
                    far = FAR_GROUP[h] * S
                    for c in range(NT - 1):
                        if c >= 4 and c % 2 == 0:
                            wait(eng, "h_st", i, 7 * h + c - 2)
                        ins = mm(ps[dh_bank(c)][32 * h:32 * h + 8, (c % 2) * DH:(c % 2 + 1) * DH],
                                 pfac[:, c * P + far:c * P + far + S], r[:, c, 0:DH], True, True)
                        if c % 2 == 1 or c == NT - 2:
                            ins.then_inc(s["dh_mm"], 1)
                    if h == 0:
                        filler(2)
                    for c in range(NT):
                        j = c // 2
                        wait(eng, "m_ev", i, 2 * h + 2)
                        if j >= 2:
                            wait(eng, "y_ev", i, 4 * h + j - 1)
                        out = ps[3 + j % 2][:, (c % 2) * DH:(c % 2 + 1) * DH]
                        ins = mm(out, mmat[:, c * P:(c + 1) * P], r[:, c, 0:DH], True, c == 0)
                        if c > 0:
                            wait(eng, "h_st", i, 7 * h + c)
                            ins = mm(out, qT[far:far + S, c * P:(c + 1) * P], hst[far:far + S, c - 1, :], False, True)
                        if c % 2 == 1:
                            ins.then_inc(s["y_mm"], 1)
                for k in range(KC):
                    if k == 0:
                        wait(eng, "y_in", i, 16 * HEADS * NT)
                        wait(eng, "y_ev", i, 4 * HEADS)
                        wait(eng, "h_st", i, 7 * HEADS)
                    if k >= 2:
                        wait(eng, "y_gate", i, k - 1)
                    for t in range(NT):
                        ins = eng.transpose(ps[yt_banks[k % 2][t // 4]][:, (t % 4) * P:(t % 4 + 1) * P],
                                            ytok[k // 2][:, t, (k % 2) * P:(k % 2 + 1) * P], ident)
                    ins.then_inc(s["yt_mm"], 1)
                def out_part(u, k):
                    half, o = divmod(u, KC)
                    return mm(ps[bank_of[32 + u]][:, :], w_out[:, k, o * P:(o + 1) * P],
                              gate[:, k, half * HALF:(half + 1) * HALF], k == 0, k == KC - 1)

                def split_part(stg, u, k):
                    half, o = divmod(u, KC)
                    his, los = ((even_hi, even_lo), (odd_hi, odd_lo))[stg % 2]
                    return passes("L%d" % stg, his, los, o, half, k, bank_of[24 + 8 * stg + u], k == 0, k == KC - 1)

                def stage_gemm(stg, base, ready, part):
                    behind(i, stg if stg > 1 else None, base, ready, part)
                    for u in range(3, 8):
                        free_bank(i, base + u)
                        for k in range(KC):
                            ins = part(u, k)
                        ins.then_inc(s["gemm_done"], 1)
                        if stg < 3 and u >= 6:
                            gn_sum(i, stg + 1, u - 6)

                stage_gemm(1, 32, lambda k: wait(eng, "y_res", i, k + 1), out_part)
                stage_gemm(2, 40, lambda k: wait(eng, "gn_split", i, 2 * (8 + k) + 2), lambda u, k: split_part(2, u, k))
                stage_gemm(3, 48, lambda k: wait(eng, "gn_split", i, 2 * (12 + k) + 2), lambda u, k: split_part(3, u, k))

            with eng.Fori(0, B) as i:
                image(i)
    return nc


def kernel(**inputs):
    import concourse.bacc as bacc
    from concourse.bass_utils import run_bass_kernel_spmd as run

    g = {k: np.asarray(v) for k, v in inputs.items()}
    _, packed, before, grid = constants()
    cols = lambda b: b.reshape(-1, P).T
    conv_w = g["L0_conv_conv_w"]
    alog = g["L1_conv_A_log"]
    arrays = {
        "x": g["x"].reshape(B, C, N),
        "w0t": conv_w[:, :C].T,
        "wct": conv_w[:, C:].reshape(C, 5, 5).transpose(2, 1, 0).reshape(TAPS, C),
        "wint": g["L1_conv_in_proj_w"].T,
        "woutt": g["L1_conv_out_proj_w"].T,
        "wdbct": g["L1_conv_dbc_w"].T,
        "w2t": g["L2_conv_weight"].T,
        "w3t": g["L3_conv_weight"].T,
        "b0": cols(g["L0_conv_conv_b"]), "bin": cols(g["L1_conv_in_proj_b"]), "bconv": cols(g["L1_conv_dw_b"]),
        "bout": cols(g["L1_conv_out_proj_b"]), "bl2": cols(g["L2_conv_bias"]), "bl3": cols(g["L3_conv_bias"]),
        "bdbc": g["L1_conv_dbc_b"].reshape(1, HEADS * J),
        "taps": g["L1_conv_dw_w"].reshape(KC, P, 3).transpose(1, 0, 2).reshape(P, 3 * KC),
        "alog": alog.reshape(1, HEADS * S), "alog_col": alog.reshape(HEADS, S, 1),
        "dpar": g["L1_conv_Dparam"].reshape(1, HEADS), "mob": g["L1_conv_mobius"].reshape(1, 4 * HEADS),
        "cst": packed, "before": before, "grid": grid,
    }
    nc = bacc.Bacc("TRN2", target_bir_lowering=False, num_devices=1)
    feed, d = {}, {}
    for name, a in arrays.items():
        feed["in_" + name] = a = np.ascontiguousarray(a)
        d[name] = nc.dram_tensor("in_" + name, a.shape, mybir.dt.from_np(a.dtype), kind="ExternalInput").ap()
    d["out"] = nc.dram_tensor("out_x", (B, C, N), F32, kind="ExternalOutput").ap()
    build(nc, d)
    r = run(nc, [feed], core_ids=[0])
    return r.results[0]["out_x"].reshape(B, C, H, W)
```

```python
from contextlib import ExitStack

import numpy as np

import concourse.bass as bass
from concourse import mybir

F32, F16, I32 = mybir.dt.float32, mybir.dt.float16, mybir.dt.int32
ALU, ACT, AX = mybir.AluOpType, mybir.ActivationFunctionType, mybir.AxisListType

P = 128
B, C, H, W = 8, 512, 32, 32
N = H * W
KC = C // P
HALF = 512
NT = N // P
S, HEADS = 8, 2
DH = C // HEADS
J = 1 + 2 * S
ROW = DH + J
G = 16
T8 = 8
TAPS = 25
ROWS_T = P // W
WIN = 2 * P
PITCH = WIN + 4
EPS = 1e-5
BIG = 1e20
FAR_GROUP = (0, 4)


def constants():
    v = np.arange(P)
    parts = {}
    parts["ident"] = np.eye(P)
    parts["upto"] = v[:, None] <= v[None, :]
    parts["after"] = v[:, None] > v[None, :]
    same8 = (v[:, None] // T8) == (v[None, :] // T8)
    parts["same8"] = same8
    parts["after8"] = same8 & (v[:, None] > v[None, :])
    parts["group_mean"] = ((v[:, None] // 16) == (v[None, :] // 16)) / 16.0
    parts["ones"] = np.ones((P, P))
    blocks = [(s, size) for size in (128, 64, 32, 16) for s in range(0, P, size)]
    left, right = np.zeros((P, HEADS, G)), np.zeros((P, HEADS, G))
    keep = np.ones((P, HEADS))
    for h in range(HEADS):
        groups = [g for g in range(G) if g != FAR_GROUP[h]]
        for g, (s, size) in zip(groups, blocks):
            left[s:s + size // 2, h, g] = 1
            right[s + size // 2:s + size, h, g] = 1
        left[:, h, FAR_GROUP[h]] = right[:, h, FAR_GROUP[h]] = 1
        keep[FAR_GROUP[h] * S:(FAR_GROUP[h] + 1) * S, h] = 0
    parts["left"], parts["right"] = left, right
    parts["off_left"], parts["off_right"] = BIG * (1 - left), BIG * (1 - right)
    parts["keep"] = keep
    parts["within8"] = (v[:, None] % T8) <= np.arange(T8)[None, :]
    parts["eq8"] = (v[:, None] % T8) == np.arange(T8)[None, :]
    parts["block16"] = (v[:, None] // T8) == np.arange(P // T8)[None, :]
    n = np.arange(N).reshape(NT, P).T
    y, x = n // W, n % W
    inside = np.zeros((P, NT, 5, 5))
    for r in range(5):
        for c in range(5):
            inside[:, :, r, c] = ((y + r - 2 >= 0) & (y + r - 2 < H) & (x + c - 2 >= 0) & (x + c - 2 < W))
    parts["inside"] = inside
    step = np.arange(W - 1, dtype=np.float32) / np.float32(W - 1)
    line = np.concatenate([np.float32(-1) * (np.float32(1) - step) + step, [np.float32(1)]]).astype(np.float32)
    parts["grid"] = np.concatenate([line[x], line[y]], axis=1)
    at, cols = {}, []
    pos = 0
    for name, a in parts.items():
        a = np.asarray(a, np.float32).reshape(P, -1)
        at[name] = (pos, a.shape[1])
        pos += a.shape[1]
        cols.append(a)
    j = np.arange(2 * N - P)
    before = (j[None, :] - (N - P) < v[:, None]).astype(np.float32)
    n = np.arange(N)
    return at, np.concatenate(cols, axis=1), before, np.stack([line[n % W], line[n // W]])


def build(nc, d):
    at, packed, before_np, _ = constants()
    with ExitStack() as ctx:
        def sb(name, shape, dt=F32):
            return ctx.enter_context(nc.sbuf_tensor(name, shape, dt))

        def sem(name):
            return ctx.enter_context(nc.semaphore(name))

        w_hi = {"L0": sb("w0_hi", [P, KC, C], F16), "in": sb("win_hi", [P, KC, 3 * C], F16),
                "L2": sb("w2_hi", [P, KC, C], F16), "L3": sb("w3_hi", [P, KC, C], F16)}
        w_lo = {"L0": sb("w0_lo", [P, KC, C], F16), "in": sb("win_lo", [P, KC, 3 * C], F16),
                "L2": sb("w2_lo", [P, KC, C], F16), "L3": sb("w3_lo", [P, KC, C], F16)}
        w_corr = sb("w_corr", [P, C], F16)
        w_out = sb("w_out", [P, KC, C])
        w_dbc = sb("w_dbc", [P, KC, HEADS * J])
        cst = sb("cst", [P, packed.shape[1]])

        def const(name):
            o, n = at[name]
            return cst[:, o:o + n]

        ident, upto, after, same8, after8 = map(const, ("ident", "upto", "after", "same8", "after8"))
        x = sb("x", [P, KC, N])
        x_next = sb("x_next", [P, KC, N])
        even = sb("even", [P, KC * N + 16])
        odd = sb("odd", [P, KC * N])
        gate = sb("gate", [P, KC, N])
        res = sb("res", [P, KC, N])
        rows = sb("rows", [P, HEADS * NT * ROW])
        work = sb("work", [P, 2 * N])
        work2 = sb("work2", [P, 7 * DH])
        arg8 = sb("arg8", [P, NT * T8, S])
        mvc = sb("mvc", [P, NT, T8, S])
        mv = sb("mv", [P, 2, NT, G])
        mv8 = sb("mv8", [P, NT, T8])
        md8 = sb("md8", [P, NT * T8])
        gam = sb("gam", [P, NT])
        sm = sb("sm", [P, 8, 16])
        bn = sb("bn", [P, KC, 2, 6])
        st = sb("st", [P, KC, 8])
        par = sb("par", [P, 64])
        corr = sb("corr", [P, 2 * HALF], F16)
        rank = sb("rank", [P, HEADS, NT], I32)
        deq8 = sb("deq8", [P, HEADS, T8])
        amat = sb("amat", [P, HEADS, S])
        gdiag = sb("gdiag", [P, 2, NT])

        def pair(t):
            v = t[:, 0:KC * N].bitcast(F16).rearrange("p (a k n) -> p a k n", a=2, k=KC)
            return v[:, 0], v[:, 1]

        even_hi, even_lo = pair(even)
        odd_hi, odd_lo = pair(odd)
        conv_in = even[:, 0:2 * (N + 2)].rearrange("p (b n) -> p b n", b=2)
        conv_out = even[:, 2 * (N + 2):2 * (N + 2) + 2 * N].rearrange("p (b n) -> p b n", b=2)
        yscan = even[:, 0:KC * N].rearrange("p (h c d) -> p h c d", h=HEADS, c=NT)
        rows4 = rows[:, :].rearrange("p (h t r) -> p h t r", h=HEADS, t=NT)
        ytok = [rows[:, h * NT * ROW:h * NT * ROW + NT * DH].rearrange("p (t d) -> p t d", t=NT)
                for h in range(HEADS)]
        gram = rows[:, 0:NT * PITCH].rearrange("p (t w) -> p t w", t=NT)
        rnorm = rows[:, NT * PITCH:NT * PITCH + N + 2 * 64]
        rdiag = rows[:, NT * PITCH + N + 128:NT * PITCH + 2 * N + 128].rearrange("p (t k) -> p t k", t=NT)
        corr_tok = gate[:, 0, 0:NT * TAPS].rearrange("p (t k) -> p t k", t=NT)
        corr3 = gate[:, 1, 0:NT * 96].rearrange("p (t a k) -> p t a k", t=NT, a=3)
        xn = x_next[:, :, :].rearrange("p k n -> p (k n)")
        pfac, qfac, pT, qT = (xn[:, a * N:(a + 1) * N] for a in range(4))
        mmat = work[:, 0:N]
        diag = work[:, N:2 * N]
        normed = work[:, :].rearrange("p (b n) -> p b n", b=2)
        tmp = work2[:, 0:3 * HALF].rearrange("p (b n) -> p b n", b=3)
        hst = work2[:, :].rearrange("p (c d) -> p c d", c=7)

        bdbc_sb = sb("bdbc_sb", [P, HEADS * J])
        ps = [ctx.enter_context(nc.psum_tensor(f"bank{i}", [P, HALF], F32)) for i in range(8)]

        gn_ps = ps[7][:, 0:2]
        gram_ps = lambda t: ps[t // 2][:, (t % 2) * WIN:(t % 2 + 1) * WIN]
        tok_banks = ((4, 5), (6, 3))
        yt_banks = ((3, 4), (5, 6), (3, 4), (3, 4))
        dh_bank = lambda c: 5 + (c // 2) % 2
        bank_of = ([4, 5, 6, 0, 1, 2, 3, 4] + [0, 1, 2, 3, 6, 4, 5, 0] + [1, 2] * 8
                   + [0, 1, 2, 5, 6, 3, 4, 0] + [1, 2, 3, 4, 5, 6, 0, 1] + [2, 3, 4, 5, 6, 0, 1, 2])
        bank_free = [max([p + 1 for p in range(n) if bank_of[p] == bank_of[n]], default=0) for n in range(56)]

        d_gram = nc.dram_tensor("d_gram", (NT, P, PITCH), F32, kind="Internal").ap()
        d_scan = [nc.dram_tensor(f"d_scan{h}", (N, ROW), F32, kind="Internal").ap() for h in range(HEADS)]
        d_y = [nc.dram_tensor(f"d_y{h}", (N, DH), F32, kind="Internal").ap() for h in range(HEADS)]

        B0, BIN, BCONV, BOUT, BL2, BL3, TAP, WMAX, SCL, INV = 0, 4, 16, 20, 24, 28, 32, 44, 48, 52
        WI = {"L0": 0, "in": 1, "L2": 2, "L3": 3}

        names = """w_in w_stage w_done w_max w_maxt w_maxr w_maxb w_scl w_corrz par_in cst_in
            p_abcd p_sqrt p_score p_rank a_in a_exp
            x_in x_out gn_raw gn_stat gn_sum gn_got gn_var gn_neg gn_rstd gn_bias gn_hi gn_split
            gram_mm gram_d gram_sqrt gram_r gram_rd gram_rb gram_row gram_ev gram_pad gram_out gram_in corr_msk corr_t corr_cp corr_lo
            gemm_done gemm_evac res_added
            conv_pad conv_mac conv_act tok_mm tok_ev dbc_mm sp_z sp_dve sp_act row_ready scattered0 scattered1 scanrows0 scanrows1
            fac_mv fac_mm fac_arg fac_exp fac_gam fac_pq fac_8 fac_diag fac_tp fac_ptq mm_m m_ev dh_mm h_st y_mm y_ev y_out0 y_out1 y_in0 y_in1
            yt_mm y_gate y_res silu2 zeros""".split()
        s = {n: sem(n) for n in names}
        per = dict(x_in=16 * KC, x_out=16 * KC, gn_raw=48, gn_stat=16, gn_sum=16, gn_got=16, gn_var=16, gn_neg=16, gn_rstd=16,
                   gn_bias=16, gn_hi=16, gn_split=32,
                   gram_mm=NT, gram_d=NT, gram_sqrt=1, gram_r=2, gram_rd=1, gram_rb=2, gram_row=2, gram_ev=NT,
                   gram_pad=5, gram_out=16, gram_in=16 * NT, corr_msk=1, corr_t=2, corr_cp=2, corr_lo=2,
                   gemm_done=56, gemm_evac=56, res_added=32,
                   conv_pad=1, conv_mac=3 * KC, conv_act=KC, tok_mm=KC, tok_ev=KC, dbc_mm=1, sp_z=2,
                   sp_dve=10, sp_act=2, row_ready=1, scattered0=16 * NT, scattered1=16 * NT, scanrows0=16, scanrows1=16,
                   fac_mv=8, fac_mm=2 * HEADS, fac_arg=3 * HEADS, fac_exp=3 * HEADS, fac_gam=HEADS, fac_pq=2 * HEADS,
                   fac_8=5 * HEADS, fac_diag=HEADS, fac_tp=4 * HEADS, fac_ptq=4 * HEADS, mm_m=2 * HEADS,
                   m_ev=2 * HEADS, dh_mm=4 * HEADS, h_st=7 * HEADS, y_mm=4 * HEADS, y_ev=4 * HEADS,
                   y_out0=16, y_out1=16, y_in0=16 * NT, y_in1=16 * NT, yt_mm=KC, y_gate=KC, y_res=KC, silu2=8)

        primed = {"x_out": 16}

        def wait(eng, name, i, n):
            if n or name in primed:
                eng.wait_ge(s[name], i * per[name] + n + primed.get(name, 0))

        def gn_split_n(g, k):
            return 8 * g + 2 * k + 2

        block = ctx.enter_context(nc.Block())

        wsrc = {"L0": (d["w0t"], C), "in": (d["wint"], 3 * C), "L2": (d["w2t"], C), "L3": (d["w3t"], C)}
        flat = lambda t: t[:, :, :].rearrange("p k n -> p (k n)")
        stage = {"L0": flat(x)[:, 0:KC * C], "L2": flat(x)[:, KC * C:2 * KC * C],
                 "L3": xn[:, 0:KC * C],
                 "in0": flat(gate), "in1": flat(res)[:, 0:2 * C]}
        in_stage = [flat(gate)[:, 0:3 * C], flat(gate)[:, 3 * C:6 * C], flat(res)[:, 0:3 * C], flat(res)[:, 3 * C:6 * C]] \
            if 6 * C <= KC * N else None
        wchunks = []
        for name in ("L0", "L2", "L3"):
            for k in range(KC):
                wchunks.append((name, k, stage[name][:, k * C:(k + 1) * C]))
        for k in range(KC):
            wchunks.append(("in", k, in_stage[k]))
        corr_stage = xn[:, KC * C:KC * C + C]
        before = odd[:, 0:2 * N - P]
        grow = even[:, 0:2 * N].rearrange("p (a n) -> p a n", a=2)
        score_row = work[:, :].rearrange("p (h n) -> p h n", h=HEADS)
        scr = [even[:, (2 + a) * N:(3 + a) * N] for a in range(2)] + [odd[:, 2 * N:3 * N], odd[:, 3 * N:4 * N]]
        mob = sb("mob", [P, 24])
        N_W = 16 * (12 + 4 + 3)

        @block.sync
        def _(eng):
            eng.dma_start(cst[:, :], d["cst"]).then_inc(s["cst_in"], 16)
            for name, k, v in wchunks:
                src, n = wsrc[name]
                eng.dma_start(v, src[k * P:(k + 1) * P, :]).then_inc(s["w_in"], 16)
            eng.wait_ge(s["w_corrz"], 1)
            for r in range(3):
                eng.dma_start(corr_stage[32 * r:32 * r + TAPS, :], d["wct"]).then_inc(s["w_in"], 16)
            eng.dma_start(before, d["before"]).then_inc(s["par_in"], 16)
            for a in range(2):
                eng.dma_start(grow[:, a, :], d["grid"][a:a + 1, :].broadcast_to([P, N])).then_inc(s["par_in"], 16)
            eng.dma_start(mob[:, 0:8], d["mob"].broadcast_to([P, 8])).then_inc(s["par_in"], 16)
            for name, col, n in (("b0", B0, 4), ("bin", BIN, 12), ("bconv", BCONV, 4), ("bout", BOUT, 4),
                                 ("bl2", BL2, 4), ("bl3", BL3, 4)):
                eng.dma_start(par[:, col:col + n], d[name]).then_inc(s["par_in"], 16)
            eng.dma_start(par[:, TAP:TAP + 3 * KC], d["taps"]).then_inc(s["par_in"], 16)
            eng.dma_start(w_out[:, :, :], d["woutt"].rearrange("(k p) o -> p k o", p=P)).then_inc(s["par_in"], 16)
            eng.dma_start(w_dbc[:, :, :], d["wdbct"].rearrange("(k p) o -> p k o", p=P)).then_inc(s["par_in"], 16)
            eng.dma_start(bdbc_sb[:, :], d["bdbc"].broadcast_to([P, HEADS * J])).then_inc(s["par_in"], 16)
            eng.dma_start(mob[:, 8:24], d["alog"].broadcast_to([P, 16])).then_inc(s["a_in"], 16)
            eng.dma_start(par[:, 56:58], d["dpar"].broadcast_to([P, 2])).then_inc(s["a_in"], 16)
            for h in range(HEADS):
                eng.dma_start(par[32 * h:32 * h + 8, 58:59], d["alog_col"][h]).then_inc(s["a_in"], 16)
            eng.wait_ge(s["w_done"], len(wchunks) * 2 + 2)
            for k in range(KC):
                eng.dma_start(x_next[:, k, :], d["x"][0, k * P:(k + 1) * P, :]).then_inc(s["x_in"], 16)

            def image(i, last):
                wait(eng, "gram_ev", i, NT)
                wait(eng, "gram_pad", i, 5)
                eng.dma_start(d_gram.rearrange("t p w -> p t w"), gram).then_inc(s["gram_out"], 16)
                wait(eng, "gram_out", i, 16)
                for t in range(NT):
                    band = bass.AP(d_gram.tensor, d_gram.offset + t * P * PITCH, [[PITCH + 1, P], [W, 5], [1, 5]])
                    eng.dma_start(corr_tok[:, t, :].rearrange("p (r c) -> p r c", r=5), band).then_inc(s["gram_in"], 16)
                for h in range(HEADS):
                    wait(eng, f"scattered{h}", i, 16 * NT)
                    eng.dma_start(rows4[:, h], d_scan[h].rearrange("(c p) r -> p c r", p=P)).then_inc(s[f"scanrows{h}"], 16)
                for h in range(HEADS):
                    wait(eng, "y_ev", i, 4 * (h + 1))
                    eng.dma_start(d_y[h].rearrange("(c p) r -> p c r", p=P), yscan[:, h]).then_inc(s[f"y_out{h}"], 16)
                if not last:
                    wait(eng, "y_mm", i, 4 * HEADS)
                    for k in range(KC):
                        eng.dma_start(x_next[:, k, :], d["x"][bass.ds(i + 1, 1), k * P:(k + 1) * P, :].rearrange("a p n -> (a p) n")).then_inc(s["x_in"], 16)
                for k in range(KC):
                    wait(eng, "res_added", i, 29 + k)
                    eng.dma_start(d["out"][bass.ds(i, 1), k * P:(k + 1) * P, :].rearrange("a p n -> (a p) n"), x[:, k, :]).then_inc(s["x_out"], 16)

            with eng.Fori(0, B - 1) as i:
                image(i, False)
            image(B - 1, True)
            eng.wait_ge(s["x_out"], B * per["x_out"] + primed["x_out"])

        @block.gpsimd
        def _(eng):
            minus_half = st[:, :, 7:8]
            eng.sem_inc(s["x_out"], primed["x_out"])
            eng.memset(corr_stage, 0.0).then_inc(s["w_corrz"], 1)
            eng.memset(st[:, :, :], -0.5).then_inc(s["zeros"], 1)
            eng.wait_ge(s["zeros"], 1)
            eng.wait_ge(s["p_rank"], 1)

            def rstd(i, g, k):
                q = 4 * g + k
                wait(eng, "gn_var", i, q + 1)
                eng.tensor_tensor(st[:, k, 4:5], st[:, k, 3:4], minus_half[:, k, :], ALU.pow).then_inc(s["gn_rstd"], 1)

            def add(i, u, src, base):
                half, o = divmod(u % 8, KC)
                if u == 0:
                    wait(eng, "x_out", i, 0)
                wait(eng, "gemm_evac", i, base + u % 8 + 1)
                c = slice(half * HALF, (half + 1) * HALF)
                eng.tensor_tensor(x[:, o, c], src[:, o, c], tmp[:, u % 3, :], ALU.add).then_inc(s["res_added"], 1)

            for k in range(KC):
                rstd(0, 0, k)

            def image(i, last):
                eng.memset(gram[:, :, 0:2], 0.0).then_inc(s["gram_pad"], 1)
                eng.memset(gram[:, :, 2 + WIN:PITCH], 0.0).then_inc(s["gram_pad"], 1)
                eng.memset(gram[:, 0, 2:2 + 64], 0.0).then_inc(s["gram_pad"], 1)
                eng.memset(gram[:, NT - 1, 2 + WIN - 64:2 + WIN], 0.0).then_inc(s["gram_pad"], 1)
                eng.memset(corr3[:, :, :, TAPS:], 0.0).then_inc(s["gram_pad"], 1)
                adds(i, 0, x_next, 0)
                wait(eng, "gemm_done", i, 8)
                eng.nop(nofuse=True)
                eng.memset(conv_in[:, :, 0:N + 2:N + 1], 0.0).then_inc(s["conv_pad"], 1)
                wait(eng, "row_ready", i, 1)
                wait(eng, "tok_ev", i, KC)
                eng.nop(nofuse=True)
                for h in range(HEADS):
                    for t in range(NT):
                        eng.indirect_dma_start(d_scan[h], bass.IndirectOffsetOnAxis(ap=rank[:, h, t:t + 1], axis=0),
                                               rows4[:, h, t, :], None).then_inc(s[f"scattered{h}"], 16)
                def diagonal(h):
                    wait(eng, "fac_8", i, 5 * h + 5)
                    wait(eng, "m_ev", i, 2 * h)
                    eng.tensor_tensor(diag.rearrange("p (c b t) -> p c b t", c=NT, t=T8),
                                      md8[:, :].rearrange("p (c t) -> p c t", c=NT).unsqueeze(2).broadcast_to([P, NT, 16, T8]),
                                      const("block16").unsqueeze(1).unsqueeze(3).broadcast_to([P, NT, 16, T8]),
                                      ALU.mult).then_inc(s["fac_diag"], 1)

                def gather(h):
                    wait(eng, f"y_out{h}", i, 16)
                    wait(eng, "y_mm", i, 4 * (h + 1))
                    eng.nop(nofuse=True)
                    for t in range(NT):
                        eng.indirect_dma_start(ytok[h][:, t, :], None, d_y[h],
                                               bass.IndirectOffsetOnAxis(ap=rank[:, h, t:t + 1], axis=0)).then_inc(s[f"y_in{h}"], 16)

                diagonal(0)
                diagonal(1)
                gather(0)
                gather(1)
                for k in range(KC):
                    wait(eng, "y_gate", i, k + 1)
                    wait(eng, "gemm_evac", i, 32)
                    eng.tensor_tensor(gate[:, k, :], gate[:, k, :], res[:, k, :], ALU.add).then_inc(s["y_res"], 1)
                adds(i, 1, x, 32)
                adds(i, 2, x, 40)
                for u in range(8):
                    add(i, 24 + u, x, 48)
                    if 2 <= u < 6 and not last:
                        rstd(i + 1, 0, u - 2)

            def adds(i, stg, src, base):
                for u in range(8):
                    add(i, 8 * stg + u, src, base)
                    if u >= 6:
                        rstd(i, stg + 1, u - 6)
                rstd(i, stg + 1, 2)
                rstd(i, stg + 1, 3)

            with eng.Fori(0, B - 1) as i:
                image(i, False)
            image(B - 1, True)

        @block.scalar
        def _(eng):
            act = eng.activation
            eng.wait_ge(s["a_in"], 64)
            eng.wait_ge(s["par_in"], 16 * 14)
            act(amat[:, :, :].rearrange("p h s -> p (h s)"), mob[:, 8:24], ACT.Exp).then_inc(s["a_exp"], 1)
            for h in range(HEADS):
                act(par[32 * h:32 * h + 8, 59:60], par[32 * h:32 * h + 8, 58:59], ACT.Exp).then_inc(s["a_exp"], 1)
            eng.wait_ge(s["w_scl"], 4)
            for n, (name, k, v) in enumerate(wchunks):
                act(w_hi[name][:, k, :], v, ACT.Copy, scale=par[:, SCL + WI[name]:SCL + WI[name] + 1]).then_inc(s["w_stage"], 1)
            for r in range(3):
                act(w_corr[32 * r:32 * r + 32, :], corr_stage[32 * r:32 * r + 32, :], ACT.Copy, scale=par[32 * r:32 * r + 32, SCL:SCL + 1]).then_inc(s["w_stage"], 1)
            eng.wait_ge(s["p_abcd"], 3)
            act(mob[:, 20:22], mob[:, 18:20], ACT.Sqrt).then_inc(s["p_sqrt"], 1)

            def hi(i, g, k, src):
                q = 4 * g + k
                dst = (even_hi, odd_hi)[g % 2]
                wait(eng, "gn_bias", i, q + 1)
                if g == 2:
                    wait(eng, "y_out0", i, 16)
                    wait(eng, "y_out1", i, 16)
                if g == 3:
                    wait(eng, "gemm_done", i, 32)
                act(dst[:, k, :], src[:, k, :], ACT.Identity, bias=st[:, k, 5:6], scale=st[:, k, 4:5]).then_inc(s["gn_hi"], 1)

            def evac_res(i, u, base, bias, inv, func):
                half, o = divmod(u % 8, KC)
                wait(eng, "gemm_done", i, base + u % 8 + 1)
                wait(eng, "res_added", i, max(u - 2, 0))
                bank = bank_of[base + u % 8]
                act(tmp[:, u % 3, :], ps[bank][:, :], func, bias=par[:, bias + o:bias + o + 1],
                    scale=inv).then_inc(s["gemm_evac"], 1)

            def inv(name):
                return par[:, INV + WI[name]:INV + WI[name] + 1]

            def evac_unit(i, q):
                o3, half = divmod(q, 2)
                part, o = divmod(o3, KC)
                wait(eng, "gemm_done", i, 8 + q + 1)
                c = slice(half * HALF, (half + 1) * HALF)
                if part == 0:
                    if half == 0 and o >= 2:
                        wait(eng, "conv_mac", i, 3 * (o - 1))
                    dst = conv_in[:, o % 2, 1 + half * HALF:1 + (half + 1) * HALF]
                else:
                    dst = (gate, res)[part - 1][:, o, c]
                col = BIN + (0, 8, 4)[part] + o
                act(dst, ps[bank_of[8 + q]][:, :], ACT.Silu, bias=par[:, col:col + 1], scale=inv("in")).then_inc(s["gemm_evac"], 1)
                if part == 1:
                    wait(eng, "gemm_evac", i, 8 + q + 1)
                    act(dst, dst, ACT.Silu).then_inc(s["silu2"], 1)

            for k in range(KC):
                hi(0, 0, k, x_next)

            def evacs(i, u0, base, bias, scale, func):
                for u in range(8):
                    evac_res(i, u0 + u, base, bias, scale, func)
                    if u >= 6:
                        hi(i, u0 // 8 + 1, u - 6, x)
                hi(i, u0 // 8 + 1, 2, x)
                hi(i, u0 // 8 + 1, 3, x)

            def image(i, last):
                wait(eng, "gram_d", i, NT)
                act(gdiag[:, 1, :], gdiag[:, 0, :], ACT.Sqrt).then_inc(s["gram_sqrt"], 1)
                for half in range(2):
                    wait(eng, "gram_rb", i, half + 1)
                    act(rnorm[:, 64 + half * HALF:64 + (half + 1) * HALF], ps[7][:, :], ACT.Copy).then_inc(s["gram_row"], 1)
                for half in range(2):
                    wait(eng, "corr_t", i, half + 1)
                    act(corr[0:96, half * HALF:(half + 1) * HALF], ps[7][0:96, :], ACT.Copy).then_inc(s["corr_cp"], 1)
                evacs(i, 0, 0, B0, inv("L0"), ACT.Relu)
                wait(eng, "conv_pad", i, 1)
                for q in range(8):
                    evac_unit(i, q)
                    if q in (3, 5, 7):
                        conv_silu(i, (q - 3) // 2)
                fill = iter(range(8, 24))

                def filler(n):
                    for _ in range(n):
                        evac_unit(i, next(fill))

                tok_evac(i, 0)
                filler(1)
                conv_silu(i, 3)
                tok_evac(i, 1)
                filler(1)
                tok_evac(i, 2)
                filler(1)
                wait(eng, "sp_dve", i, 1)
                act(sm[:, 4, :], sm[:, 3, :], ACT.Exp, scale=-1.0).then_inc(s["sp_act"], 1)
                wait(eng, "sp_dve", i, 2)
                act(sm[:, 6, :], sm[:, 5, :], ACT.Ln).then_inc(s["sp_act"], 1)
                tok_evac(i, 3)
                filler(7)
                for h in range(HEADS):
                    wait(eng, "fac_mm", i, 2 * h + 2)
                    act(gam[32 * h:32 * h + 8, :], ps[7][32 * h:32 * h + 8, 320:328], ACT.Exp,
                        scale=par[32 * h:32 * h + 8, 60:61]).then_inc(s["fac_gam"], 1)
                    for n, t in enumerate((pfac, qfac, arg8[:, :, :].rearrange("p a s -> p (a s)"))):
                        wait(eng, "fac_arg", i, 3 * h + n + 1)
                        act(t, t, ACT.Exp).then_inc(s["fac_exp"], 1)
                    filler(2 - h)
                    for half in range(2):
                        wait(eng, "fac_tp", i, 4 * h + half + 1)
                        act(pT[:, half * HALF:(half + 1) * HALF], ps[3 + half][:, :], ACT.Copy,
                            scale=const("keep")[:, h:h + 1]).then_inc(s["fac_ptq"], 1)
                    for half in range(2):
                        wait(eng, "fac_tp", i, 4 * h + half + 3)
                        act(qT[:, half * HALF:(half + 1) * HALF], ps[5 + half][:, :], ACT.Copy).then_inc(s["fac_ptq"], 1)
                    filler(1 + h)
                    for j in range(4):
                        wait(eng, "y_mm", i, 4 * h + j + 1)
                        act(yscan[:, h, 2 * j:2 * j + 2, :], ps[3 + j % 2][:, :].rearrange("p (c d) -> p c d", c=2),
                            ACT.Copy).then_inc(s["y_ev"], 1)
                evacs(i, 8, 32, BOUT, 1.0, ACT.Silu)
                evacs(i, 16, 40, BL2, inv("L2"), ACT.Identity)
                for u in range(8):
                    evac_res(i, 24 + u, 48, BL3, inv("L3"), ACT.Identity)
                    if 3 <= u < 7 and not last:
                        wait(eng, "gemm_done", i, 48)
                        hi(i + 1, 0, u - 3, x_next)

            def conv_silu(i, k):
                wait(eng, "conv_mac", i, 3 * k + 3)
                act(conv_out[:, k % 2, :], conv_out[:, k % 2, :], ACT.Silu).then_inc(s["conv_act"], 1)

            def tok_evac(i, k):
                wait(eng, "tok_mm", i, k + 1)
                for half in range(2):
                    ins = act(rows4[:, k // 2, 4 * half:4 * half + 4, (k % 2) * P:(k % 2) * P + P],
                              ps[tok_banks[k % 2][half]][:, :].rearrange("p (t c) -> p t c", t=4), ACT.Copy)
                ins.then_inc(s["tok_ev"], 1)

            with eng.Fori(0, B - 1) as i:
                image(i, False)
            image(B - 1, True)

        @block.vector
        def _(eng):
            TT, TS, STT = eng.tensor_tensor, eng.tensor_scalar, eng.scalar_tensor_tensor
            eng.memset(par[:, WMAX:WMAX + 4], 0.0).then_inc(s["w_max"], 1)
            eng.wait_ge(s["cst_in"], 16)
            eng.wait_ge(s["par_in"], 16 * 14)
            eng.wait_ge(s["zeros"], 1)
            eng.wait_ge(s["w_in"], N_W)
            eng.wait_ge(s["w_max"], 1)
            cnt = 1
            parts = [(WI[name], v) for name, k, v in wchunks] + [(0, corr_stage)]
            for w, v in parts:
                eng.tensor_reduce(par[:, 62:63], v, AX.X, ALU.max, apply_absolute_value=True).then_inc(s["w_max"], 1)
                eng.wait_ge(s["w_max"], cnt + 1)
                TT(par[:, WMAX + w:WMAX + w + 1], par[:, WMAX + w:WMAX + w + 1], par[:, 62:63], ALU.max).then_inc(s["w_max"], 1)
                eng.wait_ge(s["w_max"], cnt + 2)
                cnt += 2
            eng.wait_ge(s["w_maxt"], 1)
            eng.tensor_reduce(par[0:4, 62:63], ps[7][0:4, 0:P], AX.X, ALU.max).then_inc(s["w_maxr"], 1)
            eng.wait_ge(s["w_maxr"], 1)
            TS(par[0:4, WMAX:WMAX + 4], ident[0:4, 0:4], par[0:4, 62:63], None, ALU.mult).then_inc(s["w_maxr"], 1)
            eng.wait_ge(s["w_maxb"], 1)
            scl = par[:, SCL:SCL + 4].bitcast(I32)
            invs = par[:, INV:INV + 4].bitcast(I32)
            eng.tensor_copy(par[:, SCL:SCL + 4], ps[7][:, 0:4]).then_inc(s["w_scl"], 1)
            eng.wait_ge(s["w_scl"], 1)
            TS(scl, scl, 0x7F800000, None, ALU.bitwise_and).then_inc(s["w_scl"], 1)
            eng.wait_ge(s["w_scl"], 2)
            TS(invs, scl, float(14 << 23), float(-(13 << 23)), ALU.max, ALU.add).then_inc(s["w_scl"], 1)
            eng.wait_ge(s["w_scl"], 3)
            TS(scl, invs, -1.0, float(254 << 23), ALU.mult, ALU.add).then_inc(s["w_scl"], 1)
            eng.wait_ge(s["w_scl"], 4)
            for n, (name, k, v) in enumerate(wchunks):
                eng.wait_ge(s["w_stage"], n + 1)
                STT(w_lo[name][:, k, :], v, par[:, SCL + WI[name]:SCL + WI[name] + 1], w_hi[name][:, k, :],
                    ALU.mult, ALU.subtract).then_inc(s["w_done"], 2)
            eng.wait_ge(s["w_stage"], len(wchunks) + 3)
            STT(w_corr[64:96, :], corr_stage[64:96, :], par[64:96, SCL:SCL + 1], w_corr[64:96, :],
                ALU.mult, ALU.subtract).then_inc(s["w_done"], 2)
            eng.wait_ge(s["a_exp"], 3)
            TS(amat[:, :, :], amat[:, :, :], -1.0, None, ALU.mult).then_inc(s["p_score"], 1)
            TS(par[0:8, 60:61], par[0:8, 59:60], -1.0, None, ALU.mult).then_inc(s["p_score"], 1)
            TS(par[32:40, 60:61], par[32:40, 59:60], -1.0, None, ALU.mult).then_inc(s["p_score"], 1)
            for h in range(HEADS):
                TS(deq8[:, h, :], const("eq8"), par[:, 56 + h:57 + h], None, ALU.mult).then_inc(s["p_score"], 1)
            m = mob[:, 0:8].rearrange("p (h c) -> p h c", h=HEADS)
            TT(mob[:, 16:18], m[:, :, 0], m[:, :, 3], ALU.mult).then_inc(s["p_abcd"], 1)
            TT(mob[:, 18:20], m[:, :, 1], m[:, :, 2], ALU.mult).then_inc(s["p_abcd"], 1)
            eng.wait_ge(s["p_abcd"], 2)
            TT(mob[:, 16:18], mob[:, 16:18], mob[:, 18:20], ALU.subtract).then_inc(s["p_score"], 1)
            eng.wait_ge(s["p_score"], 6)
            STT(mob[:, 18:20], mob[:, 16:18], -1.0, mob[:, 16:18], ALU.mult, ALU.max).then_inc(s["p_score"], 1)
            eng.wait_ge(s["p_score"], 7)
            TS(mob[:, 18:20], mob[:, 18:20], 0.001, None, ALU.max).then_inc(s["p_abcd"], 1)
            eng.wait_ge(s["p_sqrt"], 1)
            eng.reciprocal(mob[:, 22:24], mob[:, 20:22]).then_inc(s["p_score"], 1)
            c = 8
            eng.wait_ge(s["p_score"], c)
            for h in range(HEADS):
                TS(mob[:, 8 + 4 * h:12 + 4 * h], mob[:, 4 * h:4 * h + 4], mob[:, 22 + h:23 + h], None, ALU.mult).then_inc(s["p_score"], 1)
                c += 1
                eng.wait_ge(s["p_score"], c)

            def score(out, xs, ys, t, h, c):
                a, b, cc, dd = (mob[:, 8 + 4 * h + j:9 + 4 * h + j] for j in range(4))
                nr, dr, di = t
                steps = [
                    lambda: TS(nr, xs, a, b, ALU.mult, ALU.add),
                    lambda: TS(dr, xs, cc, dd, ALU.mult, ALU.add),
                    lambda: TS(di, ys, cc, None, ALU.mult),
                    lambda: TS(dr, dr, 1e-6, None, ALU.add),
                    lambda: STT(out, di, -1.3, dr, ALU.mult, ALU.add),
                    lambda: TT(nr, nr, out, ALU.mult),
                    lambda: STT(out, dr, 1.3, di, ALU.mult, ALU.add),
                    lambda: STT(out, ys, a, out, ALU.mult, ALU.mult),
                    lambda: TT(nr, nr, out, ALU.add),
                    lambda: TT(dr, dr, dr, ALU.mult),
                    lambda: TT(di, di, di, ALU.mult),
                    lambda: TT(dr, dr, di, ALU.add),
                    lambda: eng.reciprocal(dr, dr),
                    lambda: TT(out, nr, dr, ALU.mult),
                ]
                for f in steps:
                    f().then_inc(s["p_score"], 1)
                    c += 1
                    eng.wait_ge(s["p_score"], c)
                return c

            for h in range(HEADS):
                c = score(score_row[:, h, :], grow[:, 0, :], grow[:, 1, :], scr[0:3], h, c)
                c = score(md8[:, 8 * h:8 * h + 8], const("grid")[:, 0:8], const("grid")[:, 8:16],
                          [md8[:, 16 + 8 * a:24 + 8 * a] for a in range(3)], h, c)
            for h in range(HEADS):
                for t in range(NT):
                    own = md8[:, 8 * h + t:8 * h + t + 1]
                    TS(scr[0], score_row[:, h, :], own, None, ALU.is_lt).then_inc(s["p_score"], 1)
                    STT(scr[1], score_row[:, h, :], own, before[:, N - P - t * P:2 * N - P - t * P],
                        ALU.is_equal, ALU.mult).then_inc(s["p_score"], 1)
                    eng.wait_ge(s["p_score"], c + 2)
                    TT(scr[2], scr[0], scr[1], ALU.add).then_inc(s["p_score"], 1)
                    eng.wait_ge(s["p_score"], c + 3)
                    eng.tensor_reduce(md8[:, 48 + t:49 + t], scr[2], AX.X, ALU.add).then_inc(s["p_score"], 1)
                    c += 4
                eng.wait_ge(s["p_score"], c)
                ins = eng.tensor_copy(rank[:, h, :], md8[:, 48:56])
                if h == 0:
                    ins.then_inc(s["p_score"], 1)
                    c += 1
                    eng.wait_ge(s["p_score"], c)
            ins.then_inc(s["p_rank"], 1)
            eng.wait_ge(s["p_rank"], 1)

            def gn_stats(i, g, k, half, src):
                if g == 0:
                    eng.wait_ge(s["x_in"], (i + 1) * per["x_in"])
                else:
                    wait(eng, "res_added", i, 8 * (g - 1) + 4 * half + k + 1)
                eng.bn_stats(bn[:, k, half, :], src[:, k, half * HALF:(half + 1) * HALF]).then_inc(s["gn_raw"], 1)

            def gn_a(i, g, k, src):
                q = 12 * g + 4 + 2 * k
                gn_stats(i, g, k, 1, src)
                wait(eng, "gn_raw", i, q + 1)
                eng.nop(nofuse=True)
                eng.bn_aggr(st[:, k, 0:2], bn[:, k, :, :]).then_inc(s["gn_raw"], 1)
                wait(eng, "gn_raw", i, q + 2)
                STT(st[:, k, 1:2], st[:, k, 0:1], st[:, k, 0:1], st[:, k, 1:2],
                    ALU.mult, ALU.add).then_inc(s["gn_stat"], 1)

            def gn_b(i, g, k):
                q = 4 * g + k
                wait(eng, "gn_sum", i, q + 1)
                eng.tensor_copy(st[:, k, 0:2], gn_ps).then_inc(s["gn_got"], 1)
                wait(eng, "gn_got", i, q + 1)
                STT(st[:, k, 2:3], st[:, k, 0:1], st[:, k, 0:1], st[:, k, 1:2],
                    ALU.mult, ALU.subtract).then_inc(s["gn_neg"], 1)
                wait(eng, "gn_neg", i, q + 1)
                TS(st[:, k, 3:4], st[:, k, 2:3], -1.0, EPS, ALU.mult, ALU.add).then_inc(s["gn_var"], 1)

            def gn_c(i, g, k, src):
                q = 4 * g + k
                wait(eng, "gn_rstd", i, q + 1)
                STT(st[:, k, 5:6], st[:, k, 0:1], -1.0, st[:, k, 4:5],
                    ALU.mult, ALU.mult).then_inc(s["gn_bias"], 1)
                wait(eng, "gn_bias", i, q + 1)
                TS(normed[:, k % 2, :], src[:, k, :], st[:, k, 4:5], st[:, k, 5:6],
                   ALU.mult, ALU.add).then_inc(s["gn_split"], 1)

            def gn_d(i, g, k):
                q = 4 * g + k
                his, los = ((even_hi, even_lo), (odd_hi, odd_lo))[g % 2]
                wait(eng, "gn_hi", i, q + 1)
                wait(eng, "gn_split", i, gn_split_n(g, k) - 1)
                TT(los[:, k, :], normed[:, k % 2, :], his[:, k, :], ALU.subtract).then_inc(s["gn_split"], 1)

            def group_norm(i, g, src):
                for k in range(KC):
                    gn_stats(i, g, k, 0, src)
                gn_a(i, g, 0, src)
                gn_a(i, g, 1, src)
                gn_b(i, g, 0)
                gn_a(i, g, 2, src)
                gn_c(i, g, 0, src)
                gn_b(i, g, 1)
                gn_a(i, g, 3, src)
                gn_d(i, g, 0)
                gn_c(i, g, 1, src)
                gn_b(i, g, 2)
                gn_d(i, g, 1)
                gn_c(i, g, 2, src)
                gn_b(i, g, 3)
                gn_d(i, g, 2)
                gn_c(i, g, 3, src)
                gn_d(i, g, 3)

            group_norm(0, 0, x_next)

            def image(i, last):
                for t in range(NT):
                    wait(eng, "gram_mm", i, (t | 1) + 1)
                    eng.tensor_tensor_reduce(normed[:, 0, t * P:(t + 1) * P], gram_ps(t)[:, 64:64 + P], ident, 1.0, 0.0,
                                             ALU.mult, ALU.add, gdiag[:, 0, t:t + 1]).then_inc(s["gram_d"], 1)
                wait(eng, "gram_sqrt", i, 1)
                TS(gdiag[:, 1, :], gdiag[:, 1, :], 1e-12, None, ALU.max).then_inc(s["gram_r"], 1)
                wait(eng, "gram_r", i, 1)
                eng.reciprocal(gdiag[:, 0, :], gdiag[:, 1, :]).then_inc(s["gram_r"], 1)
                wait(eng, "gram_r", i, 2)
                wait(eng, "yt_mm", i, 0)
                TT(rdiag, ident.unsqueeze(1).broadcast_to([P, NT, P]),
                   gdiag[:, 0, :].unsqueeze(2).broadcast_to([P, NT, P]), ALU.mult).then_inc(s["gram_rd"], 1)
                wait(eng, "gram_row", i, 2)
                for t in range(NT):
                    a, z = (64 if t == 0 else 0), (WIN - 64 if t == NT - 1 else WIN)
                    STT(gram[:, t, 2 + a:2 + z], gram_ps(t)[:, a:z], gdiag[:, 0, t:t + 1],
                        rnorm[:, t * P + a:t * P + z], ALU.mult, ALU.mult).then_inc(s["gram_ev"], 1)
                wait(eng, "gram_in", i, 16 * NT)
                TT(corr3[:, :, :, 0:TAPS], corr_tok.unsqueeze(2).broadcast_to([P, NT, 3, TAPS]),
                   const("inside").rearrange("p (t k) -> p t k", t=NT).unsqueeze(2).broadcast_to([P, NT, 3, TAPS]),
                   ALU.mult).then_inc(s["corr_msk"], 1)
                for half in range(2):
                    wait(eng, "corr_cp", i, half + 1)
                    c = slice(half * HALF, (half + 1) * HALF)
                    TT(corr[32:64, c], ps[7][32:64, :], corr[32:64, c], ALU.subtract).then_inc(s["corr_lo"], 1)
                group_norm(i, 1, x)
                for k in range(KC):
                    wait(eng, "gemm_evac", i, 8 + 2 * k + 2)
                    wait(eng, "conv_pad", i, 1)
                    if k >= 2:
                        wait(eng, "tok_mm", i, k - 1)
                    src, dst = conv_in[:, k % 2, :], conv_out[:, k % 2, :]
                    w = [par[:, TAP + 3 * k + j:TAP + 3 * k + j + 1] for j in range(3)]
                    TS(dst, src[:, 1:N + 1], w[1], par[:, BCONV + k:BCONV + k + 1], ALU.mult, ALU.add).then_inc(s["conv_mac"], 1)
                    wait(eng, "conv_mac", i, 3 * k + 1)
                    STT(dst, src[:, 0:N], w[0], dst, ALU.mult, ALU.add).then_inc(s["conv_mac"], 1)
                    wait(eng, "conv_mac", i, 3 * k + 2)
                    STT(dst, src[:, 2:N + 2], w[2], dst, ALU.mult, ALU.add).then_inc(s["conv_mac"], 1)
                wait(eng, "dbc_mm", i, 1)
                dbc = rows4[:, :, :, DH:ROW]
                for h in range(HEADS):
                    ins = TT(rows4[:, h, :, DH:ROW], ps[0][:, 0:NT * HEADS * J].rearrange("p (t h j) -> p h t j", t=NT, h=HEADS)[:, h],
                             bdbc_sb[:, h * J:(h + 1) * J].unsqueeze(1).broadcast_to([P, NT, J]), ALU.add)
                    ins.then_inc(s["sp_z"], 1)
                wait(eng, "sp_z", i, 2)
                z = rows4[:, :, :, DH]
                v = lambda a: sm[:, a, :].rearrange("p (h t) -> p h t", h=HEADS)
                STT(v(3), z, -1.0, z, ALU.mult, ALU.max).then_inc(s["sp_dve"], 1)
                wait(eng, "sp_act", i, 1)
                TS(v(5), v(4), 1.0, None, ALU.add).then_inc(s["sp_dve"], 1)
                wait(eng, "sp_dve", i, 2)
                TS(v(7), v(5), -1.0, None, ALU.add).then_inc(s["sp_dve"], 1)
                wait(eng, "sp_dve", i, 3)
                TS(v(3), v(7), 0.0, None, ALU.is_equal).then_inc(s["sp_dve"], 1)
                wait(eng, "sp_dve", i, 4)
                wait(eng, "sp_act", i, 2)
                TT(v(7), v(7), v(3), ALU.add).then_inc(s["sp_dve"], 1)
                TT(v(6), v(6), v(3), ALU.add).then_inc(s["sp_dve"], 1)
                wait(eng, "sp_dve", i, 6)
                eng.reciprocal(v(5), v(7)).then_inc(s["sp_dve"], 1)
                TT(v(6), v(6), v(4), ALU.mult).then_inc(s["sp_dve"], 1)
                wait(eng, "sp_dve", i, 8)
                TT(v(6), v(6), v(5), ALU.mult).then_inc(s["sp_dve"], 1)
                wait(eng, "sp_dve", i, 9)
                STT(z, z, 0.0, v(6), ALU.max, ALU.add).then_inc(s["sp_dve"], 1)
                wait(eng, "sp_dve", i, 10)
                for h in range(HEADS):
                    ins = TT(rows4[:, h, :, DH + 1:DH + 1 + S], rows4[:, h, :, DH + 1:DH + 1 + S],
                             rows4[:, h, :, DH].unsqueeze(2).broadcast_to([P, NT, S]), ALU.mult)
                ins.then_inc(s["row_ready"], 1)
                for h in range(HEADS):
                    scan_vec(i, h)
                for k in range(KC):
                    wait(eng, "yt_mm", i, k + 1)
                    wait(eng, "silu2", i, 8)
                    for half in range(2):
                        c = slice(half * HALF, (half + 1) * HALF)
                        ins = TT(gate[:, k, c], ps[yt_banks[k][half]][:, :], gate[:, k, c], ALU.mult)
                    ins.then_inc(s["y_gate"], 1)
                group_norm(i, 2, x)
                group_norm(i, 3, x)
                if not last:
                    group_norm(i + 1, 0, x_next)

            def scan_vec(i, h):
                r = rows4[:, h]
                dt, wgt, cst_c = r[:, :, DH], r[:, :, DH + 1:DH + 1 + S], r[:, :, DH + 1 + S:ROW]
                wait(eng, f"scanrows{h}", i, 16)
                wait(eng, "fac_mm", i, 2 * h)
                dtg = dt.unsqueeze(2).broadcast_to([P, NT, G])
                left = const("left").rearrange("p (h g) -> p h g", h=HEADS)[:, h]
                right = const("right").rearrange("p (h g) -> p h g", h=HEADS)[:, h]
                TT(mv[:, 0], dtg, left.unsqueeze(1).broadcast_to([P, NT, G]), ALU.mult).then_inc(s["fac_mv"], 1)
                TT(mv[:, 1], dtg, right.unsqueeze(1).broadcast_to([P, NT, G]), ALU.mult).then_inc(s["fac_mv"], 1)
                TT(mv8[:, :, :], dt.unsqueeze(2).broadcast_to([P, NT, T8]),
                   const("within8").unsqueeze(1).broadcast_to([P, NT, T8]), ALU.mult).then_inc(s["fac_mv"], 1)
                TT(mvc[:, :, :, :], cst_c.unsqueeze(2).broadcast_to([P, NT, T8, S]),
                   const("eq8").unsqueeze(1).unsqueeze(3).broadcast_to([P, NT, T8, S]), ALU.mult).then_inc(s["fac_mv"], 1)
                a = amat[:, h, :].unsqueeze(1)
                wait(eng, "fac_mm", i, 2 * h + 2)
                wait(eng, "fac_gam", i, h + 1)
                wait(eng, "y_mm", i, 4 * h)
                for n, (dst, lo, cols) in enumerate(((pfac, 0, P), (qfac, P, P), (arg8[:, :, :].rearrange("p a s -> p (a s)"), 2 * P, 64))):
                    TT(dst.rearrange("p (c s) -> p c s", s=S), ps[7][:, lo:lo + cols].unsqueeze(2).broadcast_to([P, cols, S]),
                       a.broadcast_to([P, cols, S]), ALU.mult).then_inc(s["fac_arg"], 1)
                p4 = pfac.rearrange("p (c g s) -> p c g s", c=NT, g=G)
                q4 = qfac.rearrange("p (c g s) -> p c g s", c=NT, g=G)
                wait(eng, "fac_exp", i, 3 * h + 1)
                TT(p4, p4, wgt.unsqueeze(2).broadcast_to([P, NT, G, S]), ALU.mult).then_inc(s["fac_pq"], 1)
                wait(eng, "fac_exp", i, 3 * h + 2)
                TT(q4, q4, cst_c.unsqueeze(2).broadcast_to([P, NT, G, S]), ALU.mult).then_inc(s["fac_pq"], 1)
                wait(eng, "fac_exp", i, 3 * h + 3)
                a8 = arg8[:, :, :].rearrange("p (c t) s -> p c t s", c=NT)
                TT(arg8[:, :, :], ps[0][:, :].rearrange("p (a s) -> p a s", s=S), arg8[:, :, :], ALU.mult).then_inc(s["fac_8"], 1)
                wait(eng, "fac_8", i, 5 * h + 1)
                TT(a8, a8, wgt.unsqueeze(2).broadcast_to([P, NT, T8, S]), ALU.mult).then_inc(s["fac_8"], 1)
                wait(eng, "fac_8", i, 5 * h + 2)
                wait(eng, "fac_diag", i, h)
                eng.tensor_reduce(md8[:, :], arg8[:, :, :], AX.X, ALU.add).then_inc(s["fac_8"], 1)
                wait(eng, "fac_8", i, 5 * h + 3)
                m8 = md8[:, :].rearrange("p (c t) -> p c t", c=NT)
                TT(m8, m8, const("within8").unsqueeze(1).broadcast_to([P, NT, T8]), ALU.mult).then_inc(s["fac_8"], 1)
                wait(eng, "fac_8", i, 5 * h + 4)
                TT(m8, m8, deq8[:, h, :].unsqueeze(1).broadcast_to([P, NT, T8]), ALU.add).then_inc(s["fac_8"], 1)
                hp = slice(32 * h, 32 * h + 8)
                for c in range(NT - 1):
                    wait(eng, "dh_mm", i, 4 * h + c // 2 + 1)
                    inc = ps[dh_bank(c)][hp, (c % 2) * DH:(c % 2 + 1) * DH]
                    if c == 0:
                        eng.tensor_copy(hst[hp, 0, :], inc).then_inc(s["h_st"], 1)
                    else:
                        wait(eng, "h_st", i, 7 * h + c)
                        STT(hst[hp, c, :], hst[hp, c - 1, :], gam[hp, c:c + 1], inc, ALU.mult, ALU.add).then_inc(s["h_st"], 1)
                wait(eng, "fac_diag", i, h + 1)
                for half in range(2):
                    wait(eng, "mm_m", i, 2 * h + half + 1)
                    c = slice(half * HALF, (half + 1) * HALF)
                    TT(mmat[:, c], ps[3 + half][:, :], diag[:, c], ALU.add).then_inc(s["m_ev"], 1)

            with eng.Fori(0, B - 1) as i:
                image(i, False)
            image(B - 1, True)

        @block.tensor
        def _(eng):
            def mm(out, lhsT, rhs, start, stop, **kw):
                return eng.matmul(out, lhsT, rhs, start=start, stop=stop, skip_group_check=True, **kw)

            eng.wait_ge(s["cst_in"], 16)
            eng.wait_ge(s["w_max"], 1 + 2 * (len(wchunks) + 1))
            eng.transpose(ps[7][0:4, 0:P], par[:, WMAX:WMAX + 4], ident).then_inc(s["w_maxt"], 1)
            eng.wait_ge(s["w_maxr"], 2)
            mm(ps[7][:, 0:4], const("ones")[0:4, :], par[0:4, WMAX:WMAX + 4], True, True).then_inc(s["w_maxb"], 1)
            eng.wait_ge(s["p_rank"], 1)
            eng.wait_ge(s["w_done"], len(wchunks) * 2 + 2)

            def gn_sum(i, g, k):
                wait(eng, "gn_stat", i, 4 * g + k + 1)
                if g or k:
                    wait(eng, "gn_got", i, 4 * g + k)
                mm(gn_ps, const("group_mean"), st[:, k, 0:2], True, True).then_inc(s["gn_sum"], 1)

            def passes(wname, his, los, o, half, k, bank, start, stop):
                c = slice(half * HALF, (half + 1) * HALF)
                oc = slice(o * P, (o + 1) * P)
                a = ((w_hi[wname], his), (w_hi[wname], los), (w_lo[wname], his))
                for n, (w, v) in enumerate(a):
                    ins = mm(ps[bank][:, :], w[:, k, oc], v[:, k, c], start and n == 0, stop and n == 2)
                return ins

            def free_bank(i, n):
                wait(eng, "gemm_evac", i, bank_free[n])
                if bank_of[n] >= 3 and 35 <= n <= 36:
                    wait(eng, "y_gate", i, 2)
                if bank_of[n] >= 3 and 37 <= n <= 38:
                    wait(eng, "y_gate", i, KC)

            def behind(i, g, base, ready, part, first=3):
                for k in range(KC):
                    if g is not None and k < 2:
                        gn_sum(i, g, k + 2)
                    ready(k)
                    for u in range(first):
                        if k == 0:
                            free_bank(i, base + u)
                        ins = part(u, k)
                        if k == KC - 1:
                            ins.then_inc(s["gemm_done"], 1)

            for k in range(KC):
                gn_sum(0, 0, k)

            def image(i, last):
                wait(eng, "gn_split", i, 2 * KC)
                for t in range(NT):
                    a, z = (64 if t == 0 else 0), (WIN - 64 if t == NT - 1 else WIN)
                    tok, win = slice(t * P, (t + 1) * P), slice(t * P - 64 + a, t * P - 64 + z)
                    for k in range(KC):
                        for n, (l, r) in enumerate(((even_hi, even_hi), (even_hi, even_lo), (even_lo, even_hi))):
                            ins = mm(gram_ps(t)[:, a:z], l[:, k, tok], r[:, k, win], k == 0 and n == 0, k == KC - 1 and n == 2)
                    ins.then_inc(s["gram_mm"], 1)
                def main(u):
                    half, o = divmod(u, KC)
                    for k in range(KC):
                        passes("L0", even_hi, even_lo, o, half, k, bank_of[u], k == 0, False)

                def corr_part(u):
                    half, o = divmod(u, KC)
                    mm(ps[bank_of[u]][:, :], w_corr[0:96, o * P:(o + 1) * P], corr[0:96, half * HALF:(half + 1) * HALF],
                       False, True).then_inc(s["gemm_done"], 1)

                main(0)
                main(1)
                wait(eng, "gram_rd", i, 1)
                for half in range(2):
                    wait(eng, "gram_row", i, half)
                    mm(ps[7][:, :], const("ones"), rdiag[:, 4 * half:4 * half + 4, :].rearrange("p t k -> p (t k)"),
                       True, True).then_inc(s["gram_rb"], 1)
                main(2)
                wait(eng, "gram_ev", i, NT)
                for u in (3, 4, 5, 6):
                    main(u)
                wait(eng, "corr_msk", i, 1)
                wait(eng, "gram_pad", i, 5)
                wait(eng, "gram_row", i, 2)
                for half in range(2):
                    wait(eng, "corr_lo", i, half)
                    for t in range(4):
                        ins = eng.transpose(ps[7][0:96, t * P:(t + 1) * P],
                                            corr3[:, 4 * half + t].rearrange("p a k -> p (a k)"), ident)
                    ins.then_inc(s["corr_t"], 1)
                for u in (0, 1, 2, 3):
                    corr_part(u)
                wait(eng, "corr_lo", i, 2)
                for u in (4, 5, 6):
                    corr_part(u)
                free_bank(i, 7)
                main(7)
                gn_sum(i, 1, 0)
                corr_part(7)
                gn_sum(i, 1, 1)
                def in_part(q, k):
                    o3, half = divmod(q, 2)
                    part, o = divmod(o3, KC)
                    col = (0, 2, 1)[part] * KC + o
                    return passes("in", odd_hi, odd_lo, col, half, k, bank_of[8 + q], k == 0, k == KC - 1)

                def in_unit(q):
                    free_bank(i, 8 + q)
                    for k in range(KC):
                        ins = in_part(q, k)
                    ins.then_inc(s["gemm_done"], 1)

                behind(i, 1, 8, lambda k: wait(eng, "gn_split", i, 2 * (4 + k) + 2), in_part)
                for q in range(3, 8):
                    in_unit(q)
                fill = iter(range(8, 24))

                def filler(n):
                    for _ in range(n):
                        in_unit(next(fill))

                def tokens(k):
                    wait(eng, "conv_act", i, k + 1)
                    if k == 0:
                        wait(eng, "gemm_evac", i, 16)
                    if k >= 2:
                        wait(eng, "tok_ev", i, k - 1)
                    for t in range(NT):
                        lhsT = conv_out[:, k % 2, t * P:(t + 1) * P]
                        ins = mm(ps[0][:, t * HEADS * J:(t + 1) * HEADS * J], lhsT, w_dbc[:, k, :],
                                 k == 0 and t == 0, k == KC - 1)
                        if k == KC - 1 and t == NT - 1:
                            ins.then_inc(s["dbc_mm"], 1)
                    for t in range(NT):
                        ins = eng.transpose(ps[tok_banks[k % 2][t // 4]][:, (t % 4) * P:(t % 4 + 1) * P],
                                            conv_out[:, k % 2, t * P:(t + 1) * P], ident)
                    ins.then_inc(s["tok_mm"], 1)

                for k in range(KC):
                    tokens(k)
                    filler(1)
                filler(6)
                for h in range(HEADS):
                    wait(eng, "fac_mv", i, 4 * h + 4)
                    r = rows4[:, h]
                    offl = const("off_left").rearrange("p (h g) -> p h g", h=HEADS)[:, h].unsqueeze(1).broadcast_to([P, NT, G])
                    offr = const("off_right").rearrange("p (h g) -> p h g", h=HEADS)[:, h].unsqueeze(1).broadcast_to([P, NT, G])
                    b7 = ps[7]
                    v3 = lambda t: t.rearrange("p (c g) -> p c g", c=NT)
                    mm(v3(b7[:, 0:P]), after, mv[:, 0], True, False)
                    mm(v3(b7[:, 0:P]), ident, offl, False, True)
                    mm(v3(b7[:, P:2 * P]), upto, mv[:, 1], True, False)
                    mm(v3(b7[:, P:2 * P]), ident, offr, False, True)
                    mm(b7[:, 2 * P:2 * P + 64].rearrange("p (c t) -> p c t", c=NT), after8, mv8[:, :, :], True, True)
                    mm(b7[0:40, 320:328], const("ones")[:, 0:40], r[:, :, DH], True, True).then_inc(s["fac_mm"], 1)
                    if h == 0:
                        wait(eng, "sp_z", i, 2)
                    else:
                        wait(eng, "fac_8", i, 1)
                    mm(ps[0][:, :].rearrange("p (c t s) -> p c t s", c=NT, t=T8).rearrange("p c t s -> p (c t s)"), same8,
                       mvc[:, :, :, :].rearrange("p c t s -> p (c t s)"), True, True).then_inc(s["fac_mm"], 1)
                    filler(2 - h)
                    if h == 0:
                        wait(eng, "tok_ev", i, KC)
                    else:
                        wait(eng, "y_ev", i, 4)
                        wait(eng, "h_st", i, 7)
                    for a, f in enumerate((pfac, qfac)):
                        wait(eng, "fac_pq", i, 2 * h + a + 1)
                        for c in range(NT):
                            ins = eng.transpose(ps[3 + 2 * a + c // 4][:, (c % 4) * P:(c % 4 + 1) * P],
                                                f[:, c * P:(c + 1) * P], ident)
                            if c % 4 == 3:
                                ins.then_inc(s["fac_tp"], 1)
                    for half in range(2):
                        wait(eng, "fac_ptq", i, 4 * h + (3 if half == 0 else 4))
                        for c in range(4 * half, 4 * half + 4):
                            ins = mm(ps[3 + half][:, (c % 4) * P:(c % 4 + 1) * P], pT[:, c * P:(c + 1) * P],
                                     qT[:, c * P:(c + 1) * P], True, True)
                        ins.then_inc(s["mm_m"], 1)
                    far = FAR_GROUP[h] * S
                    for c in range(NT - 1):
                        if c >= 4 and c % 2 == 0:
                            wait(eng, "h_st", i, 7 * h + c - 2)
                        ins = mm(ps[dh_bank(c)][32 * h:32 * h + 8, (c % 2) * DH:(c % 2 + 1) * DH],
                                 pfac[:, c * P + far:c * P + far + S], r[:, c, 0:DH], True, True)
                        if c % 2 == 1 or c == NT - 2:
                            ins.then_inc(s["dh_mm"], 1)
                    filler(1 + h)
                    for c in range(NT):
                        j = c // 2
                        wait(eng, "m_ev", i, 2 * h + 2)
                        if j >= 2:
                            wait(eng, "y_ev", i, 4 * h + j - 1)
                        out = ps[3 + j % 2][:, (c % 2) * DH:(c % 2 + 1) * DH]
                        ins = mm(out, mmat[:, c * P:(c + 1) * P], r[:, c, 0:DH], True, c == 0)
                        if c > 0:
                            wait(eng, "h_st", i, 7 * h + c)
                            ins = mm(out, qT[far:far + S, c * P:(c + 1) * P], hst[far:far + S, c - 1, :], False, True)
                        if c % 2 == 1:
                            ins.then_inc(s["y_mm"], 1)
                def y_chunk(k):
                    if k == 0:
                        wait(eng, "y_ev", i, 4 * HEADS)
                        wait(eng, "h_st", i, 7 * HEADS)
                    if k % 2 == 0:
                        wait(eng, f"y_in{k // 2}", i, 16 * NT)
                    if k >= 2:
                        wait(eng, "y_gate", i, (1, 3)[k - 2])
                    for t in range(NT):
                        ins = eng.transpose(ps[yt_banks[k][t // 4]][:, (t % 4) * P:(t % 4 + 1) * P],
                                            ytok[k // 2][:, t, (k % 2) * P:(k % 2 + 1) * P], ident)
                    ins.then_inc(s["yt_mm"], 1)

                def out_part(u, k):
                    half, o = divmod(u, KC)
                    return mm(ps[bank_of[32 + u]][:, :], w_out[:, k, o * P:(o + 1) * P],
                              gate[:, k, half * HALF:(half + 1) * HALF], k == 0, k == KC - 1)

                def split_part(stg, u, k):
                    half, o = divmod(u, KC)
                    his, los = ((even_hi, even_lo), (odd_hi, odd_lo))[stg % 2]
                    return passes("L%d" % stg, his, los, o, half, k, bank_of[24 + 8 * stg + u], k == 0, k == KC - 1)

                def stage_gemm(stg, base, ready, part, first=3):
                    behind(i, stg if stg > 1 else None, base, ready, part, first)
                    for u in range(first, 8):
                        free_bank(i, base + u)
                        for k in range(KC):
                            ins = part(u, k)
                        ins.then_inc(s["gemm_done"], 1)
                        if stg < 3 and u >= 6:
                            gn_sum(i, stg + 1, u - 6)
                        if stg == 3 and u < 7 and not last:
                            gn_sum(i + 1, 0, u - 3)

                def y_ready(k):
                    if k in (0, 2):
                        y_chunk(k)
                        y_chunk(k + 1)
                    wait(eng, "y_res", i, k + 1)

                stage_gemm(1, 32, y_ready, out_part, 5)
                stage_gemm(2, 40, lambda k: wait(eng, "gn_split", i, 2 * (8 + k) + 2), lambda u, k: split_part(2, u, k))
                stage_gemm(3, 48, lambda k: wait(eng, "gn_split", i, 2 * (12 + k) + 2), lambda u, k: split_part(3, u, k))
                if not last:
                    wait(eng, "gemm_evac", i, 56)

            with eng.Fori(0, B - 1) as i:
                image(i, False)
            image(B - 1, True)
    return nc


def kernel(**inputs):
    import concourse.bacc as bacc
    from concourse.bass_utils import run_bass_kernel_spmd as run

    g = {k: np.asarray(v) for k, v in inputs.items()}
    _, packed, before, grid = constants()
    cols = lambda b: b.reshape(-1, P).T
    conv_w = g["L0_conv_conv_w"]
    alog = g["L1_conv_A_log"]
    arrays = {
        "x": g["x"].reshape(B, C, N),
        "w0t": conv_w[:, :C].T,
        "wct": conv_w[:, C:].reshape(C, 5, 5).transpose(2, 1, 0).reshape(TAPS, C),
        "wint": g["L1_conv_in_proj_w"].T,
        "woutt": g["L1_conv_out_proj_w"].T,
        "wdbct": g["L1_conv_dbc_w"].T,
        "w2t": g["L2_conv_weight"].T,
        "w3t": g["L3_conv_weight"].T,
        "b0": cols(g["L0_conv_conv_b"]), "bin": cols(g["L1_conv_in_proj_b"]), "bconv": cols(g["L1_conv_dw_b"]),
        "bout": cols(g["L1_conv_out_proj_b"]), "bl2": cols(g["L2_conv_bias"]), "bl3": cols(g["L3_conv_bias"]),
        "bdbc": g["L1_conv_dbc_b"].reshape(1, HEADS * J),
        "taps": g["L1_conv_dw_w"].reshape(KC, P, 3).transpose(1, 0, 2).reshape(P, 3 * KC),
        "alog": alog.reshape(1, HEADS * S), "alog_col": alog.reshape(HEADS, S, 1),
        "dpar": g["L1_conv_Dparam"].reshape(1, HEADS), "mob": g["L1_conv_mobius"].reshape(1, 4 * HEADS),
        "cst": packed, "before": before, "grid": grid,
    }
    nc = bacc.Bacc("TRN2", target_bir_lowering=False, num_devices=1)
    feed, d = {}, {}
    for name, a in arrays.items():
        feed["in_" + name] = a = np.ascontiguousarray(a)
        d[name] = nc.dram_tensor("in_" + name, a.shape, mybir.dt.from_np(a.dtype), kind="ExternalInput").ap()
    d["out"] = nc.dram_tensor("out_x", (B, C, N), F32, kind="ExternalOutput").ap()
    build(nc, d)
    r = run(nc, [feed], core_ids=[0])
    return r.results[0]["out_x"].reshape(B, C, H, W)
```

```python
from contextlib import ExitStack

import numpy as np

import concourse.bass as bass
from concourse import mybir

F32, F16, I32 = mybir.dt.float32, mybir.dt.float16, mybir.dt.int32
ALU, ACT, AX = mybir.AluOpType, mybir.ActivationFunctionType, mybir.AxisListType

P = 128
B, C, H, W = 8, 512, 32, 32
N = H * W
KC = C // P
HALF = 512
NT = N // P
S, HEADS = 8, 2
DH = C // HEADS
J = 1 + 2 * S
ROW = DH + J
G = 16
T8 = 8
TAPS = 25
ROWS_T = P // W
WIN = 2 * P
PITCH = WIN + 4
EPS = 1e-5
REACH = 2 * W + 2
BIG = 1e20
FAR_GROUP = (0, 4)


def constants():
    v = np.arange(P)
    parts = {}
    parts["ident"] = np.eye(P)
    parts["upto"] = v[:, None] <= v[None, :]
    parts["after"] = v[:, None] > v[None, :]
    same8 = (v[:, None] // T8) == (v[None, :] // T8)
    parts["same8"] = same8
    parts["after8"] = same8 & (v[:, None] > v[None, :])
    parts["group_mean"] = ((v[:, None] // 16) == (v[None, :] // 16)) / 16.0
    parts["ones"] = np.ones((P, P))
    blocks = [(s, size) for size in (128, 64, 32, 16) for s in range(0, P, size)]
    left, right = np.zeros((P, HEADS, G)), np.zeros((P, HEADS, G))
    keep = np.ones((P, HEADS))
    for h in range(HEADS):
        groups = [g for g in range(G) if g != FAR_GROUP[h]]
        for g, (s, size) in zip(groups, blocks):
            left[s:s + size // 2, h, g] = 1
            right[s + size // 2:s + size, h, g] = 1
        left[:, h, FAR_GROUP[h]] = right[:, h, FAR_GROUP[h]] = 1
        keep[FAR_GROUP[h] * S:(FAR_GROUP[h] + 1) * S, h] = 0
    parts["left"], parts["right"] = left, right
    parts["off_left"], parts["off_right"] = BIG * (1 - left), BIG * (1 - right)
    parts["keep"] = keep
    parts["within8"] = (v[:, None] % T8) <= np.arange(T8)[None, :]
    parts["eq8"] = (v[:, None] % T8) == np.arange(T8)[None, :]
    parts["block16"] = (v[:, None] // T8) == np.arange(P // T8)[None, :]
    n = np.arange(N).reshape(NT, P).T
    y, x = n // W, n % W
    inside = np.zeros((P, NT, 5, 5))
    for r in range(5):
        for c in range(5):
            inside[:, :, r, c] = ((y + r - 2 >= 0) & (y + r - 2 < H) & (x + c - 2 >= 0) & (x + c - 2 < W))
    parts["inside"] = inside
    step = np.arange(W - 1, dtype=np.float32) / np.float32(W - 1)
    line = np.concatenate([np.float32(-1) * (np.float32(1) - step) + step, [np.float32(1)]]).astype(np.float32)
    parts["grid"] = np.concatenate([line[x], line[y]], axis=1)
    at, cols = {}, []
    pos = 0
    for name, a in parts.items():
        a = np.asarray(a, np.float32).reshape(P, -1)
        at[name] = (pos, a.shape[1])
        pos += a.shape[1]
        cols.append(a)
    return at, np.concatenate(cols, axis=1)


def build(nc, d):
    at, packed = constants()
    with ExitStack() as ctx:
        def sb(name, shape, dt=F32):
            return ctx.enter_context(nc.sbuf_tensor(name, shape, dt))

        def sem(name):
            return ctx.enter_context(nc.semaphore(name))

        w_hi = {"L0": sb("w0_hi", [P, KC, C], F16), "in": sb("win_hi", [P, KC, 3 * C], F16),
                "L2": sb("w2_hi", [P, KC, C], F16), "L3": sb("w3_hi", [P, KC, C], F16)}
        w_lo = {"L0": sb("w0_lo", [P, KC, C], F16), "in": sb("win_lo", [P, KC, 3 * C], F16),
                "L2": sb("w2_lo", [P, KC, C], F16), "L3": sb("w3_lo", [P, KC, C], F16)}
        w_corr = sb("w_corr", [P, C], F16)
        w_out = sb("w_out", [P, KC, C])
        w_dbc = sb("w_dbc", [P, KC, HEADS * J])
        cst = sb("cst", [P, packed.shape[1]])

        def const(name):
            o, n = at[name]
            return cst[:, o:o + n]

        ident, upto, after, same8, after8 = map(const, ("ident", "upto", "after", "same8", "after8"))
        x = sb("x", [P, KC, N])
        x_next = sb("x_next", [P, KC, N])
        even = sb("even", [P, KC * N + 16])
        odd = sb("odd", [P, KC * N])
        gate = sb("gate", [P, KC, N])
        res = sb("res", [P, KC, N])
        rows = sb("rows", [P, HEADS * NT * ROW])
        work = sb("work", [P, 2 * N])
        work2 = sb("work2", [P, 7 * DH])
        arg8 = sb("arg8", [P, NT * T8, S])
        mvc = sb("mvc", [P, NT, T8, S])
        mv = sb("mv", [P, 2, NT, G])
        mv8 = sb("mv8", [P, NT, T8])
        md8 = sb("md8", [P, NT * T8])[:, :]
        gam = sb("gam", [P, NT])
        sm = sb("sm", [P, 8, 16])
        bn = sb("bn", [P, KC, 2, 6])
        st = sb("st", [P, KC, 6])
        bn_next = sb("bn_next", [P, KC, 2, 6])
        st_next = sb("st_next", [P, KC, 6])
        minus_half = sb("minus_half", [P, 1])[:, :]
        par = sb("par", [P, 64])
        corr = sb("corr", [P, 2 * HALF], F16)
        rank = sb("rank", [P, HEADS, NT], I32)
        deq8 = sb("deq8", [P, HEADS, T8])
        amat = sb("amat", [P, HEADS, S])
        square = sb("square", [P, 2, NT])
        norm_row = sb("norm_row", [NT, P])[:, :]
        zero_pad = sb("zero_pad", [2, REACH])[:, :]

        def pair(t):
            v = t[:, 0:KC * N].bitcast(F16).rearrange("p (a k n) -> p a k n", a=2, k=KC)
            return v[:, 0], v[:, 1]

        even_hi, even_lo = pair(even)
        odd_hi, odd_lo = pair(odd)
        conv_in = even[:, 0:KC * (N + 2)].rearrange("p (b n) -> p b n", b=KC)
        conv_out = res[:, 2:4, :]
        yscan = even[:, 0:KC * N].rearrange("p (h c d) -> p h c d", h=HEADS, c=NT)
        rows4 = rows[:, :].rearrange("p (h t r) -> p h t r", h=HEADS, t=NT)
        ytok = [rows[:, h * NT * ROW:h * NT * ROW + NT * DH].rearrange("p (t d) -> p t d", t=NT)
                for h in range(HEADS)]
        gram = rows[:, 0:NT * PITCH].rearrange("p (t w) -> p t w", t=NT)
        near = rows[:, NT * PITCH:NT * (PITCH + 2 * REACH + 1)].rearrange("p (t j) -> p t j", t=NT)
        near_shifts = bass.AP(near.tensor, near.offset, [list(near.ap[0]), [2 * REACH + 1, NT], [W, 5], [1, 5]])
        factors = rows[:, NT * (PITCH + 2 * REACH + 1):NT * (PITCH + 2 * REACH + 1) + 2 * NT * TAPS] \
            .rearrange("p (a t k) -> p a t k", a=2, t=NT)
        corr_tok = work2[:, 3 * HALF:3 * HALF + NT * TAPS].rearrange("p (t k) -> p t k", t=NT)
        corr3 = work[:, N:N + NT * 96].rearrange("p (t a k) -> p t a k", t=NT, a=3)
        xn = x_next[:, :, :].rearrange("p k n -> p (k n)")
        pfac, qfac, pT, qT = (xn[:, a * N:(a + 1) * N] for a in range(4))
        mmat = work[:, 0:N]
        diag = work[:, N:2 * N]
        normed = work[:, :].rearrange("p (b n) -> p b n", b=4)
        tmp = work2[:, 0:3 * HALF].rearrange("p (b n) -> p b n", b=3)
        hst = work2[:, :].rearrange("p (c d) -> p c d", c=7)

        bdbc_sb = sb("bdbc_sb", [P, HEADS * J])
        ps = [ctx.enter_context(nc.psum_tensor(f"bank{i}", [P, HALF], F32)) for i in range(8)]

        gn_ps = ps[7][:, 0:2]
        first_ps = ps[7][:, 0:2 * KC]
        gram_ps = lambda t: ps[2 + t // 2][:, (t % 2) * WIN:(t % 2 + 1) * WIN]
        tok_banks = ((4, 5), (6, 3))
        yt_banks = ((3, 4), (5, 6), (3, 4), (3, 4))
        dh_bank = lambda c: 5 + (c // 2) % 2
        bank_of = ([6, 0, 1, 2, 3, 4, 5, 6] + [0, 1, 2, 3, 4, 5, 6, 0] + [1, 2] * 7 + [1, 3]
                   + [0, 1, 2, 7, 5, 6, 3, 4] + [0, 1, 2, 3, 4, 5, 6, 0] + [1, 2, 3, 4, 5, 6, 0, 1])
        bank_free = [max([p + 1 for p in range(n) if bank_of[p] == bank_of[n]], default=0) for n in range(56)]

        d_gram = nc.dram_tensor("d_gram", (NT, P, PITCH), F32, kind="Internal").ap()
        d_norm = nc.dram_tensor("d_norm", (1, N + 2 * REACH), F32, kind="Internal").ap()
        d_scan = [nc.dram_tensor(f"d_scan{h}", (N, ROW), F32, kind="Internal").ap() for h in range(HEADS)]
        d_score = nc.dram_tensor("d_score", (P, HEADS * NT), F32, kind="Internal").ap()
        d_y = [nc.dram_tensor(f"d_y{h}", (N, DH), F32, kind="Internal").ap() for h in range(HEADS)]

        B0, BIN, BCONV, BOUT, BL2, BL3, TAP, WMAX, SCL, INV = 0, 4, 16, 20, 24, 28, 32, 44, 48, 52
        WI = {"L0": 0, "in": 1, "L2": 2, "L3": 3}

        names = """w_in_L0 w_in_in w_in_L2 w_in_L3 w_hi_L0 w_hi_in w_hi_L2 w_hi_L3 w_lo_L0 w_lo_in w_lo_rest
            w_sc_in w_max w_maxc w_maxt w_maxr w_maxb w_scl w_corrz mob_in par_in cst_in score_out score_in
            p_abcd p_sqrt p_count p_zero a_neg p_score p_rank a_in a_exp
            x_in x_out gn_raw first_raw first_stat first_sum first_step first_rstd first_bias gn_stat gn_sum gn_got gn_var gn_neg gn_rstd gn_bias gn_hi gn_norm gn_split
            pad_zero pad_out gram_mm gram_d norm_t norm_max norm_pow norm_row norm_out norm_in norm_m gram_ev gram_pad gram_out0 gram_out1 gram_out2 gram_out3 gram_in corr_msk corr_t corr_cp corr_lo
            gemm_done gemm_evac res_pool res_dve
            conv_pad conv_mac conv_act tok_mm tok_ev dbc_mm sp_z sp_dve sp_act row_ready scattered0 scattered1 scanrows0 scanrows1
            fac_mv fac_mm fac_arg fac_exp fac_gam fac_pq fac_8 fac_diag fac_tp fac_ptq mm_m m_ev dh_mm h_st y_mm y_ev y_out0 y_out1 y_in0 y_in1
            yt_mm y_gate y_res silu2 half_in""".split()
        s = {n: sem(n) for n in names}
        per = dict(x_in=16 * KC, x_out=16 * KC, gn_raw=36, first_raw=12, first_stat=4, first_sum=1, first_step=4, first_rstd=1, first_bias=1,
                   gn_stat=12, gn_sum=12, gn_got=12, gn_var=12, gn_neg=12, gn_rstd=12,
                   gn_bias=12, gn_hi=32, gn_norm=32, gn_split=32,
                   gram_mm=NT, gram_d=NT, norm_t=1, norm_max=2, norm_pow=2, norm_row=1, norm_out=16, norm_in=16, norm_m=2, gram_ev=NT,
                   gram_pad=5, gram_out0=16, gram_out1=16, gram_out2=16, gram_out3=16, gram_in=16 * NT, corr_msk=1, corr_t=2, corr_cp=2, corr_lo=2,
                   gemm_done=56, gemm_evac=56, res_pool=16, res_dve=16,
                   conv_pad=1, conv_mac=3 * KC, conv_act=KC, tok_mm=KC, tok_ev=KC, dbc_mm=1, sp_z=2,
                   sp_dve=10, sp_act=2, row_ready=1, scattered0=16 * NT, scattered1=16 * NT, scanrows0=16, scanrows1=16,
                   fac_mv=8, fac_mm=2 * HEADS, fac_arg=3 * HEADS, fac_exp=3 * HEADS, fac_gam=HEADS, fac_pq=2 * HEADS,
                   fac_8=5 * HEADS, fac_diag=HEADS, fac_tp=4 * HEADS, fac_ptq=4 * HEADS, mm_m=2 * HEADS,
                   m_ev=2 * HEADS, dh_mm=4 * HEADS, h_st=7 * HEADS, y_mm=4 * HEADS, y_ev=4 * HEADS,
                   y_out0=16, y_out1=16, y_in0=16 * NT, y_in1=16 * NT, yt_mm=KC, y_gate=2 * KC, y_res=2 * KC, silu2=8)

        CMP_STEPS = 3 * NT + 2 * NT - 2 + 1
        SCORES = 5 + 2 * 14
        primed = {"x_out": 16}

        def wait(eng, name, i, n):
            if n or name in primed:
                eng.wait_ge(s[name], i * per[name] + n + primed.get(name, 0))

        def added(u):
            mine = [v for v in range(u + 1) if pool_adds(v) == pool_adds(u)]
            return ("res_pool" if pool_adds(u) else "res_dve"), len(mine)

        def pool_adds(u):
            stg, v = divmod(u, 8)
            return v in ((0, 2), (0, 2), range(4), range(8))[stg]

        def add(eng, i, u, src, base):
            half, o = divmod(u % 8, KC)
            if u in (0, 1):
                wait(eng, "x_out", i, 0)
            wait(eng, "gemm_evac", i, base + u % 8 + 1)
            c = slice(half * HALF, (half + 1) * HALF)
            eng.tensor_tensor(x[:, o, c], src[:, o, c], tmp[:, u % 3, :], ALU.add).then_inc(s[added(u)[0]], 1)

        def split_n(g, n):
            return 8 * g + n + 1

        def in_unit_at(q):
            part, u = divmod(q, 8)
            return (part,) + divmod(u, KC)

        block = ctx.enter_context(nc.Block())

        wsrc = {"L0": (d["w0t"], C), "in": (d["wint"], 3 * C), "L2": (d["w2t"], C), "L3": (d["w3t"], C)}
        flat = lambda t: t[:, :, :].rearrange("p k n -> p (k n)")
        stage = {"L0": flat(x)[:, 0:KC * C], "L2": flat(res)[:, KC * C:2 * KC * C], "L3": odd[:, 0:KC * C]}
        in_stage = [flat(gate)[:, 0:3 * C], flat(gate)[:, 3 * C:6 * C], flat(res)[:, 0:3 * C], flat(x)[:, 5 * C:8 * C]]
        wchunks = {}
        for name in ("L0", "L2", "L3"):
            wchunks[name] = [(k, stage[name][:, k * C:(k + 1) * C]) for k in range(KC)]
        wchunks["in"] = [(k, in_stage[k]) for k in range(KC)]
        corr_stage = flat(x)[:, KC * C:KC * C + C]
        ROW_SPARE = NT * (PITCH + 2 * REACH + 1) + 2 * NT * TAPS
        score_rows = (odd[:, KC * C:KC * C + HEADS * N], xn[:, 0:HEADS * N])
        cmp_room = (rows[:, ROW_SPARE:ROW_SPARE + N // 2 + 2 * P], xn[:, HEADS * N:HEADS * N + N // 2 + 2 * P])
        score_col = md8[:, 0:HEADS * NT]
        counts = sm[:, 0:3, :]
        mob = sb("mob", [P, 40])
        rank_sum = sb("rank_sum", [P, HEADS * NT])
        wmax = sb("wmax", [P, 17])

        @block.sync
        def _(eng):
            def weights(name):
                src, n = wsrc[name]
                for k, v in wchunks[name]:
                    eng.dma_start(v, src[k * P:(k + 1) * P, :]).then_inc(s["w_in_" + name], 16)

            weights("L0")
            eng.wait_ge(s["pad_zero"], 1)
            eng.dma_start(bass.AP(d_norm.tensor, d_norm.offset, [[N + REACH, 2], [1, REACH]]), zero_pad).then_inc(s["pad_out"], 16)
            eng.wait_ge(s["pad_out"], 16)
            eng.wait_ge(s["w_corrz"], 1)
            for r in range(3):
                eng.dma_start(corr_stage[32 * r:32 * r + TAPS, :], d["wct"]).then_inc(s["w_in_L0"], 16)
            for k in range(KC):
                eng.dma_start(x_next[:, k, :], d["x"][0, k * P:(k + 1) * P, :]).then_inc(s["x_in"], 16)
            weights("in")
            weights("L2")
            weights("L3")
            eng.dma_start(w_dbc[:, :, :], d["wdbct"].rearrange("(k p) o -> p k o", p=P)).then_inc(s["par_in"], 16)
            eng.dma_start(w_out[:, :, :], d["woutt"].rearrange("(k p) o -> p k o", p=P)).then_inc(s["par_in"], 16)

            def image(i, last):
                first = isinstance(i, int) and i == 0
                wait(eng, "gram_pad", i, 5)
                def band_in(pair):
                    wait(eng, f"gram_out{pair}", i, 16)
                    for t in (2 * pair, 2 * pair + 1):
                        band = bass.AP(d_gram.tensor, d_gram.offset + t * P * PITCH, [[PITCH + 1, P], [W, 5], [1, 5]])
                        eng.dma_start(corr_tok[:, t, :].rearrange("p (r c) -> p r c", r=5), band).then_inc(s["gram_in"], 16)

                for pair in range(NT // 2):
                    wait(eng, "gram_ev", i, 2 * pair + 2)
                    eng.dma_start(d_gram[2 * pair:2 * pair + 2].rearrange("t p w -> p t w"),
                                  gram[:, 2 * pair:2 * pair + 2, :]).then_inc(s[f"gram_out{pair}"], 16)
                    if pair:
                        band_in(pair - 1)
                band_in(NT // 2 - 1)
                if first:
                    wait(eng, added(7)[0], i, added(7)[1])
                    eng.dma_start(score_rows[1], d_score.rearrange("p q -> (p q)").unsqueeze(0).broadcast_to([P, HEADS * N])).then_inc(s["score_in"], 16)
                for h in range(HEADS):
                    wait(eng, f"scattered{h}", i, 16 * NT)
                    eng.dma_start(rows4[:, h], d_scan[h].rearrange("(c p) r -> p c r", p=P)).then_inc(s[f"scanrows{h}"], 16)
                for h in range(HEADS):
                    wait(eng, "y_ev", i, 4 * (h + 1))
                    eng.dma_start(d_y[h].rearrange("(c p) r -> p c r", p=P), yscan[:, h]).then_inc(s[f"y_out{h}"], 16)
                if not last:
                    wait(eng, "y_mm", i, 4 * HEADS)
                    for k in range(KC):
                        eng.dma_start(x_next[:, k, :], d["x"][bass.ds(i + 1, 1), k * P:(k + 1) * P, :].rearrange("a p n -> (a p) n")).then_inc(s["x_in"], 16)
                for k in range(KC):
                    wait(eng, added(28 + k)[0], i, added(28 + k)[1])
                    eng.dma_start(d["out"][bass.ds(i, 1), k * P:(k + 1) * P, :].rearrange("a p n -> (a p) n"), x[:, k, :]).then_inc(s["x_out"], 16)

            image(0, False)
            with eng.Fori(1, B - 1) as i:
                image(i, False)
            image(B - 1, True)
            eng.wait_ge(s["x_out"], B * per["x_out"] + primed["x_out"])

        @block.gpsimd
        def _(eng):
            eng.sem_inc(s["x_out"], primed["x_out"])
            eng.memset(corr_stage, 0.0).then_inc(s["w_corrz"], 1)
            eng.memset(zero_pad, 0.0).then_inc(s["pad_zero"], 1)
            eng.memset(minus_half, -0.5).then_inc(s["half_in"], 1)
            eng.wait_ge(s["half_in"], 1)

            def rstd(i, g):
                for k in range(KC):
                    wait(eng, "gn_var", i, 4 * (g - 1) + k + 1)
                    eng.tensor_tensor(st[:, k, 4:5], st[:, k, 3:4], minus_half, ALU.pow).then_inc(s["gn_rstd"], 1)

            def first_rstd(i):
                wait(eng, "first_step", i, 4)
                eng.tensor_tensor(st_next[:, :, 4], st_next[:, :, 3], minus_half.broadcast_to([P, KC]), ALU.pow).then_inc(s["first_rstd"], 1)

            first_rstd(0)

            def image(i, last):
                first = isinstance(i, int) and i == 0
                eng.memset(gram[:, :, 0:2], 0.0).then_inc(s["gram_pad"], 1)
                eng.memset(gram[:, :, 2 + WIN:PITCH], 0.0).then_inc(s["gram_pad"], 1)
                eng.memset(gram[:, 0, 2:2 + 64], 0.0).then_inc(s["gram_pad"], 1)
                eng.memset(gram[:, NT - 1, 2 + WIN - 64:2 + WIN], 0.0).then_inc(s["gram_pad"], 1)
                wait(eng, "gn_split", i, 8)
                eng.nop(nofuse=True)
                eng.memset(corr3[:, :, :, TAPS:], 0.0).then_inc(s["gram_pad"], 1)
                for half in range(2):
                    wait(eng, "norm_max", i, half + 1)
                    c = slice(half * NT // 2, (half + 1) * NT // 2)
                    eng.tensor_tensor(square[:, 1, c], square[:, 0, c], minus_half.broadcast_to([P, NT // 2]), ALU.pow).then_inc(s["norm_pow"], 1)
                if first:
                    for n, (k, v) in enumerate(wchunks["in"]):
                        eng.wait_ge(s["w_hi_in"], n + 1)
                        eng.tensor_tensor(w_lo["in"][:, k, :], v, w_hi["in"][:, k, :], ALU.subtract).then_inc(s["w_lo_in"], 1)
                for u in (0, 2):
                    add(eng, i, u, x_next, 0)
                rstd(i, 1)
                wait(eng, "gemm_done", i, 8)
                eng.nop(nofuse=True)
                eng.memset(conv_in[:, :, 0:N + 2:N + 1], 0.0).then_inc(s["conv_pad"], 1)
                wait(eng, "row_ready", i, 1)
                wait(eng, "tok_ev", i, KC)
                eng.nop(nofuse=True)
                for h in range(HEADS):
                    if first:
                        eng.wait_ge(s["p_rank"], h + 1)
                        eng.nop(nofuse=True)
                    for t in range(NT):
                        eng.indirect_dma_start(d_scan[h], bass.IndirectOffsetOnAxis(ap=rank[:, h, t:t + 1], axis=0),
                                               rows4[:, h, t, :], None).then_inc(s[f"scattered{h}"], 16)
                def diagonal(h):
                    wait(eng, "fac_8", i, 5 * h + 5)
                    wait(eng, "m_ev", i, 2 * h)
                    eng.tensor_tensor(diag.rearrange("p (c b t) -> p c b t", c=NT, t=T8),
                                      md8[:, :].rearrange("p (c t) -> p c t", c=NT).unsqueeze(2).broadcast_to([P, NT, 16, T8]),
                                      const("block16").unsqueeze(1).unsqueeze(3).broadcast_to([P, NT, 16, T8]),
                                      ALU.mult).then_inc(s["fac_diag"], 1)

                def gather(h):
                    wait(eng, f"y_out{h}", i, 16)
                    wait(eng, "y_mm", i, 4 * (h + 1))
                    eng.nop(nofuse=True)
                    for t in range(NT):
                        eng.indirect_dma_start(ytok[h][:, t, :], None, d_y[h],
                                               bass.IndirectOffsetOnAxis(ap=rank[:, h, t:t + 1], axis=0)).then_inc(s[f"y_in{h}"], 16)

                diagonal(0)
                diagonal(1)
                gather(0)
                gather(1)
                for u in (8, 10):
                    add(eng, i, u, x, 32)
                rstd(i, 2)
                for u in range(16, 20):
                    add(eng, i, u, x, 40)
                rstd(i, 3)
                if not last:
                    first_rstd(i + 1)
                for u in range(24, 32):
                    add(eng, i, u, x, 48)

            image(0, False)
            with eng.Fori(1, B - 1) as i:
                image(i, False)
            image(B - 1, True)

        @block.scalar
        def _(eng):
            act = eng.activation
            eng.dma_start(cst[:, :], d["cst"]).then_inc(s["cst_in"], 16)
            eng.dma_start(mob[:, 0:8], d["mob"].broadcast_to([P, 8])).then_inc(s["mob_in"], 16)
            for name, col, n in (("b0", B0, 4), ("bin", BIN, 12), ("bconv", BCONV, 4), ("bout", BOUT, 4),
                                 ("bl2", BL2, 4), ("bl3", BL3, 4)):
                eng.dma_start(par[:, col:col + n], d[name]).then_inc(s["par_in"], 16)
            eng.dma_start(par[:, TAP:TAP + 3 * KC], d["taps"]).then_inc(s["par_in"], 16)
            eng.dma_start(bdbc_sb[:, :], d["bdbc"].broadcast_to([P, HEADS * J])).then_inc(s["par_in"], 16)
            eng.dma_start(mob[:, 24:40], d["alog"].broadcast_to([P, 16])).then_inc(s["a_in"], 16)
            eng.dma_start(par[:, 56:58], d["dpar"].broadcast_to([P, 2])).then_inc(s["a_in"], 16)
            for h in range(HEADS):
                eng.dma_start(par[32 * h:32 * h + 8, 58:59], d["alog_col"][h]).then_inc(s["a_in"], 16)
            eng.wait_ge(s["p_abcd"], 3)
            act(mob[:, 20:22], mob[:, 18:20], ACT.Sqrt).then_inc(s["p_sqrt"], 1)
            eng.wait_ge(s["p_score"], SCORES)
            eng.dma_start(d_score, score_col).then_inc(s["score_out"], 16)
            scale = lambda name: par[:, SCL + WI[name]:SCL + WI[name] + 1]
            eng.wait_ge(s["w_scl"], 4)
            for k, v in wchunks["L0"]:
                act(w_hi["L0"][:, k, :], v, ACT.Copy, scale=scale("L0")).then_inc(s["w_hi_L0"], 1)
            for r in range(3):
                act(w_corr[32 * r:32 * r + 32, :], corr_stage[32 * r:32 * r + 32, :], ACT.Copy, scale=par[32 * r:32 * r + 32, SCL:SCL + 1]).then_inc(s["w_hi_L0"], 1)
            eng.wait_ge(s["score_out"], 16)
            eng.dma_start(score_rows[0], d_score.rearrange("p q -> (p q)").unsqueeze(0).broadcast_to([P, HEADS * N])).then_inc(s["score_in"], 16)
            eng.wait_ge(s["a_in"], 64)
            act(amat[:, :, :].rearrange("p h s -> p (h s)"), mob[:, 24:40], ACT.Exp).then_inc(s["a_exp"], 1)
            for h in range(HEADS):
                act(par[32 * h:32 * h + 8, 59:60], par[32 * h:32 * h + 8, 58:59], ACT.Exp).then_inc(s["a_exp"], 1)
            eng.wait_ge(s["par_in"], 16 * 10)

            def hi(i, g, n, src):
                half, k = divmod(n, KC)
                c = slice(half * HALF, (half + 1) * HALF)
                dst = (even_hi, odd_hi)[g % 2]
                if g == 0:
                    wait(eng, "first_bias", i, 1)
                elif half == 0:
                    wait(eng, "gn_bias", i, 4 * (g - 1) + k + 1)
                if g == 2 and n == 0:
                    wait(eng, "y_out0", i, 16)
                    wait(eng, "y_out1", i, 16)
                if g == 3 and n == 0:
                    wait(eng, "gemm_done", i, 32)
                stat = st if g else st_next
                act(dst[:, k, c], src[:, k, c], ACT.Identity, bias=stat[:, k, 5:6], scale=stat[:, k, 4:5]).then_inc(s["gn_hi"], 1)

            def evac_res(i, u, base, bias, inv, func):
                half, o = divmod(u % 8, KC)
                wait(eng, "gemm_done", i, base + u % 8 + 1)
                if u >= 3:
                    wait(eng, added(u - 3)[0], i, added(u - 3)[1])
                bank = bank_of[base + u % 8]
                act(tmp[:, u % 3, :], ps[bank][:, :], func, bias=par[:, bias + o:bias + o + 1],
                    scale=inv).then_inc(s["gemm_evac"], 1)

            def inv(name):
                return par[:, INV + WI[name]:INV + WI[name] + 1]

            def evac_unit(i, q):
                part, half, o = in_unit_at(q)
                wait(eng, "gemm_done", i, 8 + q + 1)
                c = slice(half * HALF, (half + 1) * HALF)
                if part == 0:
                    dst = conv_in[:, o, 1 + half * HALF:1 + (half + 1) * HALF]
                else:
                    dst = (gate, res)[part - 1][:, o, c]
                col = BIN + (0, 8, 4)[part] + o
                act(dst, ps[bank_of[8 + q]][:, :], ACT.Silu, bias=par[:, col:col + 1], scale=inv("in")).then_inc(s["gemm_evac"], 1)
                if part == 1:
                    wait(eng, "gemm_evac", i, 8 + q + 1)
                    act(dst, dst, ACT.Silu).then_inc(s["silu2"], 1)

            for n in range(2 * KC):
                hi(0, 0, n, x_next)

            def late_weights():
                eng.wait_ge(s["w_scl"], 8)
                for n, (k, v) in enumerate(wchunks["in"]):
                    act(v, v, ACT.Copy, scale=scale("in")).then_inc(s["w_sc_in"], 1)
                    eng.wait_ge(s["w_sc_in"], n + 1)
                    act(w_hi["in"][:, k, :], v, ACT.Copy).then_inc(s["w_hi_in"], 1)
                for name in ("L2", "L3"):
                    for k, v in wchunks[name]:
                        act(w_hi[name][:, k, :], v, ACT.Copy, scale=scale(name)).then_inc(s["w_hi_" + name], 1)

            def evacs(i, u0, base, bias, scale, func, start=0):
                for u in range(start, 8):
                    evac_res(i, u0 + u, base, bias, scale, func)
                    if u >= 5:
                        hi(i, u0 // 8 + 1, u - 5, x)
                for n in range(3, 8):
                    hi(i, u0 // 8 + 1, n, x)

            def image(i, last):
                first = isinstance(i, int) and i == 0
                wait(eng, "norm_row", i, 1)
                eng.dma_start(d_norm[0, REACH:REACH + N].rearrange("(t p) -> t p", t=NT), norm_row).then_inc(s["norm_out"], 16)
                wait(eng, "norm_out", i, 16)
                around = bass.AP(d_norm.tensor, d_norm.offset, [[1, P], [P, NT], [1, 2 * REACH + 1]])
                eng.dma_start(near, around).then_inc(s["norm_in"], 16)
                if first:
                    late_weights()

                def shifts_copy(half):
                    wait(eng, "corr_t", i, half + 1)
                    act(corr[0:96, half * HALF:(half + 1) * HALF], ps[7][0:96, :], ACT.Copy).then_inc(s["corr_cp"], 1)

                shifts_copy(0)
                evac_res(i, 0, 0, B0, inv("L0"), ACT.Relu)
                shifts_copy(1)
                evacs(i, 0, 0, B0, inv("L0"), ACT.Relu, 1)
                wait(eng, "conv_pad", i, 1)
                for q in range(8):
                    evac_unit(i, q)
                    if q >= 5:
                        conv_silu(i, q - 5)
                fill = iter(range(8, 24))

                def filler(n):
                    for _ in range(n):
                        evac_unit(i, next(fill))

                tok_evac(i, 0)
                filler(1)
                conv_silu(i, 3)
                tok_evac(i, 1)
                filler(1)
                tok_evac(i, 2)
                filler(1)
                wait(eng, "sp_dve", i, 1)
                act(sm[:, 4, :], sm[:, 3, :], ACT.Exp, scale=-1.0).then_inc(s["sp_act"], 1)
                wait(eng, "sp_dve", i, 2)
                act(sm[:, 6, :], sm[:, 5, :], ACT.Ln).then_inc(s["sp_act"], 1)
                tok_evac(i, 3)
                filler(7)

                def scan_decays(h):
                    wait(eng, "fac_mm", i, 2 * h + 2)
                    act(gam[32 * h:32 * h + 8, :], ps[7][32 * h:32 * h + 8, 320:328], ACT.Exp,
                        scale=par[32 * h:32 * h + 8, 60:61]).then_inc(s["fac_gam"], 1)

                def scan_exp(h, n):
                    factor = (pfac, qfac, arg8[:, :, :].rearrange("p a s -> p (a s)"))[n]
                    wait(eng, "fac_arg", i, 3 * h + n + 1)
                    act(factor, factor, ACT.Exp).then_inc(s["fac_exp"], 1)

                def scan_factors(h):
                    for half in range(2):
                        wait(eng, "fac_tp", i, 4 * h + half + 1)
                        act(pT[:, half * HALF:(half + 1) * HALF], ps[3 + half][:, :], ACT.Copy,
                            scale=const("keep")[:, h:h + 1]).then_inc(s["fac_ptq"], 1)
                    for half in range(2):
                        wait(eng, "fac_tp", i, 4 * h + half + 3)
                        act(qT[:, half * HALF:(half + 1) * HALF], ps[5 + half][:, :], ACT.Copy).then_inc(s["fac_ptq"], 1)

                def scan_y(h, j):
                    wait(eng, "y_mm", i, 4 * h + j + 1)
                    act(yscan[:, h, 2 * j:2 * j + 2, :], ps[3 + j % 2][:, :].rearrange("p (c d) -> p c d", c=2),
                        ACT.Copy).then_inc(s["y_ev"], 1)

                scan_decays(0)
                for n in range(3):
                    scan_exp(0, n)
                filler(2)
                scan_factors(0)
                filler(1)
                scan_decays(1)
                scan_y(0, 0)
                scan_exp(1, 0)
                scan_y(0, 1)
                scan_exp(1, 1)
                scan_y(0, 2)
                scan_y(0, 3)
                scan_exp(1, 2)
                scan_factors(1)
                filler(2)
                for j in range(4):
                    scan_y(1, j)
                filler(1)
                evacs(i, 8, 32, BOUT, 1.0, ACT.Silu)
                evacs(i, 16, 40, BL2, inv("L2"), ACT.Identity)
                for u in range(8):
                    evac_res(i, 24 + u, 48, BL3, inv("L3"), ACT.Identity)
                    if not last and 3 <= u < 7:
                        if u == 3:
                            wait(eng, "gemm_done", i, 48)
                        hi(i + 1, 0, 2 * (u - 3), x_next)
                        hi(i + 1, 0, 2 * (u - 3) + 1, x_next)
                if not last:
                    wait(eng, "res_pool", i, 16)

            def conv_silu(i, k):
                wait(eng, "conv_mac", i, 3 * k + 3)
                act(conv_out[:, k % 2, :], conv_out[:, k % 2, :], ACT.Silu).then_inc(s["conv_act"], 1)

            def tok_evac(i, k):
                wait(eng, "tok_mm", i, k + 1)
                for half in range(2):
                    ins = act(rows4[:, k // 2, 4 * half:4 * half + 4, (k % 2) * P:(k % 2) * P + P],
                              ps[tok_banks[k % 2][half]][:, :].rearrange("p (t c) -> p t c", t=4), ACT.Copy)
                ins.then_inc(s["tok_ev"], 1)

            image(0, False)
            with eng.Fori(1, B - 1) as i:
                image(i, False)
            image(B - 1, True)

        @block.vector
        def _(eng):
            TT, TS, STT = eng.tensor_tensor, eng.tensor_scalar, eng.scalar_tensor_tensor
            eng.wait_ge(s["mob_in"], 16)
            eng.wait_ge(s["cst_in"], 16)
            m = mob[:, 0:8].rearrange("p (h c) -> p h c", h=HEADS)
            TT(mob[:, 16:18], m[:, :, 0], m[:, :, 3], ALU.mult).then_inc(s["p_abcd"], 1)
            TT(mob[:, 18:20], m[:, :, 1], m[:, :, 2], ALU.mult).then_inc(s["p_abcd"], 1)
            eng.wait_ge(s["p_abcd"], 2)
            c = 1
            TT(mob[:, 16:18], mob[:, 16:18], mob[:, 18:20], ALU.subtract).then_inc(s["p_score"], 1)
            eng.wait_ge(s["p_score"], 1)
            STT(mob[:, 18:20], mob[:, 16:18], -1.0, mob[:, 16:18], ALU.mult, ALU.max).then_inc(s["p_score"], 1)
            eng.wait_ge(s["p_score"], 2)
            TS(mob[:, 18:20], mob[:, 18:20], 0.001, None, ALU.max).then_inc(s["p_abcd"], 1)
            eng.wait_ge(s["p_sqrt"], 1)
            eng.reciprocal(mob[:, 22:24], mob[:, 20:22]).then_inc(s["p_score"], 1)
            c = 3
            eng.wait_ge(s["p_score"], c)
            for h in range(HEADS):
                TS(mob[:, 8 + 4 * h:12 + 4 * h], mob[:, 4 * h:4 * h + 4], mob[:, 22 + h:23 + h], None, ALU.mult).then_inc(s["p_score"], 1)
                c += 1
            eng.wait_ge(s["p_score"], c)
            xs, ys = const("grid")[:, 0:NT], const("grid")[:, NT:2 * NT]

            def score_steps(h):
                a, b, cc, dd = (mob[:, 8 + 4 * h + j:9 + 4 * h + j] for j in range(4))
                out = score_col[:, NT * h:NT * h + NT]
                nr, dr, di = (md8[:, 16 + 8 * (3 * h + j):24 + 8 * (3 * h + j)] for j in range(3))
                return [
                    lambda: TS(nr, xs, a, b, ALU.mult, ALU.add),
                    lambda: TS(dr, xs, cc, dd, ALU.mult, ALU.add),
                    lambda: TS(di, ys, cc, None, ALU.mult),
                    lambda: TS(dr, dr, 1e-6, None, ALU.add),
                    lambda: STT(out, di, -1.3, dr, ALU.mult, ALU.add),
                    lambda: TT(nr, nr, out, ALU.mult),
                    lambda: STT(out, dr, 1.3, di, ALU.mult, ALU.add),
                    lambda: STT(out, ys, a, out, ALU.mult, ALU.mult),
                    lambda: TT(nr, nr, out, ALU.add),
                    lambda: TT(dr, dr, dr, ALU.mult),
                    lambda: TT(di, di, di, ALU.mult),
                    lambda: TT(dr, dr, di, ALU.add),
                    lambda: eng.reciprocal(dr, dr),
                    lambda: TT(out, nr, dr, ALU.mult),
                ]

            for one, other in zip(score_steps(0), score_steps(1)):
                one().then_inc(s["p_score"], 1)
                other().then_inc(s["p_score"], 1)
                c += 2
                eng.wait_ge(s["p_score"], c)
            assert c == SCORES

            def maxima(name, views, col):
                eng.wait_ge(s["w_in_" + name], 16 * len(views) if name != "L0" else 16 * (KC + 3))
                for n, v in enumerate(views):
                    ins = eng.tensor_reduce(wmax[:, col + n:col + n + 1], v, AX.X, ALU.max, apply_absolute_value=True)
                    ins.then_inc(s["w_max"], 1)

            def scales(first, n, rnd):
                eng.wait_ge(s["w_maxt"], rnd + 1)
                eng.tensor_reduce(par[0:n, 62:63], ps[7][0:n, 0:P], AX.X, ALU.max).then_inc(s["w_maxr"], 1)
                eng.wait_ge(s["w_maxr"], 2 * rnd + 1)
                TS(par[0:n, WMAX:WMAX + n], ident[0:n, 0:n], par[0:n, 62:63], None, ALU.mult).then_inc(s["w_maxr"], 1)
                eng.wait_ge(s["w_maxb"], rnd + 1)
                scl = par[:, SCL + first:SCL + first + n].bitcast(I32)
                invs = par[:, INV + first:INV + first + n].bitcast(I32)
                eng.tensor_copy(par[:, SCL + first:SCL + first + n], ps[7][:, 0:n]).then_inc(s["w_scl"], 1)
                eng.wait_ge(s["w_scl"], 4 * rnd + 1)
                TS(scl, scl, 0x7F800000, None, ALU.bitwise_and).then_inc(s["w_scl"], 1)
                eng.wait_ge(s["w_scl"], 4 * rnd + 2)
                TS(invs, scl, float(14 << 23), float(-(13 << 23)), ALU.max, ALU.add).then_inc(s["w_scl"], 1)
                eng.wait_ge(s["w_scl"], 4 * rnd + 3)
                TS(scl, invs, -1.0, float(254 << 23), ALU.mult, ALU.add).then_inc(s["w_scl"], 1)
                eng.wait_ge(s["w_scl"], 4 * rnd + 4)

            def low(name, k, v):
                return STT(w_lo[name][:, k, :], v, par[:, SCL + WI[name]:SCL + WI[name] + 1], w_hi[name][:, k, :],
                           ALU.mult, ALU.subtract)

            maxima("L0", [v for _, v in wchunks["L0"]] + [corr_stage], 0)
            eng.wait_ge(s["w_max"], 5)
            eng.tensor_reduce(par[:, 44:45], wmax[:, 0:5], AX.X, ALU.max).then_inc(s["w_maxc"], 1)
            scales(0, 1, 0)
            def stats_of(g):
                return (bn, st, "gn_raw", 12 * (g - 1)) if g else (bn_next, st_next, "first_raw", 0)

            def gn_stats(i, g, k, half, src):
                b, _, raw, _ = stats_of(g)
                if g == 0:
                    eng.wait_ge(s["x_in"], (i + 1) * per["x_in"])
                else:
                    name, n = added(8 * (g - 1) + 4 * half + k)
                    wait(eng, name, i, n)
                eng.bn_stats(b[:, k, half, :], src[:, k, half * HALF:(half + 1) * HALF]).then_inc(s[raw], 1)

            def gn_a(i, g, k, src):
                b, st, raw, q = stats_of(g)
                q += 4 + 2 * k
                gn_stats(i, g, k, 1, src)
                wait(eng, raw, i, q + 1)
                eng.nop(nofuse=True)
                eng.bn_aggr(st[:, k, 0:2], b[:, k, :, :]).then_inc(s[raw], 1)
                wait(eng, raw, i, q + 2)
                STT(st[:, k, 1:2], st[:, k, 0:1], st[:, k, 0:1], st[:, k, 1:2],
                    ALU.mult, ALU.add).then_inc(s["gn_stat" if g else "first_stat"], 1)

            def gn_b(i, g, k):
                q = 4 * (g - 1) + k
                wait(eng, "gn_sum", i, q + 1)
                eng.tensor_copy(st[:, k, 0:2], gn_ps).then_inc(s["gn_got"], 1)
                wait(eng, "gn_got", i, q + 1)
                STT(st[:, k, 2:3], st[:, k, 0:1], st[:, k, 0:1], st[:, k, 1:2],
                    ALU.mult, ALU.subtract).then_inc(s["gn_neg"], 1)
                wait(eng, "gn_neg", i, q + 1)
                TS(st[:, k, 3:4], st[:, k, 2:3], -1.0, EPS, ALU.mult, ALU.add).then_inc(s["gn_var"], 1)

            def gn_c(i, g, n, src):
                half, k = divmod(n, KC)
                _, st, _, _ = stats_of(g)
                if g == 0:
                    wait(eng, "first_bias", i, 1)
                elif half == 0:
                    wait(eng, "gn_rstd", i, 4 * (g - 1) + k + 1)
                    STT(st[:, k, 5:6], st[:, k, 0:1], -1.0, st[:, k, 4:5],
                        ALU.mult, ALU.mult).then_inc(s["gn_bias"], 1)
                    wait(eng, "gn_bias", i, 4 * (g - 1) + k + 1)
                if half == 1:
                    wait(eng, "gn_split", i, split_n(g, n - 4))
                TS(normed[:, n % 4, :], src[:, k, half * HALF:(half + 1) * HALF], st[:, k, 4:5], st[:, k, 5:6],
                   ALU.mult, ALU.add).then_inc(s["gn_norm"], 1)

            def gn_d(i, g, n):
                half, k = divmod(n, KC)
                c = slice(half * HALF, (half + 1) * HALF)
                his, los = ((even_hi, even_lo), (odd_hi, odd_lo))[g % 2]
                wait(eng, "gn_hi", i, 8 * g + n + 1)
                wait(eng, "gn_norm", i, 8 * g + n + 1)
                TT(los[:, k, c], normed[:, n % 4, :], his[:, k, c], ALU.subtract).then_inc(s["gn_split"], 1)

            def second_halves(i, g, src):
                gn_c(i, g, 4, src)
                for n in range(5, 8):
                    gn_c(i, g, n, src)
                    gn_d(i, g, n - 1)
                gn_d(i, g, 7)

            def adds_norm(i, stg, src, base, between=None):
                g = stg + 1
                for k in range(KC):
                    if not pool_adds(8 * stg + k):
                        add(eng, i, 8 * stg + k, src, base)
                    gn_stats(i, g, k, 0, x)
                for k in range(KC):
                    if k:
                        gn_b(i, g, k - 1)
                    add(eng, i, 8 * stg + 4 + k, src, base)
                    if k:
                        gn_c(i, g, k - 1, x)
                    gn_a(i, g, k, x)
                    if k:
                        gn_d(i, g, k - 1)
                gn_b(i, g, 3)
                gn_c(i, g, 3, x)
                gn_d(i, g, 3)
                if between:
                    between()
                second_halves(i, g, x)

            def first_stats(i):
                for k in range(KC):
                    gn_stats(i, 0, k, 0, x_next)

            def first_moments(i):
                for k in range(KC):
                    gn_a(i, 0, k, x_next)

            def first_variance(i):
                mean, second, square, var = (st_next[:, :, j] for j in range(4))
                wait(eng, "first_sum", i, 1)
                eng.tensor_copy(st_next[:, :, 0:2], first_ps.rearrange("p (k a) -> p k a", k=KC)).then_inc(s["first_step"], 1)
                wait(eng, "first_step", i, 1)
                TT(square, mean, mean, ALU.mult).then_inc(s["first_step"], 1)
                wait(eng, "first_step", i, 2)
                TT(square, second, square, ALU.subtract).then_inc(s["first_step"], 1)
                wait(eng, "first_step", i, 3)
                TS(var, square, EPS, None, ALU.add).then_inc(s["first_step"], 1)

            def first_norm(i):
                wait(eng, "first_rstd", i, 1)
                STT(st_next[:, :, 5], st_next[:, :, 0], -1.0, st_next[:, :, 4], ALU.mult, ALU.mult).then_inc(s["first_bias"], 1)
                gn_c(i, 0, 0, x_next)
                for n in range(1, 8):
                    if n == 4:
                        gn_d(i, 0, 3)
                    gn_c(i, 0, n, x_next)
                    if n != 4:
                        gn_d(i, 0, n - 1)
                gn_d(i, 0, 7)

            first_stats(0)
            first_moments(0)
            first_variance(0)
            for n, (k, v) in enumerate(wchunks["L0"]):
                eng.wait_ge(s["w_hi_L0"], n + 1)
                low("L0", k, v).then_inc(s["w_lo_L0"], 1)
            eng.wait_ge(s["w_hi_L0"], KC + 3)
            STT(w_corr[64:96, :], corr_stage[64:96, :], par[64:96, SCL:SCL + 1], w_corr[64:96, :],
                ALU.mult, ALU.subtract).then_inc(s["w_lo_L0"], 1)
            first_norm(0)

            def late_scales():
                maxima("in", [v for _, v in wchunks["in"]], 5)
                maxima("L2", [v for _, v in wchunks["L2"]], 9)
                maxima("L3", [v for _, v in wchunks["L3"]], 13)
                eng.wait_ge(s["w_max"], 17)
                eng.tensor_reduce(par[:, 44:47], wmax[:, 5:17].rearrange("p (w k) -> p w k", k=KC), AX.X, ALU.max).then_inc(s["w_maxc"], 1)
                scales(1, 3, 1)

            def late_lows():
                for name in ("L2", "L3"):
                    for n, (k, v) in enumerate(wchunks[name]):
                        eng.wait_ge(s["w_hi_" + name], n + 1)
                        low(name, k, v).then_inc(s["w_lo_rest"], 1)
                TS(amat[:, :, :], amat[:, :, :], -1.0, None, ALU.mult).then_inc(s["a_neg"], 1)
                TS(par[0:8, 60:61], par[0:8, 59:60], -1.0, None, ALU.mult).then_inc(s["a_neg"], 1)
                TS(par[32:40, 60:61], par[32:40, 59:60], -1.0, None, ALU.mult).then_inc(s["a_neg"], 1)
                for h in range(HEADS):
                    TS(deq8[:, h, :], const("eq8"), par[:, 56 + h:57 + h], None, ALU.mult).then_inc(s["a_neg"], 1)

            def count_ranks(h):
                c = CMP_STEPS * h
                if h == 0:
                    eng.memset(counts, 0.0).then_inc(s["p_zero"], 1)
                    eng.wait_ge(s["p_zero"], 1)
                eng.wait_ge(s["score_in"], 16 * (h + 1))
                cmp_row = cmp_room[h][:, 0:N // 2].bitcast(F16).rearrange("p (n t) -> p n t", t=NT)
                cmp_tile = cmp_room[h][:, N // 2:].rearrange("p (b n) -> p b n", b=2)
                row_scores = score_rows[h].rearrange("p (n q) -> p n q", q=HEADS * NT)
                for t in range(NT):
                    q = NT * h + t
                    own = score_col[:, q:q + 1]
                    tile = row_scores[:, :, q]
                    if c:
                        eng.wait_ge(s["p_count"], c)
                    STT(cmp_tile[:, 0, :], tile, own, after, ALU.is_equal, ALU.mult).then_inc(s["p_count"], 1)
                    c += 1
                    for a, (start, n, op) in enumerate(((NT * h, t, ALU.is_le), (q + 1, NT - 1 - t, ALU.is_lt))):
                        if n > 0:
                            others = row_scores[:, :, start:start + n]
                            TS(cmp_row[:, :, start % NT:start % NT + n], others, own, 0.0, op, ALU.add,
                               counts[:, a, q:q + 1]).then_inc(s["p_count"], 1)
                            c += 1
                    eng.wait_ge(s["p_count"], c)
                    STT(cmp_tile[:, 1, :], tile, own, cmp_tile[:, 0, :], ALU.is_lt, ALU.add).then_inc(s["p_count"], 1)
                    c += 1
                    eng.wait_ge(s["p_count"], c)
                    eng.tensor_reduce(counts[:, 2, q:q + 1], cmp_tile[:, 1, :], AX.X, ALU.add).then_inc(s["p_count"], 1)
                    c += 1
                eng.wait_ge(s["p_count"], c)
                own = rank_sum[:, NT * h:NT * h + NT]
                eng.tensor_reduce(own, counts[:, :, NT * h:NT * h + NT].rearrange("p a q -> p q a"), AX.X, ALU.add).then_inc(s["p_count"], 1)
                assert c + 1 == CMP_STEPS * (h + 1)
                eng.wait_ge(s["p_count"], c + 1)
                eng.tensor_copy(rank[:, h, :], own).then_inc(s["p_rank"], 1)

            def image(i, last):
                first = isinstance(i, int) and i == 0
                def diagonal_of(t):
                    wait(eng, "gram_ev", i, t + 1)
                    eng.tensor_tensor_reduce(work[:, t * P:(t + 1) * P], gram[:, t, 2 + 64:2 + 64 + P], ident, 1.0, 0.0,
                                             ALU.mult, ALU.add, square[:, 0, t:t + 1]).then_inc(s["gram_d"], 1)

                for t in range(NT):
                    a, z = (64 if t == 0 else 0), (WIN - 64 if t == NT - 1 else WIN)
                    wait(eng, "gram_mm", i, (t | 1) + 1)
                    eng.tensor_copy(gram[:, t, 2 + a:2 + z], gram_ps(t)[:, a:z]).then_inc(s["gram_ev"], 1)
                    if t:
                        diagonal_of(t - 1)
                    if t == NT // 2:
                        wait(eng, "gram_d", i, NT // 2)
                        TS(square[:, 0, 0:NT // 2], square[:, 0, 0:NT // 2], 1e-24, None, ALU.max).then_inc(s["norm_max"], 1)
                diagonal_of(NT - 1)
                wait(eng, "gram_d", i, NT)
                TS(square[:, 0, NT // 2:], square[:, 0, NT // 2:], 1e-24, None, ALU.max).then_inc(s["norm_max"], 1)
                wait(eng, "norm_t", i, 1)
                eng.tensor_copy(norm_row, ps[7][0:NT, 0:P]).then_inc(s["norm_row"], 1)
                if first:
                    late_scales()
                    count_ranks(0)
                    late_lows()
                wait(eng, "norm_in", i, 16)
                TT(factors[:, 0].rearrange("p t (r c) -> p t r c", r=5),
                   near_shifts,
                   const("inside").rearrange("p (t r c) -> p t r c", t=NT, r=5), ALU.mult).then_inc(s["norm_m"], 1)
                wait(eng, "norm_m", i, 1)
                TT(factors[:, 1], factors[:, 0], near[:, :, REACH:REACH + 1].broadcast_to([P, NT, TAPS]),
                   ALU.mult).then_inc(s["norm_m"], 1)
                wait(eng, "norm_m", i, 2)
                wait(eng, "gram_in", i, 16 * NT)
                TT(corr3[:, :, :, 0:TAPS], corr_tok.unsqueeze(2).broadcast_to([P, NT, 3, TAPS]),
                   factors[:, 1].unsqueeze(2).broadcast_to([P, NT, 3, TAPS]), ALU.mult).then_inc(s["corr_msk"], 1)
                for half in range(2):
                    wait(eng, "corr_cp", i, half + 1)
                    c = slice(half * HALF, (half + 1) * HALF)
                    TT(corr[32:64, c], ps[7][32:64, :], corr[32:64, c], ALU.subtract).then_inc(s["corr_lo"], 1)
                if first:
                    eng.wait_ge(s["w_lo_in"], KC)
                adds_norm(i, 0, x_next, 0)
                for k in range(KC):
                    wait(eng, "gemm_evac", i, 8 + 4 + k + 1)
                    wait(eng, "conv_pad", i, 1)
                    if k >= 2:
                        wait(eng, "tok_mm", i, k - 1)
                    src, dst = conv_in[:, k, :], conv_out[:, k % 2, :]
                    w = [par[:, TAP + 3 * k + j:TAP + 3 * k + j + 1] for j in range(3)]
                    TS(dst, src[:, 1:N + 1], w[1], par[:, BCONV + k:BCONV + k + 1], ALU.mult, ALU.add).then_inc(s["conv_mac"], 1)
                    wait(eng, "conv_mac", i, 3 * k + 1)
                    STT(dst, src[:, 0:N], w[0], dst, ALU.mult, ALU.add).then_inc(s["conv_mac"], 1)
                    wait(eng, "conv_mac", i, 3 * k + 2)
                    STT(dst, src[:, 2:N + 2], w[2], dst, ALU.mult, ALU.add).then_inc(s["conv_mac"], 1)
                wait(eng, "dbc_mm", i, 1)
                dbc = rows4[:, :, :, DH:ROW]
                for h in range(HEADS):
                    ins = TT(rows4[:, h, :, DH:ROW], ps[0][:, 0:NT * HEADS * J].rearrange("p (t h j) -> p h t j", t=NT, h=HEADS)[:, h],
                             bdbc_sb[:, h * J:(h + 1) * J].unsqueeze(1).broadcast_to([P, NT, J]), ALU.add)
                    ins.then_inc(s["sp_z"], 1)
                wait(eng, "sp_z", i, 2)
                z = rows4[:, :, :, DH]
                v = lambda a: sm[:, a, :].rearrange("p (h t) -> p h t", h=HEADS)
                STT(v(3), z, -1.0, z, ALU.mult, ALU.max).then_inc(s["sp_dve"], 1)
                wait(eng, "sp_act", i, 1)
                TS(v(5), v(4), 1.0, None, ALU.add).then_inc(s["sp_dve"], 1)
                wait(eng, "sp_dve", i, 2)
                TS(v(7), v(5), -1.0, None, ALU.add).then_inc(s["sp_dve"], 1)
                wait(eng, "sp_dve", i, 3)
                TS(v(3), v(7), 0.0, None, ALU.is_equal).then_inc(s["sp_dve"], 1)
                wait(eng, "sp_dve", i, 4)
                wait(eng, "sp_act", i, 2)
                TT(v(7), v(7), v(3), ALU.add).then_inc(s["sp_dve"], 1)
                TT(v(6), v(6), v(3), ALU.add).then_inc(s["sp_dve"], 1)
                wait(eng, "sp_dve", i, 6)
                eng.reciprocal(v(5), v(7)).then_inc(s["sp_dve"], 1)
                TT(v(6), v(6), v(4), ALU.mult).then_inc(s["sp_dve"], 1)
                wait(eng, "sp_dve", i, 8)
                TT(v(6), v(6), v(5), ALU.mult).then_inc(s["sp_dve"], 1)
                wait(eng, "sp_dve", i, 9)
                STT(z, z, 0.0, v(6), ALU.max, ALU.add).then_inc(s["sp_dve"], 1)
                wait(eng, "sp_dve", i, 10)
                for h in range(HEADS):
                    ins = TT(rows4[:, h, :, DH + 1:DH + 1 + S], rows4[:, h, :, DH + 1:DH + 1 + S],
                             rows4[:, h, :, DH].unsqueeze(2).broadcast_to([P, NT, S]), ALU.mult)
                ins.then_inc(s["row_ready"], 1)
                if first:
                    count_ranks(1)
                scan_masks(i, 0)
                scan_factors(i, 0)
                scan_masks(i, 1)
                scan_states(i, 0)
                scan_factors(i, 1)
                scan_states(i, 1)
                for k in range(KC):
                    if k == 2 and not last:
                        first_stats(i + 1)
                        first_moments(i + 1)
                    wait(eng, "yt_mm", i, k + 1)
                    wait(eng, "silu2", i, 8)
                    wait(eng, "gemm_evac", i, 8 + 20 + k + 1)
                    for half in range(2):
                        c = slice(half * HALF, (half + 1) * HALF)
                        TT(gate[:, k, c], ps[yt_banks[k][half]][:, :], gate[:, k, c], ALU.mult).then_inc(s["y_gate"], 1)
                        wait(eng, "y_gate", i, 2 * k + half + 1)
                        TT(gate[:, k, c], gate[:, k, c], res[:, k, c], ALU.add).then_inc(s["y_res"], 1)
                if last:
                    adds_norm(i, 1, x, 32)
                    adds_norm(i, 2, x, 40)
                else:
                    adds_norm(i, 1, x, 32)
                    adds_norm(i, 2, x, 40, between=lambda: first_variance(i + 1))
                    first_norm(i + 1)

            def scan_columns(h):
                r = rows4[:, h]
                return r[:, :, DH], r[:, :, DH + 1:DH + 1 + S], r[:, :, DH + 1 + S:ROW]

            def scan_masks(i, h):
                dt, _, cst_c = scan_columns(h)
                wait(eng, f"scanrows{h}", i, 16)
                wait(eng, "fac_mm", i, 2 * h)
                dtg = dt.unsqueeze(2).broadcast_to([P, NT, G])
                left = const("left").rearrange("p (h g) -> p h g", h=HEADS)[:, h]
                right = const("right").rearrange("p (h g) -> p h g", h=HEADS)[:, h]
                TT(mv[:, 0], dtg, left.unsqueeze(1).broadcast_to([P, NT, G]), ALU.mult).then_inc(s["fac_mv"], 1)
                TT(mv[:, 1], dtg, right.unsqueeze(1).broadcast_to([P, NT, G]), ALU.mult).then_inc(s["fac_mv"], 1)
                TT(mv8[:, :, :], dt.unsqueeze(2).broadcast_to([P, NT, T8]),
                   const("within8").unsqueeze(1).broadcast_to([P, NT, T8]), ALU.mult).then_inc(s["fac_mv"], 1)
                TT(mvc[:, :, :, :], cst_c.unsqueeze(2).broadcast_to([P, NT, T8, S]),
                   const("eq8").unsqueeze(1).unsqueeze(3).broadcast_to([P, NT, T8, S]), ALU.mult).then_inc(s["fac_mv"], 1)

            def scan_factors(i, h):
                _, wgt, cst_c = scan_columns(h)
                a = amat[:, h, :].unsqueeze(1)
                wait(eng, "fac_mm", i, 2 * h + 2)
                wait(eng, "fac_gam", i, h + 1)
                wait(eng, "dh_mm", i, 4 * h)
                wait(eng, "fac_tp", i, 4 * h)
                def exponents(n):
                    dst, lo, cols = ((pfac, 0, P), (qfac, P, P), (arg8[:, :, :].rearrange("p a s -> p (a s)"), 2 * P, 64))[n]
                    TT(dst.rearrange("p (c s) -> p c s", s=S), ps[7][:, lo:lo + cols].unsqueeze(2).broadcast_to([P, cols, S]),
                       a.broadcast_to([P, cols, S]), ALU.mult).then_inc(s["fac_arg"], 1)

                for n in range(3):
                    exponents(n)
                p4 = pfac.rearrange("p (c g s) -> p c g s", c=NT, g=G)
                q4 = qfac.rearrange("p (c g s) -> p c g s", c=NT, g=G)
                wait(eng, "fac_exp", i, 3 * h + 1)
                TT(p4, p4, wgt.unsqueeze(2).broadcast_to([P, NT, G, S]), ALU.mult).then_inc(s["fac_pq"], 1)
                wait(eng, "fac_exp", i, 3 * h + 2)
                TT(q4, q4, cst_c.unsqueeze(2).broadcast_to([P, NT, G, S]), ALU.mult).then_inc(s["fac_pq"], 1)
                wait(eng, "fac_exp", i, 3 * h + 3)
                a8 = arg8[:, :, :].rearrange("p (c t) s -> p c t s", c=NT)
                TT(arg8[:, :, :], ps[0][:, :].rearrange("p (a s) -> p a s", s=S), arg8[:, :, :], ALU.mult).then_inc(s["fac_8"], 1)
                wait(eng, "fac_8", i, 5 * h + 1)
                TT(a8, a8, wgt.unsqueeze(2).broadcast_to([P, NT, T8, S]), ALU.mult).then_inc(s["fac_8"], 1)
                wait(eng, "fac_8", i, 5 * h + 2)
                wait(eng, "fac_diag", i, h)
                eng.tensor_reduce(md8[:, :], arg8[:, :, :], AX.X, ALU.add).then_inc(s["fac_8"], 1)
                wait(eng, "fac_8", i, 5 * h + 3)
                m8 = md8[:, :].rearrange("p (c t) -> p c t", c=NT)
                TT(m8, m8, const("within8").unsqueeze(1).broadcast_to([P, NT, T8]), ALU.mult).then_inc(s["fac_8"], 1)
                wait(eng, "fac_8", i, 5 * h + 4)
                TT(m8, m8, deq8[:, h, :].unsqueeze(1).broadcast_to([P, NT, T8]), ALU.add).then_inc(s["fac_8"], 1)

            def scan_states(i, h):
                hp = slice(32 * h, 32 * h + 8)
                for c in range(NT - 1):
                    wait(eng, "dh_mm", i, 4 * h + c // 2 + 1)
                    inc = ps[dh_bank(c)][hp, (c % 2) * DH:(c % 2 + 1) * DH]
                    if c == 0:
                        eng.tensor_copy(hst[hp, 0, :], inc).then_inc(s["h_st"], 1)
                    else:
                        wait(eng, "h_st", i, 7 * h + c)
                        STT(hst[hp, c, :], hst[hp, c - 1, :], gam[hp, c:c + 1], inc, ALU.mult, ALU.add).then_inc(s["h_st"], 1)
                wait(eng, "fac_diag", i, h + 1)
                for half in range(2):
                    wait(eng, "mm_m", i, 2 * h + half + 1)
                    c = slice(half * HALF, (half + 1) * HALF)
                    TT(mmat[:, c], ps[3 + half][:, :], diag[:, c], ALU.add).then_inc(s["m_ev"], 1)

            image(0, False)
            with eng.Fori(1, B - 1) as i:
                image(i, False)
            image(B - 1, True)

        @block.tensor
        def _(eng):
            def mm(out, lhsT, rhs, start, stop, **kw):
                return eng.matmul(out, lhsT, rhs, start=start, stop=stop, skip_group_check=True, **kw)

            eng.wait_ge(s["cst_in"], 16)
            def exchange(rnd, n):
                eng.wait_ge(s["w_maxc"], rnd + 1)
                eng.transpose(ps[7][0:n, 0:P], par[:, WMAX:WMAX + n], ident).then_inc(s["w_maxt"], 1)
                eng.wait_ge(s["w_maxr"], 2 * rnd + 2)
                mm(ps[7][:, 0:n], const("ones")[0:n, :], par[0:n, WMAX:WMAX + n], True, True).then_inc(s["w_maxb"], 1)

            exchange(0, 1)
            eng.wait_ge(s["w_scl"], 1)

            def gn_sum(i, g, k):
                wait(eng, "gn_stat", i, 4 * (g - 1) + k + 1)
                if k:
                    wait(eng, "gn_got", i, 4 * (g - 1) + k)
                if g == 2 and k == 0:
                    wait(eng, "gemm_evac", i, 36)
                mm(gn_ps, const("group_mean"), st[:, k, 0:2], True, True).then_inc(s["gn_sum"], 1)

            def first_sum(i):
                wait(eng, "first_stat", i, KC)
                mm(first_ps.rearrange("p (k a) -> p k a", k=KC), const("group_mean"), st_next[:, :, 0:2], True, True).then_inc(s["first_sum"], 1)

            def passes(wname, his, los, o, half, k, bank, start, stop):
                c = slice(half * HALF, (half + 1) * HALF)
                oc = slice(o * P, (o + 1) * P)
                a = ((w_hi[wname], his), (w_hi[wname], los), (w_lo[wname], his))
                for n, (w, v) in enumerate(a):
                    ins = mm(ps[bank][:, :], w[:, k, oc], v[:, k, c], start and n == 0, stop and n == 2)
                return ins

            def behind(i, g, base, ready, part, others=None):
                for k in range(KC):
                    ready(k)
                    for u in range(4):
                        if k == 0:
                            wait(eng, "gemm_evac", i, bank_free[base + u])
                        ins = part(u, k)
                        if k == KC - 1:
                            ins.then_inc(s["gemm_done"], 1)
                        if g is not None:
                            at = {(0, 0): 2, (0, 1): 3} if g == 3 else {(0, 0): 1, (3, 0): 2, (2, 1): 3}
                            if (u, k) in at:
                                gn_sum(i, g, at[u, k])
                        if others and (u, k) == (2, 2):
                            others()

            first_sum(0)

            def image(i, last):
                first = isinstance(i, int) and i == 0
                wait(eng, "gn_split", i, 8)
                for t in range(NT):
                    a, z = (64 if t == 0 else 0), (WIN - 64 if t == NT - 1 else WIN)
                    tok, win = slice(t * P, (t + 1) * P), slice(t * P - 64 + a, t * P - 64 + z)
                    for k in range(KC):
                        for n, (l, r) in enumerate(((even_hi, even_hi), (even_hi, even_lo), (even_lo, even_hi))):
                            ins = mm(gram_ps(t)[:, a:z], l[:, k, tok], r[:, k, win], k == 0 and n == 0, k == KC - 1 and n == 2)
                    ins.then_inc(s["gram_mm"], 1)
                eng.wait_ge(s["w_lo_L0"], KC + 1)

                def main(u, chunks=range(KC)):
                    half, o = divmod(u, KC)
                    for k in chunks:
                        passes("L0", even_hi, even_lo, o, half, k, bank_of[u], k == 0, False)

                def corr_part(u):
                    half, o = divmod(u, KC)
                    mm(ps[bank_of[u]][:, :], w_corr[0:96, o * P:(o + 1) * P], corr[0:96, half * HALF:(half + 1) * HALF],
                       False, True).then_inc(s["gemm_done"], 1)

                def shifts_to_rows(half):
                    for t in range(4):
                        ins = eng.transpose(ps[7][0:96, t * P:(t + 1) * P],
                                            corr3[:, 4 * half + t].rearrange("p a k -> p (a k)"), ident)
                    ins.then_inc(s["corr_t"], 1)

                if not first:
                    eng.wait_ge(s["gemm_evac"], i * per["gemm_evac"])
                main(0)
                main(1, (0, 1))
                wait(eng, "norm_pow", i, 2)
                eng.transpose(ps[7][0:NT, 0:P], square[:, 1, :], ident).then_inc(s["norm_t"], 1)
                main(1, (2, 3))
                if first:
                    wait(eng, "norm_row", i, 1)
                    exchange(1, 3)
                main(2)
                wait(eng, "gram_ev", i, NT)
                main(3)
                wait(eng, "norm_row", i, 1)
                wait(eng, "corr_msk", i, 1)
                wait(eng, "gram_pad", i, 5)
                shifts_to_rows(0)
                main(4, (0, 1, 2))
                wait(eng, "corr_lo", i, 1)
                corr_part(0)
                shifts_to_rows(1)
                for u in (1, 2, 3):
                    corr_part(u)
                main(4, (3,))
                main(5)
                wait(eng, "corr_lo", i, 2)
                corr_part(4)
                corr_part(5)
                main(6)
                corr_part(6)
                wait(eng, "gemm_evac", i, bank_free[7])
                main(7, (0, 1))
                gn_sum(i, 1, 0)
                main(7, (2, 3))
                corr_part(7)
                def in_part(q, k):
                    part, half, o = in_unit_at(q)
                    col = (0, 2, 1)[part] * KC + o
                    return passes("in", odd_hi, odd_lo, col, half, k, bank_of[8 + q], k == 0, k == KC - 1)

                def in_unit(q, ready=lambda k: None):
                    wait(eng, "gemm_evac", i, bank_free[8 + q])
                    for k in range(KC):
                        ready(k)
                        ins = in_part(q, k)
                    ins.then_inc(s["gemm_done"], 1)

                eng.wait_ge(s["w_lo_in"], KC)
                behind(i, 1, 8, lambda k: wait(eng, "gn_split", i, split_n(1, k)), in_part)
                for q in range(4, 8):
                    in_unit(q, lambda k: wait(eng, "gn_split", i, split_n(1, 4 + k)) if q == 4 else None)
                fill = iter(range(8, 24))

                def filler(n):
                    for _ in range(n):
                        in_unit(next(fill))

                def tokens(k):
                    wait(eng, "conv_act", i, k + 1)
                    if k == 0:
                        wait(eng, "gemm_evac", i, 16)
                    if k >= 2:
                        wait(eng, "tok_ev", i, k - 1)
                    for t in range(NT):
                        lhsT = conv_out[:, k % 2, t * P:(t + 1) * P]
                        ins = mm(ps[0][:, t * HEADS * J:(t + 1) * HEADS * J], lhsT, w_dbc[:, k, :],
                                 k == 0 and t == 0, k == KC - 1)
                        if k == KC - 1 and t == NT - 1:
                            ins.then_inc(s["dbc_mm"], 1)
                    for t in range(NT):
                        ins = eng.transpose(ps[tok_banks[k % 2][t // 4]][:, (t % 4) * P:(t % 4 + 1) * P],
                                            conv_out[:, k % 2, t * P:(t + 1) * P], ident)
                    ins.then_inc(s["tok_mm"], 1)

                for k in range(KC):
                    tokens(k)
                    filler(1)
                filler(6)
                def scan_sums(h):
                    wait(eng, "fac_mv", i, 4 * h + 4)
                    r = rows4[:, h]
                    offl = const("off_left").rearrange("p (h g) -> p h g", h=HEADS)[:, h].unsqueeze(1).broadcast_to([P, NT, G])
                    offr = const("off_right").rearrange("p (h g) -> p h g", h=HEADS)[:, h].unsqueeze(1).broadcast_to([P, NT, G])
                    b7 = ps[7]
                    v3 = lambda t: t.rearrange("p (c g) -> p c g", c=NT)
                    mm(v3(b7[:, 0:P]), after, mv[:, 0], True, False)
                    mm(v3(b7[:, 0:P]), ident, offl, False, True)
                    mm(v3(b7[:, P:2 * P]), upto, mv[:, 1], True, False)
                    mm(v3(b7[:, P:2 * P]), ident, offr, False, True)
                    mm(b7[:, 2 * P:2 * P + 64].rearrange("p (c t) -> p c t", c=NT), after8, mv8[:, :, :], True, True)
                    mm(b7[0:40, 320:328], const("ones")[:, 0:40], r[:, :, DH], True, True).then_inc(s["fac_mm"], 1)
                    if h == 0:
                        wait(eng, "sp_z", i, 2)
                    else:
                        wait(eng, "fac_8", i, 1)
                    mm(ps[0][:, :].rearrange("p (c t s) -> p c t s", c=NT, t=T8).rearrange("p c t s -> p (c t s)"), same8,
                       mvc[:, :, :, :].rearrange("p c t s -> p (c t s)"), True, True).then_inc(s["fac_mm"], 1)

                def scan_inner(h):
                    r = rows4[:, h]
                    if h == 0:
                        wait(eng, "tok_ev", i, KC)
                    else:
                        wait(eng, "y_ev", i, 4)
                        wait(eng, "h_st", i, 7)
                    for a, f in enumerate((pfac, qfac)):
                        wait(eng, "fac_pq", i, 2 * h + a + 1)
                        for c in range(NT):
                            ins = eng.transpose(ps[3 + 2 * a + c // 4][:, (c % 4) * P:(c % 4 + 1) * P],
                                                f[:, c * P:(c + 1) * P], ident)
                            if c % 4 == 3:
                                ins.then_inc(s["fac_tp"], 1)
                    for half in range(2):
                        wait(eng, "fac_ptq", i, 4 * h + (3 if half == 0 else 4))
                        for c in range(4 * half, 4 * half + 4):
                            ins = mm(ps[3 + half][:, (c % 4) * P:(c % 4 + 1) * P], pT[:, c * P:(c + 1) * P],
                                     qT[:, c * P:(c + 1) * P], True, True)
                        ins.then_inc(s["mm_m"], 1)
                    far = FAR_GROUP[h] * S
                    for c in range(NT - 1):
                        if c >= 4 and c % 2 == 0:
                            wait(eng, "h_st", i, 7 * h + c - 2)
                        ins = mm(ps[dh_bank(c)][32 * h:32 * h + 8, (c % 2) * DH:(c % 2 + 1) * DH],
                                 pfac[:, c * P + far:c * P + far + S], r[:, c, 0:DH], True, True)
                        if c % 2 == 1 or c == NT - 2:
                            ins.then_inc(s["dh_mm"], 1)

                def scan_y(h):
                    r = rows4[:, h]
                    far = FAR_GROUP[h] * S
                    for c in range(NT):
                        j = c // 2
                        wait(eng, "m_ev", i, 2 * h + 2)
                        if j >= 2:
                            wait(eng, "y_ev", i, 4 * h + j - 1)
                        out = ps[3 + j % 2][:, (c % 2) * DH:(c % 2 + 1) * DH]
                        ins = mm(out, mmat[:, c * P:(c + 1) * P], r[:, c, 0:DH], True, c == 0)
                        if c > 0:
                            wait(eng, "h_st", i, 7 * h + c)
                            ins = mm(out, qT[far:far + S, c * P:(c + 1) * P], hst[far:far + S, c - 1, :], False, True)
                        if c % 2 == 1:
                            ins.then_inc(s["y_mm"], 1)

                scan_sums(0)
                filler(2)
                scan_inner(0)
                scan_sums(1)
                filler(1)
                scan_y(0)
                scan_inner(1)
                filler(2)
                scan_y(1)
                def y_chunk(k):
                    if k == 0:
                        wait(eng, "y_ev", i, 4 * HEADS)
                        wait(eng, "h_st", i, 7 * HEADS)
                    if k % 2 == 0:
                        wait(eng, f"y_in{k // 2}", i, 16 * NT)
                    if k >= 2:
                        wait(eng, "y_gate", i, (2, 6)[k - 2])
                    for t in range(NT):
                        ins = eng.transpose(ps[yt_banks[k][t // 4]][:, (t % 4) * P:(t % 4 + 1) * P],
                                            ytok[k // 2][:, t, (k % 2) * P:(k % 2 + 1) * P], ident)
                    ins.then_inc(s["yt_mm"], 1)

                def out_part(u, k):
                    half, o = divmod(u, KC)
                    return mm(ps[bank_of[32 + u]][:, :], w_out[:, k, o * P:(o + 1) * P],
                              gate[:, k, half * HALF:(half + 1) * HALF], k == 0, k == KC - 1)

                def split_part(stg, u, k):
                    half, o = divmod(u, KC)
                    his, los = ((even_hi, even_lo), (odd_hi, odd_lo))[stg % 2]
                    return passes("L%d" % stg, his, los, o, half, k, bank_of[24 + 8 * stg + u], k == 0, k == KC - 1)

                def stage_gemm(stg, base, ready, part):
                    def next_sum():
                        wait(eng, "gn_got", i, 12)
                        first_sum(i + 1)

                    others = next_sum if stg == 3 and not last else (lambda: y_chunk(3)) if stg == 1 else None
                    behind(i, stg if stg > 1 else None, base, ready, part, others)
                    for u in range(4, 8):
                        wait(eng, "gemm_evac", i, bank_free[base + u])
                        for k in range(3 if stg == 1 and u < 6 else 0, KC):
                            if u == 4:
                                ready(4 + k)
                            ins = part(u, k)
                            if k == 0 and stg == 2 and u >= 6:
                                gn_sum(i, 3, u - 6)
                            if k == 3 and stg == 1 and u == 6:
                                gn_sum(i, 2, 0)
                        ins.then_inc(s["gemm_done"], 1)

                def y_ready(n):
                    if n == 0:
                        y_chunk(0)
                        y_chunk(1)
                    if n == 2:
                        wait(eng, "y_res", i, 4)
                        out_part(4, 0)
                        out_part(4, 1)
                        filler(1)
                        wait(eng, "gemm_evac", i, 32)
                        y_chunk(2)
                        out_part(5, 0)
                        out_part(5, 1)
                    if n == 3:
                        wait(eng, "y_res", i, 6)
                        out_part(4, 2)
                        out_part(5, 2)
                    wait(eng, "y_res", i, 2 * n + 1 if n < KC else 2 * (n - KC) + 2)

                eng.wait_ge(s["par_in"], 16 * 10)
                stage_gemm(1, 32, y_ready, out_part)
                eng.wait_ge(s["w_lo_rest"], 2 * KC)
                stage_gemm(2, 40, lambda n: wait(eng, "gn_split", i, split_n(2, n)), lambda u, k: split_part(2, u, k))
                stage_gemm(3, 48, lambda n: wait(eng, "gn_split", i, split_n(3, n)), lambda u, k: split_part(3, u, k))
                if not last:
                    wait(eng, "gemm_evac", i, 53)

            image(0, False)
            with eng.Fori(1, B - 1) as i:
                image(i, False)
            image(B - 1, True)
    return nc


def kernel(**inputs):
    import concourse.bacc as bacc
    from concourse.bass_utils import run_bass_kernel_spmd as run

    g = {k: np.asarray(v) for k, v in inputs.items()}
    _, packed = constants()
    cols = lambda b: b.reshape(-1, P).T
    conv_w = g["L0_conv_conv_w"]
    alog = g["L1_conv_A_log"]
    arrays = {
        "x": g["x"].reshape(B, C, N),
        "w0t": conv_w[:, :C].T,
        "wct": conv_w[:, C:].reshape(C, 5, 5).transpose(2, 1, 0).reshape(TAPS, C),
        "wint": g["L1_conv_in_proj_w"].T,
        "woutt": g["L1_conv_out_proj_w"].T,
        "wdbct": g["L1_conv_dbc_w"].T,
        "w2t": g["L2_conv_weight"].T,
        "w3t": g["L3_conv_weight"].T,
        "b0": cols(g["L0_conv_conv_b"]), "bin": cols(g["L1_conv_in_proj_b"]), "bconv": cols(g["L1_conv_dw_b"]),
        "bout": cols(g["L1_conv_out_proj_b"]), "bl2": cols(g["L2_conv_bias"]), "bl3": cols(g["L3_conv_bias"]),
        "bdbc": g["L1_conv_dbc_b"].reshape(1, HEADS * J),
        "taps": g["L1_conv_dw_w"].reshape(KC, P, 3).transpose(1, 0, 2).reshape(P, 3 * KC),
        "alog": alog.reshape(1, HEADS * S), "alog_col": alog.reshape(HEADS, S, 1),
        "dpar": g["L1_conv_Dparam"].reshape(1, HEADS), "mob": g["L1_conv_mobius"].reshape(1, 4 * HEADS),
        "cst": packed,
    }
    nc = bacc.Bacc("TRN2", target_bir_lowering=False, num_devices=1)
    feed, d = {}, {}
    for name, a in arrays.items():
        feed["in_" + name] = a = np.ascontiguousarray(a)
        d[name] = nc.dram_tensor("in_" + name, a.shape, mybir.dt.from_np(a.dtype), kind="ExternalInput").ap()
    d["out"] = nc.dram_tensor("out_x", (B, C, N), F32, kind="ExternalOutput").ap()
    build(nc, d)
    r = run(nc, [feed], core_ids=[0])
    return r.results[0]["out_x"].reshape(B, C, H, W)
```
